# Optimizing a Trainium2 kernel written in Bass

```python
import numpy as np
import jax
import jax.numpy as jnp

def _softmax(x, axis=-1):
    return jax.nn.softmax(x, axis=axis)

def _gelu(x):
    return jax.nn.gelu(x, approximate=True)

def _silu(x):
    return jax.nn.silu(x)

def _sigmoid(x):
    return jax.nn.sigmoid(x)

def _layernorm(x, axis=-1, eps=1e-05):
    m = jnp.mean(x, axis=axis, keepdims=True)
    v = jnp.var(x, axis=axis, keepdims=True)
    return (x - m) / jnp.sqrt(v + eps)

def _scatter_add(tgt, idx, src, axis=0):
    return tgt.at[idx].add(src)

def _segment_sum(src, seg, n):
    return jax.ops.segment_sum(src, seg, n)
kernel_name = 'mk_adj_resnorm_d4_adj_r2_419e8f'

def setup_inputs(seed: int=0):
    np.random.seed(seed)
    _w = jnp.asarray

    def _rec_inputs():
        import jax
        import jax.numpy as jnp
        _gk = jax.random.key(seed)
        x = -0.0005207 + 1.001 * jax.random.normal(jax.random.fold_in(_gk, 1), (64, 128, 256), jnp.float32)
        _a = jax.random.bernoulli(jax.random.fold_in(_gk, 2), 0.0625, (64, 128, 128))
        _a = jnp.logical_or(_a, jnp.swapaxes(_a, -1, -2))
        _a = jnp.logical_or(_a, jnp.eye(128, dtype=bool))
        _af = _a.astype(jnp.float32)
        adj = _af
        _nm = jnp.ones((64, 128), dtype=bool)
        nodemask = _nm
        return (x, adj, nodemask)
    x, adj, nodemask = _rec_inputs()

    def _L0_gnn_setup():
        import jax, jax.numpy as jnp
        import numpy as np
        HEADS = 8
        DIM_HEAD = 64
        LA = 0.33
        LD = 0.33
        LG = 0.33
        key = jax.random.key(seed)
        ks = jax.random.split(key, 6)
        B, N, D = (4, 512, 256)
        inner = HEADS * DIM_HEAD
        x = jax.random.normal(ks[0], (B, N, D), jnp.float32)
        mask = jax.random.uniform(ks[1], (B, N)) < 0.9
        adjacency_mat = (jax.random.uniform(ks[2], (B, N, N)) < 0.05).astype(jnp.float32)
        distance_mat = jax.random.uniform(ks[3], (B, N, N), jnp.float32) * 5.0
        W_qkv = jax.random.normal(ks[4], (D, inner * 3), jnp.float32) * 0.02
        W_out = jax.random.normal(ks[5], (inner, D), jnp.float32) * 0.02
        b_out = jnp.zeros((D,), jnp.float32)
        return {'x': x, 'mask': mask, 'adjacency_mat': adjacency_mat, 'distance_mat': distance_mat, 'W_qkv': W_qkv, 'W_out': W_out, 'b_out': b_out}
    _L0_gnn_all = _L0_gnn_setup()
    _L0_gnn_in = {k: v for k, v in _L0_gnn_all.items() if k in ('W_qkv', 'W_out', 'b_out')}
    del _L0_gnn_all

    def _L1_gnn_setup():
        import jax, jax.numpy as jnp
        import numpy as np
        EPS_LN = 1e-05

        def hypergraph_conv(x, adj, W, b):
            N, C, _ = adj.shape
            H = (adj != 0).astype(x.dtype)
            w = adj.reshape(N, -1)[:, :C]
            xw = jnp.einsum('ncd,hd->nch', x, W)
            Dn = jnp.einsum('nce,ne->nc', H, w)
            Dn = jnp.where(Dn > 0, 1.0 / Dn, 0.0)
            Be = H.sum(axis=1)
            Be = jnp.where(Be > 0, 1.0 / Be, 0.0)
            m = Be[:, :, None] * jnp.einsum('nce,nch->neh', H, xw)
            out = Dn[:, :, None] * jnp.einsum('nce,neh->nch', H, m)
            return out + b

        def layer_norm(x, g, b):
            mu = jnp.mean(x, axis=-1, keepdims=True)
            var = jnp.var(x, axis=-1, keepdims=True)
            return (x - mu) * jax.lax.rsqrt(var + EPS_LN) * g + b
        key = jax.random.key(seed)
        ks = jax.random.split(key, 4)
        N, C, Din, Dh, Dout = (16, 512, 256, 512, 256)
        x = jax.random.normal(ks[0], (N, C, Din), dtype=jnp.float32)
        adj = jax.random.uniform(ks[1], (N, C, C), dtype=jnp.float32, minval=0.1, maxval=1.0)
        W1 = jax.random.normal(ks[2], (Dh, Din), dtype=jnp.float32) * (1.0 / np.sqrt(Din))
        b1 = jnp.zeros((Dh,), dtype=jnp.float32)
        gamma = jnp.ones((Dh,), dtype=jnp.float32)
        beta = jnp.zeros((Dh,), dtype=jnp.float32)
        W2 = jax.random.normal(ks[3], (Dout, Dh), dtype=jnp.float32) * (1.0 / np.sqrt(Dh))
        b2 = jnp.zeros((Dout,), dtype=jnp.float32)
        return {'x': x, 'adj': adj, 'W1': W1, 'b1': b1, 'gamma': gamma, 'beta': beta, 'W2': W2, 'b2': b2}
    _L1_gnn_all = _L1_gnn_setup()
    _L1_gnn_in = {k: v for k, v in _L1_gnn_all.items() if k in ('W1', 'b1', 'gamma', 'beta', 'W2', 'b2')}
    del _L1_gnn_all

    def _L2_gnn_setup():
        import jax, jax.numpy as jnp
        import numpy as np
        B, N, DIN, DOUT, K = (4, 1024, 256, 256, 3)
        key = jax.random.key(seed)
        ks = jax.random.split(key, 8)
        X = jax.random.normal(ks[0], (B, N, DIN), dtype=jnp.float32)
        A = jax.random.uniform(ks[1], (B, N, N), dtype=jnp.float32)
        Wv = jax.random.normal(ks[2], (DIN, DOUT), dtype=jnp.float32) * 0.02
        bv = jax.random.normal(ks[3], (DOUT,), dtype=jnp.float32) * 0.02
        aw = jax.random.normal(ks[4], (2 * DOUT, 1), dtype=jnp.float32) * 0.05
        ab = jax.random.normal(ks[5], (1,), dtype=jnp.float32) * 0.05
        Wk = jax.random.normal(ks[6], (K, DIN, DOUT), dtype=jnp.float32) * 0.02
        bk = jax.random.normal(ks[7], (K, DOUT), dtype=jnp.float32) * 0.02
        return {'X': X, 'A': A, 'Wv': Wv, 'bv': bv, 'aw': aw, 'ab': ab, 'Wk': Wk, 'bk': bk}
    _L2_gnn_all = _L2_gnn_setup()
    _L2_gnn_in = {k: v for k, v in _L2_gnn_all.items() if k in ('Wv', 'bv', 'aw', 'ab', 'Wk', 'bk')}
    del _L2_gnn_all

    def _L3_gnn_setup():
        import jax, jax.numpy as jnp
        import numpy as np
        EPS = 1e-06
        key = jax.random.key(seed)
        k1, k2, k3 = jax.random.split(key, 3)
        B, N, F, O = (8, 2048, 256, 256)
        x = jax.random.normal(k1, (B, N, F), dtype=jnp.float32)
        adj = jax.random.uniform(k2, (B, N, N), dtype=jnp.float32)
        W = jax.random.normal(k3, (O, 2 * F), dtype=jnp.float32) * (1.0 / np.sqrt(2 * F))
        return {'x': x, 'adj': adj, 'W': W}
    _L3_gnn_all = _L3_gnn_setup()
    _L3_gnn_in = {k: v for k, v in _L3_gnn_all.items() if k in ('W',)}
    del _L3_gnn_all
    return {'x': x, 'adj': adj, 'nodemask': nodemask, 'L0_gnn_W_qkv': _L0_gnn_in['W_qkv'], 'L0_gnn_W_out': _L0_gnn_in['W_out'], 'L0_gnn_b_out': _L0_gnn_in['b_out'], 'L1_gnn_W1': _L1_gnn_in['W1'], 'L1_gnn_b1': _L1_gnn_in['b1'], 'L1_gnn_gamma': _L1_gnn_in['gamma'], 'L1_gnn_beta': _L1_gnn_in['beta'], 'L1_gnn_W2': _L1_gnn_in['W2'], 'L1_gnn_b2': _L1_gnn_in['b2'], 'L2_gnn_Wv': _L2_gnn_in['Wv'], 'L2_gnn_bv': _L2_gnn_in['bv'], 'L2_gnn_aw': _L2_gnn_in['aw'], 'L2_gnn_ab': _L2_gnn_in['ab'], 'L2_gnn_Wk': _L2_gnn_in['Wk'], 'L2_gnn_bk': _L2_gnn_in['bk'], 'L3_gnn_W': _L3_gnn_in['W']}

def reference(x, adj, nodemask, L0_gnn_W_qkv, L0_gnn_W_out, L0_gnn_b_out, L1_gnn_W1, L1_gnn_b1, L1_gnn_gamma, L1_gnn_beta, L1_gnn_W2, L1_gnn_b2, L2_gnn_Wv, L2_gnn_bv, L2_gnn_aw, L2_gnn_ab, L2_gnn_Wk, L2_gnn_bk, L3_gnn_W):
    import jax
    import jax.numpy as jnp

    def _L0_gnn_ref(x, mask, adjacency_mat, distance_mat, W_qkv, W_out, b_out):
        import jax, jax.numpy as jnp
        import numpy as np
        HEADS = 8
        DIM_HEAD = 64
        LA = 0.33
        LD = 0.33
        LG = 0.33
        B, N, _ = x.shape
        scale = DIM_HEAD ** (-0.5)
        qkv = (x @ W_qkv).reshape(B, N, HEADS, 3, DIM_HEAD)
        q, k, v = (jnp.transpose(qkv[..., i, :], (0, 2, 1, 3)) for i in range(3))
        dots = jnp.einsum('bhid,bhjd->bhij', q, k) * scale
        big = jnp.finfo(dots.dtype).max
        m2 = mask[:, None, :, None] & mask[:, None, None, :]
        dots = jnp.where(m2, dots, -big)
        attn = jax.nn.softmax(dots, axis=-1) * LA
        adj = jnp.where(m2, adjacency_mat[:, None], 0.0)
        dist = jnp.where(m2, distance_mat[:, None], big)
        attn = attn + LG * adj + LD * jnp.exp(-dist)
        out = jnp.einsum('bhij,bhjd->bhid', attn, v)
        out = jnp.transpose(out, (0, 2, 1, 3)).reshape(B, N, HEADS * DIM_HEAD)
        return out @ W_out + b_out

    def _L1_gnn_ref(x, adj, W1, b1, gamma, beta, W2, b2):
        import jax, jax.numpy as jnp
        import numpy as np
        EPS_LN = 1e-05

        def hypergraph_conv(x, adj, W, b):
            N, C, _ = adj.shape
            H = (adj != 0).astype(x.dtype)
            w = adj.reshape(N, -1)[:, :C]
            xw = jnp.einsum('ncd,hd->nch', x, W)
            Dn = jnp.einsum('nce,ne->nc', H, w)
            Dn = jnp.where(Dn > 0, 1.0 / Dn, 0.0)
            Be = H.sum(axis=1)
            Be = jnp.where(Be > 0, 1.0 / Be, 0.0)
            m = Be[:, :, None] * jnp.einsum('nce,nch->neh', H, xw)
            out = Dn[:, :, None] * jnp.einsum('nce,neh->nch', H, m)
            return out + b

        def layer_norm(x, g, b):
            mu = jnp.mean(x, axis=-1, keepdims=True)
            var = jnp.var(x, axis=-1, keepdims=True)
            return (x - mu) * jax.lax.rsqrt(var + EPS_LN) * g + b
        h = jax.nn.relu(hypergraph_conv(x, adj, W1, b1))
        h = layer_norm(h, gamma, beta)
        y = hypergraph_conv(h, adj, W2, b2)
        return y + x

    def _L2_gnn_ref(X, A, Wv, bv, aw, ab, Wk, bk):
        import jax, jax.numpy as jnp
        import numpy as np
        B, N, DIN, DOUT, K = (4, 1024, 256, 256, 3)
        d = Wv.shape[1]
        Xw = X @ Wv + bv
        sj = Xw @ aw[:d, 0]
        si = Xw @ aw[d:, 0]
        e = jax.nn.leaky_relu(sj[:, None, :] + si[:, :, None] + ab[0], negative_slope=0.2)
        alpha_matrix = A * jnp.exp(e)
        transition = alpha_matrix / (jnp.sum(alpha_matrix, axis=-1, keepdims=True) + 1e-12)
        H = jnp.zeros(X.shape[:-1] + (d,), dtype=X.dtype)
        Xk = X
        for k in range(Wk.shape[0]):
            H = H + Xk @ Wk[k] + bk[k]
            Xk = jnp.einsum('bij,bjd->bid', transition, Xk)
        return jax.nn.relu(H)

    def _L3_gnn_ref(x, adj, W):
        import jax, jax.numpy as jnp
        import numpy as np
        EPS = 1e-06
        deg = jnp.sum(adj, axis=-1, keepdims=True)
        agg = jnp.einsum('bij,bjf->bif', adj, x) / jnp.maximum(deg, EPS)
        cat = jnp.concatenate([x, agg], axis=2)
        out = jnp.einsum('bnf,of->bno', cat, W)
        return jax.nn.relu(out)
    x = _layernorm(x + _L0_gnn_ref(x, nodemask, adj, adj, L0_gnn_W_qkv, L0_gnn_W_out, L0_gnn_b_out), axis=-1)
    x = _layernorm(x + _L1_gnn_ref(x, adj, L1_gnn_W1, L1_gnn_b1, L1_gnn_gamma, L1_gnn_beta, L1_gnn_W2, L1_gnn_b2), axis=-1)
    x = _layernorm(x + _L2_gnn_ref(x, adj, L2_gnn_Wv, L2_gnn_bv, L2_gnn_aw, L2_gnn_ab, L2_gnn_Wk, L2_gnn_bk), axis=-1)
    x = _layernorm(x + _L3_gnn_ref(x, adj, L3_gnn_W), axis=-1)
    return x

_drawn_inputs = setup_inputs


def setup_inputs(seed=0):
    import zlib

    import numpy as np

    out = dict(_drawn_inputs(seed))
    spreads = {'L0_gnn_b_out': (0.0, 0.1),
     'L1_gnn_b1': (0.0, 0.1),
     'L1_gnn_gamma': (1.0, 0.2),
     'L1_gnn_beta': (0.0, 0.1),
     'L1_gnn_b2': (0.0, 0.289)}
    factors = {'L2_gnn_Wv': 7.132, 'L2_gnn_bv': 30.414, 'L2_gnn_aw': 7.559}
    for name, (base, spread) in spreads.items():
        noise = np.random.default_rng([zlib.crc32(name.encode()), seed]).standard_normal(out[name].shape)
        drawn = base * np.exp(spread * noise) if base else spread * noise
        out[name] = jnp.asarray(drawn.astype(out[name].dtype))
    for name, factor in factors.items():
        out[name] = (out[name] * factor).astype(out[name].dtype)
    return out
```

```python
from contextlib import ExitStack

import concourse.bass as bass
from concourse import mybir

F32 = mybir.dt.float32
F32R = mybir.dt.float32r
BF16 = mybir.dt.bfloat16
U8 = mybir.dt.uint8
ALU = mybir.AluOpType
ACT = mybir.ActivationFunctionType
AX_X = mybir.AxisListType.X
AX_XY = mybir.AxisListType.XY

P = 128
HEADS = 8
DH = 64
MIX = 0.33
LN_EPS = 1e-5
DEG_EPS = 1e-6
DEN_EPS = 1e-12
TINY = 1.2e-38
SLOPE = 0.2
BIG = float(2.0 ** 100)


def gnn_stack_kernel(nc, x, adj, nodemask, W_qkv, W_out, b_out, W1, b1, gamma, beta, W2, b2,
                     Wv, bv, aw, ab, Wk, bk, W3, out):
    NG, N, D = x.shape
    G = 2
    ITERS = NG // G
    DC = D // P
    INNER = HEADS * DH
    IC = INNER // P
    DHID = W1.shape[0]
    HC = DHID // P
    QKB = 2 * INNER // P
    SCALE = float(DH) ** -0.5
    VX = DH + 1
    assert N == P and D == 256 and DHID == 512 and INNER == 512 and QKB == 8

    ctx = ExitStack()
    with ctx:
        free = nc.sbuf_bytes_remaining - 64
        arena = ctx.enter_context(nc.sbuf_tensor("arena", [P, free // 4], F32))
        arena_base = (nc.sbuf_base - free + 31) // 32 * 32
        place = [arena_base]

        def at(name, shape, dt=F32, keep=True):
            size = 1
            for n in shape[1:]:
                size *= n
            size *= {F32: 4, F32R: 4, BF16: 2, U8: 1}[dt]
            t = nc.alloc_sbuf_tensor_at(name, shape, dt, offset=place[0])
            place[0] += (size + 31) // 32 * 32
            assert place[0] <= arena_base + free - 32, (name, place[0])
            return t

        def pair(name, shape):
            return at(name + "_hi", shape, F32R), at(name + "_lo", shape, F32R)

        ident = at("ident", [P, P])
        wqk = pair("wqk", [P, DC, 2, HEADS, DH])
        wvo = pair("wvo", [P, DC, INNER + D])
        wout = pair("wout", [P, IC, D])
        w1t = pair("w1t", [P, DC, DHID])
        w2t = pair("w2t", [P, HC, D])
        wk01 = pair("wk01", [P, DC, 2, D])
        wk2 = pair("wk2", [P, DC, D + 2])
        wi = pair("wi", [P, DC, P])
        w3t = pair("w3t", [P, DC, 2, D])
        bout_bc = at("bout_bc", [P, D])
        b1_bc = at("b1_bc", [P, DHID])
        b2_bc = at("b2_bc", [P, D])
        bk_bc = at("bk_bc", [P, D])
        bw_bc = at("bw_bc", [P, D])
        mask33 = at("mask33", [P, NG])
        gate_c = at("gate_c", [P, 1])
        mask_ab = at("mask_ab", [P, 4])
        mhalf = at("mhalf", [P, 1])
        eps_c = at("eps_c", [P, 1])

        vext = at("vext", [P, G, HEADS, VX])
        z2 = pair("z2", [P, G, D + 2])
        wone = at("wone", [P, G, 2])
        mrow_l = at("mrow_l", [P, G, P], BF16)
        mrow_r = at("mrow_r", [P, G, P], BF16)
        xin = at("xin", [P, G, D])
        adj_in = at("adj_in", [P, G, P])
        mask_bc8 = at("mask_bc8", [P, G * P], U8)
        work_base = place[0]

        adjT = at("adjT", [P, G, P])
        adjTb = at("adjTb", [P, G, P])
        gate = at("gate", [P, G, P])
        gT = pair("gT", [P, G, P])
        aT = pair("aT", [P, G, P])
        HT = at("HT", [P, G, P])
        BHT = at("BHT", [P, G, P])
        DHn = at("DHn", [P, G, P])
        DHT = at("DHT", [P, G, P])
        AT = at("AT", [P, G, P])
        mbc = at("mbc", [P, G * P])
        xT0 = pair("xT0", [P, DC, G, P])
        xT2 = pair("xT2", [P, DC, G, P])
        qk = at("qk", [P, QKB, G, P])
        vo = pair("vo", [P, G, D])
        prob = at("prob", [P, 2, HEADS, P])
        probT = at("probT", [P, HEADS, P])
        osb = at("osb", [P, HEADS, DH])
        oT = pair("oT", [P, IC, P])
        ys0 = at("ys0", [P, G, D])
        ysb = at("ysb", [P, G, D])
        x1 = at("x1", [P, G, D])
        x2 = at("x2", [P, G, D])
        x3 = at("x3", [P, G, D])
        xout = at("xout", [P, G, D])
        resid = at("resid", [P, G, D])
        axT = pair("axT", [P, G, DC, P])
        hid = at("hid", [P, G, DHID])
        hT = pair("hT", [P, G, HC, P])
        z0 = at("z0", [P, G, D])
        z1 = at("z1", [P, G, D])
        e1 = at("e1", [P, G, P])
        e2 = at("e2", [P, G, P])
        al = at("al", [P, G, P])
        alT = pair("alT", [P, G, P])
        yv = at("yv", [P, G, D])
        yT = pair("yT", [P, G, D])
        za = at("za", [P, G, D])
        zb = pair("zb", [P, G, D])
        m33 = at("m33", [P, G])
        cnt = at("cnt", [P, G])
        Be = at("Be", [P, G])
        degf = at("degf", [P, G])
        degb = at("degb", [P, G])
        dcol = at("dcol", [P, G, 2])
        dpos = at("dpos", [P, G])
        dsafe = at("dsafe", [P, G])
        drec = at("drec", [P, G])
        Dn = at("Dn", [P, G])
        rA = at("rA", [P, G])
        m8 = at("m8", [P, G, HEADS])
        rl = at("rl", [P, G, 2, HEADS // 2])
        sj = at("sj", [P, G, 2])
        den = at("den", [P, G])
        rden = at("rden", [P, G])
        NORM0, NORMH, NORM1, NORM2, NORM3 = range(5)
        st = at("st", [P, 5, G, 6])
        mv = at("mv", [P, 5, G, 2])
        rs = at("rs", [P, 5, G, 2])
        work_end = place[0]

        place[0] = work_base
        wqkv_raw = at("wqkv_raw", [P, DC, HEADS, 3, DH])
        wv_flat = at("wv_flat", [P, DC, INNER])
        wout_raw = at("wout_raw", [P, IC, D])
        w1_raw = at("w1_raw", [P, HC, D])
        w2_raw = at("w2_raw", [P, DC, DHID])
        w3_raw = at("w3_raw", [P, DC, 2 * D])
        wk_raw = at("wk_raw", [P, 3, DC, D])
        wv2_raw = at("wv2_raw", [P, DC, D])
        aw_bc = at("aw_bc", [P, 2, D])
        bv_bc = at("bv_bc", [P, D])
        ab_bc = at("ab_bc", [P, 1])
        bk_raw = at("bk_raw", [P, 3, D])
        gamma_c = at("gamma_c", [P, HC])
        beta_c = at("beta_c", [P, HC])
        beta_bc = at("beta_bc", [P, HC, P])
        wvT = at("wvT", [P, IC, D])
        w2T_raw = at("w2T_raw", [P, HC, D])
        prod = at("prod", [P, 2, DC, D])
        wji = at("wji", [P, 2, DC])
        bprod = at("bprod", [P, 2, D])
        bsum = at("bsum", [P, 1])
        mask8 = at("mask8", [NG, P], U8)
        maskf = at("maskf", [NG, P])
        assert place[0] <= work_end

        PS = ctx.enter_context(nc.psum_tensor("PS", [P, 8, 512], F32))
        bA, bB, bD, bC, bE, bP, bQ, bR = range(8)

        def sem(name):
            return ctx.enter_context(nc.semaphore(name))

        ld_wqkv, ld_wout, ld_w1, ld_w2, ld_w3, ld_wk, ld_vec, ld_mask, ld_gb = (
            sem(n) for n in ("ld_wqkv", "ld_wout", "ld_w1", "ld_w2", "ld_w3", "ld_wk", "ld_vec", "ld_mask", "ld_gb"))
        ident_ok = sem("ident_ok")
        pool_const = sem("pool_const")
        set_flat = sem("set_flat")
        set_maskf = sem("set_maskf")
        set_beta = sem("set_beta")
        set_prod = sem("set_prod")
        set_wji = sem("set_wji")
        set_pe = sem("set_pe")
        set_copy = sem("set_copy")
        set_hi = sem("set_hi")
        set_lo = sem("set_lo")
        set_small = sem("set_small")
        x_in, a_in, m_in, y_out = (sem(n) for n in ("x_in", "a_in", "m_in", "y_out"))
        (pe_adjT, pe_xT0, pe_qk, pe_D, pe_v, pe_vo, pe_DHT, pe_AT, pe_S, pe_PT, pe_PV, pe_OT, pe_y0) = (
            sem("pe_" + n) for n in ("adjT", "xT0", "qk", "D", "v", "vo", "DHT", "AT", "S", "PT", "PV", "OT", "y0"))
        (act_adjT, act_xT0, act_gate, act_qk, act_v, act_vo, act_DHT, act_AT, act_exp, act_PT, act_OT,
         act_gT, act_adjTb) = (
            sem("act_" + n) for n in ("adjT", "xT0", "gate", "qk", "v", "vo", "DHT", "AT", "exp", "PT", "OT",
                                        "gT", "adjTb"))
        (dve_xT0, dve_HT, dve_wone, dve_m33, dve_Be, dve_Dn, dve_DH, dve_vo, dve_sub, dve_O, dve_OT, dve_y0, dve_mv0,
         dve_deg, dve_x1) = (sem("dve_" + n) for n in ("xT0", "HT", "wone", "m33", "Be", "Dn", "DH", "vo", "sub", "O", "OT", "y0",
                                                "mv0", "deg", "x1"))
        (pool_mrow, pool_mbc, pool_resid0, pool_BHT, pool_gate, pool_gT, pool_rs0) = (
            sem("pool_" + n) for n in ("mrow", "mbc", "resid0", "BHT", "gate", "gT", "rs0"))
        (pe_ax, pe_h, pe_hT, pe_y1, pe_xT2, pe_Z01, pe_Z2, pe_si, pe_T1, pe_T2, pe_xT3, pe_Z3, pe_T3) = (
            sem("pe_" + n) for n in ("ax", "h", "hT", "y1", "xT2", "Z01", "Z2", "si", "T1", "T2", "xT3", "Z3", "T3"))
        (act_ax, act_relu, act_hT, act_xT2, act_Z1, act_Z2, act_E, act_Y, act_xT3, act_za, act_zb,
         act_u, act_aT) = (
            sem("act_" + n) for n in ("ax", "relu", "hT", "xT2", "Z1", "Z2", "E", "Y", "xT3", "za", "zb", "u",
                                        "aT"))
        (dve_ax, dve_hb, dve_mvh, dve_hT, dve_mv1, dve_xT2, dve_Z0, dve_Z2, dve_sj, dve_al, dve_Y, dve_Yl, dve_o2,
         dve_mv2, dve_xT3, dve_zb, dve_o3, dve_mv3, dve_hn, dve_x2, dve_x3) = (
            sem("dve_" + n) for n in ("ax", "hb", "mvh", "hT", "mv1", "xT2", "Z0", "Z2", "sj", "al", "Y", "Yl", "o2",
                                      "mv2", "xT3", "zb", "o3", "mv3", "hn", "x2", "x3"))
        (pool_resid1, pool_rsh, pool_rs1, pool_rs2, pool_aT, pool_out) = (
            sem("pool_" + n) for n in ("resid1", "rsh", "rs1", "rs2", "aT", "out"))
        dve_fstep, dve_bstep, pool_fstep, pool_bstep = (
            sem(n) for n in ("dve_fstep", "dve_bstep", "pool_fstep", "pool_bstep"))

        DVE_FSTEPS, DVE_BSTEPS, POOL_FSTEPS, POOL_BSTEPS = 7 + 3 * G, 2 + 13 * G, 1 + G, 7 * G

        class Steps:

            def __init__(self, eng, counter, i, per_group):
                self.eng, self.counter, self.i, self.per_group, self.n = eng, counter, i, per_group, 0

            def done(self, ins):
                self.n += 1
                ins.then_inc(self.counter, 1)
                self.eng.wait_ge(self.counter, self.i * self.per_group + self.n)

        raw = wqkv_raw
        splits = []
        for c in range(DC):
            splits.append((raw[:, c, :, 0:2, :].rearrange("p h t d -> p t h d"), wqk[0][:, c], wqk[1][:, c], None,
                           (ld_wqkv, 16)))
        for c in range(DC):
            splits.append((raw[:, c, :, 2, :], wvo[0][:, c, 0:INNER].rearrange("p (h d) -> p h d", h=HEADS),
                           wvo[1][:, c, 0:INNER].rearrange("p (h d) -> p h d", h=HEADS), None, (ld_wqkv, 16)))
        splits.append((wout_raw[:], wout[0][:], wout[1][:], None, (ld_wout, 16)))
        for k in range(2):
            splits.append((wk_raw[:, k], wk01[0][:, :, k, :], wk01[1][:, :, k, :], None, (ld_wk, 48)))
        splits.append((wk_raw[:, 2], wk2[0][:, :, 0:D], wk2[1][:, :, 0:D], None, (ld_wk, 48)))
        splits.append((wji[:, 0, :], wk2[0][:, :, D], wk2[1][:, :, D], None, (set_wji, 1)))
        for c in range(DC):
            splits.append((wji[:, 1, c:c + 1].to_broadcast([P, P]), wi[0][:, c, :], wi[1][:, c, :], None,
                           (set_wji, 1)))
        SET_WVT, SET_W2T, SET_W1, SET_W3, SET_WVO, SET_BW, SET_MASK = 1, 2, 3, 4, 5, 6, 7
        for c in range(DC):
            splits.append((PS[:, 2 + c, :], w1t[0][:, c], w1t[1][:, c], None, (set_pe, SET_W1)))
        for c in range(DC):
            splits.append((PS[:, 4 + c, :].rearrange("p (t o) -> p t o", t=2), w3t[0][:, c], w3t[1][:, c], None,
                           (set_pe, SET_W3)))
        splits.append((PS[:, bQ, :].rearrange("p (c d) -> p c d", c=DC), wvo[0][:, :, INNER:], wvo[1][:, :, INNER:],
                       None, (set_pe, SET_WVO)))
        for k in range(HC):
            splits.append((w2T_raw[:, k], w2t[0][:, k], w2t[1][:, k], gamma_c[:, k:k + 1], (set_copy, 2)))
        N_SPLITS = len(splits)
        N_COPIES = 4
        N_SMALL = 3

        xg = x.rearrange("g n d -> n g d")
        ag = adj.rearrange("g n m -> n g m")
        og = out.rearrange("g n d -> n g d")
        mask_rows = nodemask.rearrange("(i g) n -> i (g n)", g=G)

        def set_up_done(eng):
            eng.wait_ge(set_hi, N_SPLITS)
            eng.wait_ge(set_lo, N_SPLITS)
            eng.wait_ge(set_copy, N_COPIES)
            eng.wait_ge(set_small, N_SMALL)
            eng.wait_ge(pool_const, 16)

        dve_past, pool_past = sem("dve_past"), sem("pool_past")

        def settle(eng):
            eng.sem_inc(dve_past if eng is nc.vector else pool_past, 1)

        block = ctx.enter_context(nc.Block())

        @block.sync
        def _(sp):
            sp.dma_start(wqkv_raw[:].rearrange("p c h t d -> p c (h t d)"),
                         W_qkv.rearrange("(c p) n -> p c n", p=P)).then_inc(ld_wqkv, 16)
            sp.dma_start(w2_raw[:], W2.rearrange("(c p) n -> p c n", p=P)).then_inc(ld_w2, 16)
            sp.dma_start(w1_raw[:], W1.rearrange("(c p) n -> p c n", p=P)).then_inc(ld_w1, 16)
            sp.dma_start(wout_raw[:], W_out.rearrange("(c p) n -> p c n", p=P)).then_inc(ld_wout, 16)
            sp.dma_start(w3_raw[:], W3.rearrange("(c p) n -> p c n", p=P)).then_inc(ld_w3, 16)
            for k in range(3):
                sp.dma_start(wk_raw[:, k], Wk[k].rearrange("(c p) n -> p c n", p=P)).then_inc(ld_wk, 16)

            def load_group(i):
                sp.dma_start(adj_in[:], ag[:, bass.ds(i * G, G), :]).then_inc(a_in, 16)
                sp.dma_start(xin[:], xg[:, bass.ds(i * G, G), :]).then_inc(x_in, 16)
                sp.dma_start(mask_bc8[:], mask_rows[bass.ds(i, 1), :].rearrange("a n -> (a n)").partition_broadcast(P))\
                    .then_inc(m_in, 16)

            def used(i):
                sp.wait_ge(pe_adjT, i + 1)
                sp.wait_ge(pe_xT0, i + 1)
                sp.wait_ge(dve_deg, i + 1)
                sp.wait_ge(dve_DH, i * G + G)
                sp.wait_ge(pool_resid0, i + 1)
                sp.wait_ge(pool_mbc, i + 1)
                sp.wait_ge(pool_mrow, i * 4 + 4)

            def store_group(j):
                sp.wait_ge(pool_out, j * G + G)
                sp.dma_start(og[:, bass.ds(j * G, G), :], xout[:]).then_inc(y_out, 16)

            load_group(0)
            used(0)
            load_group(1)
            with sp.Fori(0, ITERS - 2) as j:
                used(j + 1)
                load_group(j + 2)
                store_group(j)
            store_group(ITERS - 2)
            store_group(ITERS - 1)
            sp.wait_ge(y_out, 16 * ITERS)

        @block.tensor
        def _(pe):
            def mm3(dst, lhs, rhs, start=True, stop=True):
                pe.matmul(dst, lhs[0], rhs[0], start=start, stop=False)
                pe.matmul(dst, lhs[0], rhs[1], start=False, stop=False)
                return pe.matmul(dst, lhs[1], rhs[0], start=False, stop=stop)

            def both(t, *index):
                return t[0][index], t[1][index]

            A = slice(None)

            def set_up():
                pe.wait_ge(ident_ok, 2)
                pe.wait_ge(set_flat, 1)
                for k in range(IC):
                    for c in range(DC):
                        last = pe.transpose(PS[:, bA + k // 2, (k % 2) * D + c * P:(k % 2) * D + (c + 1) * P],
                                            wv_flat[:, c, k * P:(k + 1) * P], ident[:])
                last.then_inc(set_pe, 1)
                pe.wait_ge(ld_w2, 16)
                for k in range(HC):
                    for c in range(DC):
                        last = pe.transpose(PS[:, bQ + k // 2, (k % 2) * D + c * P:(k % 2) * D + (c + 1) * P],
                                            w2_raw[:, c, k * P:(k + 1) * P], ident[:])
                last.then_inc(set_pe, 1)
                pe.wait_ge(ld_w1, 16)
                for c in range(DC):
                    for k in range(HC):
                        last = pe.transpose(PS[:, 2 + c, k * P:(k + 1) * P], w1_raw[:, k, c * P:(c + 1) * P], ident[:])
                last.then_inc(set_pe, 1)
                pe.wait_ge(ld_w3, 16)
                for c in range(DC):
                    for t in range(2):
                        for o in range(DC):
                            last = pe.transpose(PS[:, 4 + c, t * D + o * P:t * D + (o + 1) * P],
                                                w3_raw[:, o, t * D + c * P:t * D + (c + 1) * P], ident[:])
                last.then_inc(set_pe, 1)
                pe.wait_ge(set_copy, 2)
                pe.wait_ge(ld_wout, 16)
                for c in range(DC):
                    for k in range(IC):
                        last = pe.matmul(PS[:, bQ, c * D:(c + 1) * D], wvT[:, k, c * P:(c + 1) * P], wout_raw[:, k, :],
                                         start=(k == 0), stop=(k == IC - 1))
                last.then_inc(set_pe, 1)
                pe.wait_ge(set_beta, 1)
                for k in range(HC):
                    last = pe.matmul(PS[:, bR, 0:D], beta_bc[:, k, :], w2T_raw[:, k, :],
                                     start=(k == 0), stop=(k == HC - 1))
                last.then_inc(set_pe, 1)
                pe.wait_ge(set_maskf, 1)
                pe.transpose(PS[:, bA, 0:NG], maskf[:], ident[0:NG, 0:NG]).then_inc(set_pe, 1)

            def adjT_(i):
                pe.wait_ge(a_in, i * 16 + 16)
                for g in range(G):
                    last = pe.transpose(PS[:, bA, g * P:(g + 1) * P], adj_in[:, g, :], ident[:])
                last.then_inc(pe_adjT, 1)

            def xT0_(i):
                pe.wait_ge(x_in, i * 16 + 16)
                pe.wait_ge(dve_y0, i * G)
                for c in range(DC):
                    for g in range(G):
                        last = pe.transpose(PS[:, bB, (c * G + g) * P:(c * G + g + 1) * P],
                                            xin[:, g, c * P:(c + 1) * P], ident[:])
                last.then_inc(pe_xT0, 1)

            def qk_(i, k):
                bank = (bC, bD, bE, bC)[k]
                if k == 0:
                    pe.wait_ge(act_xT0, i + 1)
                    pe.wait_ge(dve_xT0, i + 1)
                if k == 3:
                    pe.wait_ge(act_qk, i * 4 + 1)
                for m in range(2 * k, 2 * k + 2):
                    t, h = m // 4, 2 * (m % 4)
                    for c in range(DC):
                        last = mm3(PS[:, bank, (m % 2) * G * P:(m % 2 + 1) * G * P],
                                   both(wqk, A, c, t, slice(h, h + 2)), both(xT0, A, c),
                                   start=(c == 0), stop=(c == DC - 1))
                last.then_inc(pe_qk, 1)

            def D_(i):
                pe.wait_ge(act_adjT, i + 1)
                pe.wait_ge(dve_HT, i + 1)
                pe.wait_ge(dve_wone, i + 1)
                for g in range(G):
                    last = pe.matmul(PS[:, bA, 2 * g:2 * g + 2], HT[:, g, :], wone[:, g, :], start=True, stop=True)
                last.then_inc(pe_D, 1)

            def v_(i, g):
                if g == 0:
                    pe.wait_ge(act_qk, i * 4 + 2)
                else:
                    pe.wait_ge(act_qk, i * 4 + 4)
                bv_, bo_ = ((bB, bD), (bE, bC))[g]
                for c in range(DC):
                    last = mm3(PS[:, bv_, :], both(xT0, A, c, g), both(wvo, A, c, slice(0, INNER)),
                               start=(c == 0), stop=(c == DC - 1))
                last.then_inc(pe_v, 1)
                for c in range(DC):
                    last = mm3(PS[:, bo_, 0:D], both(xT0, A, c, g), both(wvo, A, c, slice(INNER, INNER + D)),
                               start=(c == 0), stop=(c == DC - 1))
                last.then_inc(pe_vo, 1)

            def DHT_(i):
                pe.wait_ge(dve_DH, i * G + G)
                for g in range(G):
                    last = pe.transpose(PS[:, bA, g * P:(g + 1) * P], DHn[:, g, :], ident[:])
                last.then_inc(pe_DHT, 1)

            def AT_(i):
                pe.wait_ge(act_DHT, i + 1)
                pe.wait_ge(pool_BHT, i * G + G)
                for g in range(G):
                    last = pe.matmul(PS[:, bA, g * P:(g + 1) * P], BHT[:, g, :], DHT[:, g, :], start=True, stop=True)
                last.then_inc(pe_AT, 1)

            def S_(i, t):
                if t == 0:
                    pe.wait_ge(pool_mrow, i * 4 + 4)
                pe.wait_ge(act_v, i * G + t + 1)
                pe.wait_ge(act_vo, i * G + t + 1)
                pe.wait_ge(dve_vo, i * G + t + 1)
                banks = ((bB, bD), (bC, bE))[t]
                for par in range(2):
                    p = par * DH
                    pe.matmul(PS[:, banks[par], :], mrow_l[p:p + DH, t, :],
                              mrow_r[p:p + DH, t:t + 1, :].to_broadcast([DH, HEADS // 2, P]),
                              start=True, stop=False, skip_group_check=True)
                for k in range(HEADS // 2):
                    for par in range(2):
                        p = par * DH
                        last = pe.matmul(PS[:, banks[par], k * P:(k + 1) * P], qk[p:p + DH, k, t, :],
                                         qk[p:p + DH, QKB // 2 + k, t, :], start=False,
                                         stop=(k == HEADS // 2 - 1), skip_group_check=True)
                last.then_inc(pe_S, 1)

            def PT_(i, t):
                pe.wait_ge(act_exp, i * G + t + 1)
                for h in range(HEADS):
                    last = pe.transpose(PS[:, (bB, bD)[h // 4], (h % 4) * P:(h % 4 + 1) * P], prob[:, t, h, :],
                                        ident[:])
                last.then_inc(pe_PT, 1)

            def PV_(i, t):
                if t == 0:
                    pe.wait_ge(dve_sub, i * G + G)
                    pe.wait_ge(act_v, i * G + G)
                pe.wait_ge(act_PT, i * G + t + 1)
                for slot in range(HEADS):
                    h = 2 * (slot % 4) + slot // 4
                    last = pe.matmul(PS[:, (bC, bE)[h // 4], (h % 4) * VX:(h % 4 + 1) * VX], probT[:, slot, :],
                                     vext[:, t, h, :], start=True, stop=True)
                last.then_inc(pe_PV, 1)

            def OT_(i, t, j):
                pe.wait_ge(dve_O, i * G + t + 1)
                if t == 0 and j is not None:
                    pe.wait_ge(act_Z2, j * G + 1)
                    pe.wait_ge(dve_Z2, j * G + 1)
                    pe.wait_ge(dve_sj, j * G + 1)
                for k in range(IC):
                    last = pe.transpose(PS[:, bQ, k * P:(k + 1) * P], osb[:, 2 * k:2 * k + 2, :], ident[:])
                last.then_inc(pe_OT, 1)

            def W_(i, t):
                pe.wait_ge(act_OT, i * G + t + 1)
                pe.wait_ge(dve_OT, i * G + t + 1)
                if t == 0:
                    pe.wait_ge(pool_gT, i + 1)
                dst = PS[:, (bB, bD)[t], 0:D]
                for k in range(IC):
                    mm3(dst, both(oT, A, k), both(wout, A, k), start=(k == 0), stop=False)
                mm3(dst, both(gT, A, t), both(vo, A, t), start=False, stop=True).then_inc(pe_y0, 1)

            def ax_(j, g):
                if g == 1:
                    pe.wait_ge(dve_o3, j * G)
                pe.wait_ge(dve_x1, j * G + g + 1)
                pe.wait_ge(act_AT, j + 1)
                for c in range(DC):
                    last = pe.matmul(PS[:, (bP, bQ)[g], c * P:(c + 1) * P], x1[:, g, c * P:(c + 1) * P], AT[:, g, :],
                                     start=True, stop=True)
                last.then_inc(pe_ax, 1)

            def h_(j, g):
                pe.wait_ge(act_ax, j * G + g + 1)
                pe.wait_ge(dve_ax, j * G + g + 1)
                for c in range(DC):
                    last = mm3(PS[:, (bR, bP)[g], :], both(axT, A, g, c), both(w1t, A, c),
                               start=(c == 0), stop=(c == DC - 1))
                last.then_inc(pe_h, 1)

            def hT_(j, g):
                pe.wait_ge(dve_hn, j * G + g + 1)
                for k in range(HC):
                    last = pe.matmul(PS[:, (bQ, bR)[g], k * P:(k + 1) * P], hid[:, g, k * P:(k + 1) * P], AT[:, g, :],
                                     start=True, stop=True)
                last.then_inc(pe_hT, 1)

            def y1_(j, g):
                pe.wait_ge(act_hT, j * G + g + 1)
                pe.wait_ge(dve_hT, j * G + g + 1)
                for k in range(HC):
                    last = mm3(PS[:, (bP, bQ)[g], 0:D], both(hT, A, g, k), both(w2t, A, k),
                               start=(k == 0), stop=(k == HC - 1))
                last.then_inc(pe_y1, 1)

            def xT_(j, src, ready, done):
                pe.wait_ge(ready, j * G + G)
                for c in range(DC):
                    for g in range(G):
                        last = pe.transpose(PS[:, bR, (c * G + g) * P:(c * G + g + 1) * P],
                                            src[:, g, c * P:(c + 1) * P], ident[:])
                last.then_inc(done, 1)

            def Z_(j, g, i):
                if g == 0:
                    pe.wait_ge(act_xT2, j + 1)
                    pe.wait_ge(dve_xT2, j + 1)
                elif i is not None:
                    pe.wait_ge(act_AT, i + 1)
                for c in range(DC):
                    last = mm3(PS[:, (bP, bR)[g], :], both(xT2, A, c, g), both(wk01, A, c),
                               start=(c == 0), stop=(c == DC - 1))
                last.then_inc(pe_Z01, 1)
                for c in range(DC):
                    last = mm3(PS[:, (bQ, bA)[g], 0:D + 2], both(xT2, A, c, g), both(wk2, A, c),
                               start=(c == 0), stop=(c == DC - 1))
                last.then_inc(pe_Z2, 1)

            def si_(j):
                pe.wait_ge(dve_Z0, j * G + 1)
                pe.wait_ge(act_Z1, j * G + 1)
                for c in range(DC):
                    last = mm3(PS[:, bP, 0:G * P], both(wi, A, c), both(xT2, A, c), start=(c == 0), stop=(c == DC - 1))
                last.then_inc(pe_si, 1)

            def T1_(j, g):
                pe.wait_ge(dve_al, j * G + g + 1)
                pe.wait_ge(act_Z2, j * G + G)
                pe.wait_ge(dve_Z2, j * G + G)
                pe.wait_ge(dve_sj, j * G + G)
                pe.wait_ge(dve_Z0, j * G + G)
                pe.wait_ge(act_Z1, j * G + G)
                mm3(PS[:, (bA, bR)[g], 0:D + 2], both(alT, A, g), both(z2, A, g)).then_inc(pe_T1, 1)

            def T2_(j, g):
                if g == 0:
                    pe.wait_ge(dve_al, j * G + G)
                pe.wait_ge(act_Y, j * G + g + 1)
                pe.wait_ge(dve_Yl, j * G + g + 1)
                mm3(PS[:, (bP, bA)[g], 0:D], both(alT, A, g), both(yT, A, g)).then_inc(pe_T2, 1)

            def Z3_(j, g):
                pe.wait_ge(act_xT3, j + 1)
                pe.wait_ge(dve_xT3, j + 1)
                for c in range(DC):
                    last = mm3(PS[:, (bP, bA)[g], :], both(xT2, A, c, g), both(w3t, A, c),
                               start=(c == 0), stop=(c == DC - 1))
                last.then_inc(pe_Z3, 1)

            def T3_(j, g):
                pe.wait_ge(pool_aT, j + 1)
                pe.wait_ge(act_za, j * G + g + 1)
                pe.wait_ge(act_zb, j * G + g + 1)
                pe.wait_ge(dve_zb, j * G + g + 1)
                mm3(PS[:, (bQ, bE)[g], 0:D], both(aT, A, g), both(zb, A, g)).then_inc(pe_T3, 1)

            def group(i, j):
                F, B = i is not None, j is not None
                if F:
                    adjT_(i)
                    xT0_(i)
                if B:
                    ax_(j, 0)
                    ax_(j, 1)
                if F:
                    qk_(i, 0)
                    qk_(i, 1)
                if B:
                    h_(j, 0)
                    h_(j, 1)
                if F:
                    qk_(i, 2)
                    qk_(i, 3)
                    D_(i)
                    v_(i, 0)
                if B:
                    hT_(j, 0)
                if F:
                    DHT_(i)
                if B:
                    hT_(j, 1)
                if F:
                    v_(i, 1)
                if B:
                    y1_(j, 0)
                    y1_(j, 1)
                if F:
                    AT_(i)
                    S_(i, 0)
                if B:
                    xT_(j, x2, dve_x2, pe_xT2)
                if F:
                    S_(i, 1)
                if B:
                    Z_(j, 0, i)
                if F:
                    PT_(i, 0)
                if B:
                    Z_(j, 1, i)
                    si_(j)
                if F:
                    PV_(i, 0)
                    PT_(i, 1)
                    OT_(i, 0, j)
                if B:
                    T1_(j, 0)
                    T1_(j, 1)
                if F:
                    PV_(i, 1)
                if B:
                    T2_(j, 0)
                    T2_(j, 1)
                if F:
                    W_(i, 0)
                    OT_(i, 1, j)
                if B:
                    xT_(j, x3, dve_x3, pe_xT3)
                if F:
                    W_(i, 1)
                if B:
                    Z3_(j, 0)
                    Z3_(j, 1)
                    T3_(j, 0)
                    T3_(j, 1)

            set_up()
            set_up_done(pe)
            group(0, None)
            group(1, 0)
            with pe.Fori(1, ITERS - 1) as j:
                group(j + 1, j)
            group(None, ITERS - 1)

        @block.scalar
        def _(act):
            act.dma_start(wv2_raw[:], Wv.rearrange("(c p) n -> p c n", p=P)).then_inc(ld_vec, 16)
            act.dma_start(aw_bc[:], aw.rearrange("(t n) a -> t (n a)", t=2).partition_broadcast(P)).then_inc(ld_vec, 16)
            act.dma_start(bv_bc[:], bv.partition_broadcast(P)).then_inc(ld_vec, 16)
            act.dma_start(ab_bc[:], ab.partition_broadcast(P)).then_inc(ld_vec, 16)
            act.dma_start(bk_raw[:], bk.partition_broadcast(P)).then_inc(ld_vec, 16)
            act.dma_start(bout_bc[:], b_out.partition_broadcast(P)).then_inc(ld_vec, 16)
            act.dma_start(b1_bc[:], b1.partition_broadcast(P)).then_inc(ld_vec, 16)
            act.dma_start(b2_bc[:], b2.partition_broadcast(P)).then_inc(ld_vec, 16)
            act.dma_start(gamma_c[:], gamma.rearrange("(k p) -> p k", p=P), allow_slow_non_contiguous=True).then_inc(ld_gb, 16)
            act.dma_start(beta_c[:], beta.rearrange("(k p) -> p k", p=P), allow_slow_non_contiguous=True).then_inc(ld_gb, 16)
            act.dma_start(mask8[:], nodemask).then_inc(ld_mask, 16)

            copy = ACT.Copy

            def set_up():
                def move(dst, src, n):
                    act.wait_ge(set_pe, n)
                    act.activation(dst, src, copy).then_inc(set_copy, 1)

                act.wait_ge(ld_gb, 32)
                move(wvT[:].rearrange("p (b k) d -> p b (k d)", b=2), PS[:, bA:bA + 2, :], SET_WVT)
                move(w2T_raw[:].rearrange("p (b k) d -> p b (k d)", b=2), PS[:, bQ:bQ + 2, :], SET_W2T)
                for n, (src, hi, lo, factor, (ready, value)) in enumerate(splits):
                    act.wait_ge(ready, value)
                    if factor is None:
                        act.activation(hi, src, copy).then_inc(set_hi, 1)
                    else:
                        act.activation(hi, src, copy, scale=factor).then_inc(set_hi, 1)
                move(bw_bc[:], PS[:, bR, 0:D], SET_BW)
                move(mask33[:], PS[:, bA, 0:NG], SET_MASK)

            def adjT_(i):
                act.wait_ge(pe_adjT, i + 1)
                act.wait_ge(act_adjTb, i)
                act.activation(adjT[:].rearrange("p g n -> p (g n)"), PS[:, bA, 0:G * P], copy).then_inc(act_adjT, 1)

            def xT0_(i):
                act.wait_ge(pe_xT0, i + 1)
                act.activation(xT0[0][:].rearrange("p c g n -> p (c g n)"), PS[:, bB, :], copy).then_inc(act_xT0, 1)

            def gate_(i):
                act.wait_ge(act_adjT, i + 1)
                act.wait_ge(pool_gT, i)
                act.activation(gate[:], adjT[:], ACT.Exp, scale=-1.0).then_inc(act_gate, 1)

            def gT_(i):
                act.wait_ge(pool_gate, i + 1)
                act.activation(gT[0][:], gate[:], copy).then_inc(act_gT, 1)

            def carry(i):
                act.wait_ge(dve_al, i * G)
                act.wait_ge(pool_aT, i)
                act.activation(adjTb[:], adjT[:], copy).then_inc(act_adjTb, 1)

            def qk_(i, k):
                act.wait_ge(pe_qk, i * 4 + k + 1)
                act.activation(qk[:, 2 * k:2 * k + 2].rearrange("p m g n -> p (m g n)"),
                               PS[:, (bC, bD, bE, bC)[k], :], copy).then_inc(act_qk, 1)

            def v_(i, g):
                bv_, bo_ = ((bB, bD), (bE, bC))[g]
                act.wait_ge(pe_v, i * G + g + 1)
                act.activation(vext[:, g, :, 0:DH], PS[:, bv_, :].rearrange("p (h d) -> p h d", h=HEADS), copy)\
                    .then_inc(act_v, 1)
                act.wait_ge(pe_vo, i * G + g + 1)
                act.wait_ge(dve_m33, i + 1)
                act.activation(vo[0][:, g, :], PS[:, bo_, 0:D], copy, scale=m33[:, g:g + 1]).then_inc(act_vo, 1)

            def DHT_(i):
                act.wait_ge(pe_DHT, i + 1)
                act.activation(DHT[:].rearrange("p g n -> p (g n)"), PS[:, bA, 0:G * P], copy).then_inc(act_DHT, 1)

            def AT_(i):
                act.wait_ge(pe_AT, i + 1)
                act.activation(AT[:].rearrange("p g n -> p (g n)"), PS[:, bA, 0:G * P], copy).then_inc(act_AT, 1)

            def exp_(i, t):
                act.wait_ge(dve_sub, i * G + t + 1)
                act.activation(prob[:, t], prob[:, t], ACT.Exp, scale=SCALE).then_inc(act_exp, 1)

            def PT_(i, t):
                act.wait_ge(pe_PT, i * G + t + 1)
                act.activation(probT[:].rearrange("p (b k) n -> p b (k n)", b=2), PS[:, bB:bD + 1, :], copy)\
                    .then_inc(act_PT, 1)

            def OT_(i, t):
                act.wait_ge(pe_OT, i * G + t + 1)
                act.activation(oT[0][:].rearrange("p k n -> p (k n)"), PS[:, bQ, :], copy).then_inc(act_OT, 1)

            def u_(j, g):
                act.wait_ge(dve_Dn, j + 1)
                act.activation(resid[:, g], bw_bc[:], copy, scale=rA[:, g:g + 1]).then_inc(act_u, 1)

            def aT_(j):
                act.wait_ge(pe_T3, j * G)
                act.wait_ge(act_adjTb, j + 1)
                act.activation(aT[0][:], adjTb[:], copy).then_inc(act_aT, 1)

            def ax_(j, g):
                act.wait_ge(pe_ax, j * G + g + 1)
                act.activation(axT[0][:, g].rearrange("p c n -> p (c n)"), PS[:, (bP, bQ)[g], 0:D], copy)\
                    .then_inc(act_ax, 1)

            def relu_(j, g):
                act.wait_ge(dve_hb, j * G + g + 1)
                act.activation(hid[:, g], hid[:, g], ACT.Relu).then_inc(act_relu, 1)

            def hT_(j, g):
                act.wait_ge(pe_hT, j * G + g + 1)
                act.activation(hT[0][:, g].rearrange("p k n -> p (k n)"), PS[:, (bQ, bR)[g], :], copy)\
                    .then_inc(act_hT, 1)

            def xT_(j, pe_done, done):
                act.wait_ge(pe_done, j + 1)
                act.activation(xT2[0][:].rearrange("p c g n -> p (c g n)"), PS[:, bR, :], copy).then_inc(done, 1)

            def Z_(j, g):
                act.wait_ge(pe_Z01, j * G + g + 1)
                act.activation(z1[:, g], PS[:, (bP, bR)[g], D:2 * D], copy).then_inc(act_Z1, 1)
                act.wait_ge(pe_Z2, j * G + g + 1)
                act.activation(z2[0][:, g, 0:D], PS[:, (bQ, bA)[g], 0:D], copy).then_inc(act_Z2, 1)

            def E_(j, g):
                act.wait_ge(pe_si, j + 1)
                act.wait_ge(dve_sj, j * G + g + 1)
                src = PS[:, bP, g * P:(g + 1) * P]
                act.activation(e1[:, g], src, ACT.Exp, bias=sj[:, g, 0:1]).then_inc(act_E, 1)
                act.activation(e2[:, g], src, ACT.Exp, bias=sj[:, g, 1:2], scale=SLOPE).then_inc(act_E, 1)

            def Y_(j, g):
                act.wait_ge(dve_Y, j * G + g + 1)
                act.activation(yT[0][:, g], yv[:, g], copy).then_inc(act_Y, 1)

            def Z3_(j, g):
                act.wait_ge(pe_Z3, j * G + g + 1)
                act.activation(zb[0][:, g], PS[:, (bP, bA)[g], D:2 * D], copy).then_inc(act_zb, 1)
                act.activation(za[:, g], PS[:, (bP, bA)[g], 0:D], copy).then_inc(act_za, 1)

            def group(i, j):
                F, B = i is not None, j is not None
                if B:
                    u_(j, 0)
                    u_(j, 1)
                if F:
                    adjT_(i)
                    xT0_(i)
                if B:
                    ax_(j, 0)
                    ax_(j, 1)
                if F:
                    qk_(i, 0)
                    qk_(i, 1)
                    gate_(i)
                if B:
                    aT_(j)
                if B:
                    relu_(j, 0)
                if F:
                    qk_(i, 2)
                if B:
                    relu_(j, 1)
                if F:
                    qk_(i, 3)
                    v_(i, 0)
                if B:
                    hT_(j, 0)
                if F:
                    DHT_(i)
                if B:
                    hT_(j, 1)
                if F:
                    v_(i, 1)
                    gT_(i)
                    AT_(i)
                if B:
                    xT_(j, pe_xT2, act_xT2)
                if F:
                    exp_(i, 0)
                if B:
                    Z_(j, 0)
                if F:
                    PT_(i, 0)
                    exp_(i, 1)
                if B:
                    Z_(j, 1)
                    E_(j, 0)
                    E_(j, 1)
                if F:
                    PT_(i, 1)
                    OT_(i, 0)
                if B:
                    Y_(j, 0)
                    Y_(j, 1)
                if F:
                    OT_(i, 1)
                if B:
                    xT_(j, pe_xT3, act_xT3)
                    Z3_(j, 0)
                    Z3_(j, 1)
                if F:
                    carry(i)

            set_up()
            set_up_done(act)
            group(0, None)
            group(1, 0)
            with act.Fori(1, ITERS - 1) as j:
                group(j + 1, j)
            group(None, ITERS - 1)

        @block.vector
        def _(dve):
            def f32(t):
                return t.bitcast(F32)

            def set_up():
                dve.wait_ge(ld_wqkv, 16)
                dve.tensor_copy(wv_flat[:].rearrange("p c (h d) -> p c h d", h=HEADS), wqkv_raw[:, :, :, 2, :])\
                    .then_inc(set_flat, 1)
                dve.wait_ge(ld_mask, 16)
                dve.tensor_scalar(maskf[:], mask8[:], MIX, None, ALU.mult).then_inc(set_maskf, 1)
                dve.wait_ge(ld_gb, 32)
                dve.tensor_copy(beta_bc[:], beta_c[:].unsqueeze(2).to_broadcast([P, HC, P])).then_inc(set_beta, 1)
                dve.wait_ge(ld_vec, 16 * 8)
                for t in range(2):
                    dve.tensor_tensor(prod[:, t], wv2_raw[:], aw_bc[:, t:t + 1, :].to_broadcast([P, DC, D]), ALU.mult)\
                        .then_inc(set_prod, 1)
                dve.wait_ge(set_prod, 2)
                dve.tensor_reduce(wji[:], prod[:], AX_X, ALU.add).then_inc(set_wji, 1)
                dve.tensor_tensor(bprod[:], aw_bc[:], bv_bc[:].unsqueeze(1).to_broadcast([P, 2, D]), ALU.mult)\
                    .then_inc(set_prod, 1)
                dve.wait_ge(set_prod, 3)
                dve.tensor_reduce(bsum[:], bprod[:], AX_XY, ALU.add).then_inc(set_small, 1)
                dve.wait_ge(set_small, 1)
                dve.tensor_tensor(gate_c[:], bsum[:], ab_bc[:], ALU.add).then_inc(set_small, 1)
                dve.tensor_reduce(bk_bc[:], bk_raw[:].rearrange("p k d -> p d k"), AX_X, ALU.add).then_inc(set_small, 1)
                for n, (src, hi, lo, factor, (ready, value)) in enumerate(splits):
                    dve.wait_ge(set_hi, n + 1)
                    dve.wait_ge(ready, value)
                    if factor is None:
                        dve.tensor_tensor(lo, src, f32(hi), ALU.subtract).then_inc(set_lo, 1)
                    else:
                        dve.scalar_tensor_tensor(lo, src, factor, f32(hi), ALU.mult, ALU.subtract).then_inc(set_lo, 1)

            def low_part(lo, src, hi, hi_ready, value, done):
                dve.wait_ge(hi_ready, value)
                dve.tensor_tensor(lo, src, f32(hi), ALU.subtract).then_inc(done, 1)

            def stats(step, src, n, g, done):
                step.done(dve.bn_stats(st[:, n, g], src))
                settle(dve)
                dve.bn_aggr(mv[:, n, g], st[:, n, g]).then_inc(done, 1)

            def normalise(dst, src, n, g, scale_ready, value, done):
                dve.wait_ge(scale_ready, value)
                dve.tensor_scalar(dst, src, mv[:, n, g, 0:1], rs[:, n, g, 1:2], ALU.subtract, ALU.mult)\
                    .then_inc(done, 1)

            def front(i):
                step = Steps(dve, dve_fstep, i, DVE_FSTEPS)

                def xT0_():
                    low_part(xT0[1][:].rearrange("p c g n -> p (c g n)"), PS[:, bB, :],
                             xT0[0][:].rearrange("p c g n -> p (c g n)"), act_xT0, i + 1, dve_xT0)

                def incidence():
                    dve.wait_ge(act_adjT, i + 1)
                    dve.tensor_scalar(HT[:], adjT[:], 0.0, None, ALU.not_equal).then_inc(dve_HT, 1)
                    dve.tensor_copy(wone[:, :, 0:1], adjT[:, :, 0:1]).then_inc(dve_wone, 1)
                    dve.wait_ge(dve_HT, i + 1)
                    step.done(dve.tensor_reduce(cnt[:], HT[:], AX_X, ALU.add))
                    step.done(dve.tensor_scalar(cnt[:], cnt[:], 1.0, None, ALU.max))
                    dve.reciprocal(Be[:], cnt[:]).then_inc(dve_Be, 1)
                    dve.wait_ge(a_in, i * 16 + 16)
                    dve.tensor_reduce(degf[:], adj_in[:], AX_X, ALU.add).then_inc(dve_deg, 1)
                    dve.tensor_copy(m33[:], mask33[:, bass.ds(i * G, G)]).then_inc(dve_m33, 1)

                def Dn_():
                    dve.wait_ge(pe_D, i + 1)
                    step.done(dve.tensor_copy(dcol[:].rearrange("p g t -> p (g t)"), PS[:, bA, 0:2 * G]))
                    dve.tensor_scalar(dpos[:], dcol[:, :, 0], 0.0, None, ALU.is_gt).then_inc(dve_fstep, 1)
                    step.n += 1
                    step.done(dve.tensor_scalar(dsafe[:], dcol[:, :, 0], TINY, None, ALU.max))
                    step.done(dve.reciprocal(drec[:], dsafe[:]))
                    step.done(dve.tensor_tensor(Dn[:], drec[:], dpos[:], ALU.mult))
                    dve.wait_ge(act_u, i * G)
                    dve.tensor_tensor(rA[:], Dn[:], dcol[:, :, 1], ALU.mult).then_inc(dve_Dn, 1)
                    for g in range(G):
                        dve.tensor_scalar(DHn[:, g], adj_in[:, g], 0.0, Dn[:, g:g + 1], ALU.not_equal, ALU.mult)\
                            .then_inc(dve_DH, 1)

                def vo_(g):
                    dve.wait_ge(act_vo, i * G + g + 1)
                    dve.scalar_tensor_tensor(vo[1][:, g], PS[:, (bD, bC)[g], 0:D], m33[:, g:g + 1], f32(vo[0][:, g]),
                                             ALU.mult, ALU.subtract).then_inc(dve_vo, 1)

                def scores(t):
                    dve.wait_ge(pe_S, i * G + t + 1)
                    return (PS[:, bB:bD + 1, :], PS[:, bC:bE + 1, :])[t].rearrange("p b (h n) -> p b h n", n=P)

                def max_(t):
                    s = scores(t)
                    step.done(dve.tensor_reduce(m8[:, t].rearrange("p (b h) -> p b h", b=2), s, AX_X, ALU.max))

                def sub_(t):
                    s = scores(t)
                    m = m8[:, t].rearrange("p (b h) -> p b h", b=2).unsqueeze(3).to_broadcast([P, 2, HEADS // 2, P])
                    dve.tensor_tensor(prob[:, t].rearrange("p (b h) n -> p b h n", b=2), s, m, ALU.subtract)\
                        .then_inc(dve_sub, 1)

                def O_(t):
                    dve.wait_ge(pe_PV, i * G + t + 1)
                    o = PS[:, bC:bE + 1, 0:HEADS // 2 * VX].rearrange("p b (h d) -> p b h d", d=VX)
                    step.done(dve.reciprocal(rl[:, t], o[:, :, :, DH]))
                    dve.tensor_tensor(osb[:].rearrange("p (b h) d -> p b h d", b=2), o[:, :, :, 0:DH],
                                      rl[:, t].unsqueeze(3).to_broadcast([P, 2, HEADS // 2, DH]), ALU.mult)\
                        .then_inc(dve_O, 1)

                def OT_(t):
                    low_part(oT[1][:].rearrange("p k n -> p (k n)"), PS[:, bQ, :],
                             oT[0][:].rearrange("p k n -> p (k n)"), act_OT, i * G + t + 1, dve_OT)

                def y0_(t):
                    dve.wait_ge(pe_y0, i * G + t + 1)
                    dve.wait_ge(pool_resid0, i + 1)
                    dve.tensor_tensor(ys0[:, t], PS[:, (bB, bD)[t], 0:D], ys0[:, t], ALU.add).then_inc(dve_y0, 1)
                    dve.wait_ge(dve_y0, i * G + t + 1)
                    stats(step, ys0[:, t], NORM0, t, dve_mv0)

                def x1_(t):
                    normalise(x1[:, t], ys0[:, t], NORM0, t, pool_rs0, i * G + t + 1, dve_x1)

                return step, xT0_, incidence, Dn_, vo_, max_, sub_, O_, OT_, y0_, x1_

            def back(j):
                step = Steps(dve, dve_bstep, j, DVE_BSTEPS)

                def ax_(g):
                    low_part(axT[1][:, g].rearrange("p c n -> p (c n)"), PS[:, (bP, bQ)[g], 0:D],
                             axT[0][:, g].rearrange("p c n -> p (c n)"), act_ax, j * G + g + 1, dve_ax)

                def hb_(g):
                    dve.wait_ge(pe_h, j * G + g + 1)
                    dve.tensor_tensor(hid[:, g], PS[:, (bR, bP)[g], :], b1_bc[:], ALU.add).then_inc(dve_hb, 1)

                def hstats_(g):
                    dve.wait_ge(act_relu, j * G + g + 1)
                    stats(step, hid[:, g], NORMH, g, dve_mvh)

                def hn_(g):
                    normalise(hid[:, g], hid[:, g], NORMH, g, pool_rsh, j * G + g + 1, dve_hn)

                def hT_(g):
                    low_part(hT[1][:, g].rearrange("p k n -> p (k n)"), PS[:, (bQ, bR)[g], :],
                             hT[0][:, g].rearrange("p k n -> p (k n)"), act_hT, j * G + g + 1, dve_hT)

                def y1_(g):
                    dve.wait_ge(pe_y1, j * G + g + 1)
                    dve.wait_ge(pool_resid1, j * G + g + 1)
                    dve.wait_ge(pool_out, j * G)
                    step.done(dve.tensor_tensor(ysb[:, g], PS[:, (bP, bQ)[g], 0:D], resid[:, g], ALU.add))
                    stats(step, ysb[:, g], NORM1, g, dve_mv1)

                def x2_(g):
                    normalise(x2[:, g], ysb[:, g], NORM1, g, pool_rs1, j * G + g + 1, dve_x2)

                def xT_(hi_ready, done):
                    low_part(xT2[1][:].rearrange("p c g n -> p (c g n)"), PS[:, bR, :],
                             xT2[0][:].rearrange("p c g n -> p (c g n)"), hi_ready, j + 1, done)

                def Z_(g):
                    dve.wait_ge(act_Z1, j * G + g + 1)
                    dve.tensor_tensor(z0[:, g], PS[:, (bP, bR)[g], 0:D], bk_bc[:], ALU.add).then_inc(dve_Z0, 1)
                    low_part(z2[1][:, g, 0:D], PS[:, (bQ, bA)[g], 0:D], z2[0][:, g, 0:D], act_Z2, j * G + g + 1,
                             dve_Z2)
                    s = PS[:, (bQ, bA)[g], D:D + 1]
                    step.done(dve.tensor_tensor(sj[:, g, 0:1], s, gate_c[:], ALU.add))
                    dve.tensor_scalar(sj[:, g, 1:2], sj[:, g, 0:1], SLOPE, None, ALU.mult).then_inc(dve_sj, 1)

                def al_(g):
                    dve.wait_ge(act_E, j * 2 * G + 2 * g + 2)
                    step.done(dve.tensor_tensor(al[:, g], e1[:, g], e2[:, g], ALU.max))
                    dve.wait_ge(act_adjTb, j + 1)
                    step.done(dve.tensor_tensor(al[:, g], al[:, g], adjTb[:, g], ALU.mult))
                    step.done(dve.tensor_copy(alT[0][:, g], al[:, g]))
                    dve.tensor_tensor(alT[1][:, g], al[:, g], f32(alT[0][:, g]), ALU.subtract).then_inc(dve_al, 1)

                def Y_(g):
                    dve.wait_ge(pe_T1, j * G + g + 1)
                    dve.wait_ge(act_Z1, j * G + g + 1)
                    b = (bA, bR)[g]
                    step.done(dve.tensor_scalar(den[:, g:g + 1], PS[:, b, D:D + 1], DEN_EPS, None, ALU.add))
                    step.done(dve.reciprocal(rden[:, g:g + 1], den[:, g:g + 1]))
                    dve.scalar_tensor_tensor(yv[:, g], PS[:, b, 0:D], rden[:, g:g + 1], z1[:, g], ALU.mult, ALU.add)\
                        .then_inc(dve_Y, 1)

                def Yl_(g):
                    low_part(yT[1][:, g], yv[:, g], yT[0][:, g], act_Y, j * G + g + 1, dve_Yl)

                def o2_(g):
                    dve.wait_ge(pe_T2, j * G + g + 1)
                    dve.scalar_tensor_tensor(ysb[:, g], PS[:, (bP, bA)[g], 0:D], rden[:, g:g + 1], z0[:, g],
                                             ALU.mult, ALU.add).then_inc(dve_o2, 1)
                    dve.wait_ge(dve_o2, j * G + g + 1)
                    step.done(dve.scalar_tensor_tensor(ysb[:, g], ysb[:, g], 0.0, x2[:, g], ALU.max, ALU.add))
                    stats(step, ysb[:, g], NORM2, g, dve_mv2)

                def x3_(g):
                    normalise(x3[:, g], ysb[:, g], NORM2, g, pool_rs2, j * G + g + 1, dve_x3)

                def deg_():
                    step.done(dve.tensor_scalar(degb[:], degf[:], DEG_EPS, None, ALU.max))
                    step.done(dve.reciprocal(degb[:], degb[:]))

                def zb_(g):
                    dve.wait_ge(act_za, j * G + g + 1)
                    low_part(zb[1][:, g], PS[:, (bP, bA)[g], D:2 * D], zb[0][:, g], act_zb, j * G + g + 1, dve_zb)

                def o3_(g):
                    dve.wait_ge(pe_T3, j * G + g + 1)
                    dve.scalar_tensor_tensor(ysb[:, g], PS[:, (bQ, bE)[g], 0:D], degb[:, g:g + 1], za[:, g],
                                             ALU.mult, ALU.add).then_inc(dve_o3, 1)
                    dve.wait_ge(dve_o3, j * G + g + 1)
                    step.done(dve.scalar_tensor_tensor(ysb[:, g], ysb[:, g], 0.0, x3[:, g], ALU.max, ALU.add))
                    stats(step, ysb[:, g], NORM3, g, dve_mv3)

                return (step, ax_, hb_, hstats_, hn_, hT_, y1_, x2_, xT_, Z_, al_, Y_, Yl_, o2_, x3_, deg_, zb_,
                        o3_)

            def group(i, j):
                F, B = i is not None, j is not None
                if F:
                    fstep, xT0_, incidence, Dn_, vo_, max_, sub_, O_, fOT_, y0_, x1_ = front(i)
                if B:
                    (bstep, ax_, hb_, hstats_, hn_, hT_, y1_, x2_, xT_, Z_, al_, Y_, Yl_, o2_, x3_, deg_, zb_,
                     o3_) = back(j)
                    deg_()
                if F:
                    xT0_()
                if B:
                    ax_(0)
                    ax_(1)
                if F:
                    incidence()
                if B:
                    hb_(0)
                    hb_(1)
                    hstats_(0)
                    hstats_(1)
                    hn_(0)
                    hn_(1)
                if F:
                    Dn_()
                    vo_(0)
                if B:
                    hT_(0)
                    hT_(1)
                if F:
                    vo_(1)
                if B:
                    y1_(0)
                    y1_(1)
                    x2_(0)
                    x2_(1)
                if F:
                    max_(0)
                    sub_(0)
                if B:
                    xT_(act_xT2, dve_xT2)
                if F:
                    max_(1)
                if B:
                    Z_(0)
                if F:
                    sub_(1)
                if B:
                    Z_(1)
                    al_(0)
                if F:
                    O_(0)
                if B:
                    al_(1)
                if F:
                    fOT_(0)
                if B:
                    Y_(0)
                    Y_(1)
                    Yl_(0)
                    Yl_(1)
                if F:
                    O_(1)
                if B:
                    o2_(0)
                    o2_(1)
                    x3_(0)
                    x3_(1)
                if F:
                    fOT_(1)
                    y0_(0)
                if B:
                    xT_(act_xT3, dve_xT3)
                if F:
                    y0_(1)
                    x1_(0)
                    x1_(1)
                if B:
                    zb_(0)
                    zb_(1)
                    o3_(0)
                    o3_(1)
                if F:
                    assert fstep.n == DVE_FSTEPS, fstep.n
                if B:
                    assert bstep.n == DVE_BSTEPS, bstep.n

            set_up()
            set_up_done(dve)
            group(0, None)
            group(1, 0)
            with dve.Fori(1, ITERS - 1) as j:
                group(j + 1, j)
            group(None, ITERS - 1)

        @block.gpsimd
        def _(pool):
            def set_up():
                pool.memset(ident[:], 0.0).then_inc(ident_ok, 1)
                pool.wait_ge(ident_ok, 1)
                pool.affine_select(out=ident[:], in_=ident[:], compare_op=ALU.not_equal, fill=1.0, base=0,
                                   pattern=[[-1, P]], channel_multiplier=1).then_inc(ident_ok, 1)
                pool.memset(vext[:, :, :, DH:VX], 1.0 / MIX).then_inc(pool_const, 1)
                pool.memset(z2[0][:, :, D:D + 2].bitcast(F32), 1.0).then_inc(pool_const, 1)
                pool.memset(z2[1][:, :, D:D + 2].bitcast(F32), 0.0).then_inc(pool_const, 1)
                pool.memset(wone[:, :, 1:2], 1.0).then_inc(pool_const, 1)
                pool.memset(wk2[0][:, :, D + 1:D + 2].bitcast(F32), 0.0).then_inc(pool_const, 1)
                pool.memset(wk2[1][:, :, D + 1:D + 2].bitcast(F32), 0.0).then_inc(pool_const, 1)
                pool.memset(mhalf[:], -0.5).then_inc(pool_const, 1)
                pool.memset(eps_c[:], LN_EPS).then_inc(pool_const, 1)
                pool.memset(mrow_l[:], 0.0).then_inc(pool_const, 1)
                pool.memset(mrow_r[:], 0.0).then_inc(pool_const, 1)
                for col, first, second in ((0, BIG, 1.0), (1, -BIG, 0.0), (2, 0.0, BIG), (3, 1.0, -BIG)):
                    pool.memset(mask_ab[:, col:col + 1], second).then_inc(pool_const, 1)
                for base in (0, DH):
                    pool.wait_ge(pool_const, 14)
                    for col, first in enumerate((BIG, -BIG, 0.0, 1.0)):
                        last = pool.memset(mask_ab[base:base + 1, col:col + 1], first)
                    last.then_inc(pool_const, 1)

            def scale(step, n, g, ready, value):
                pool.wait_ge(ready, value)
                step.done(pool.tensor_tensor(rs[:, n, g, 0:1], mv[:, n, g, 1:2], eps_c[:], ALU.add))
                return pool.tensor_tensor(rs[:, n, g, 1:2], rs[:, n, g, 0:1], mhalf[:], ALU.pow)

            def front(i):
                step = Steps(pool, pool_fstep, i, POOL_FSTEPS)

                def mask_(j):
                    pool.wait_ge(m_in, i * 16 + 16)
                    pool.wait_ge(pe_S, i * G)
                    pool.wait_ge(pool_rs0, i * G)
                    if j is not None:
                        pool.wait_ge(pool_out, j * G)
                    settle(pool)
                    for base in (0, DH):
                        rows = mask_bc8[base:base + 2, :]
                        for dst, a in ((mrow_l, 0), (mrow_r, 2)):
                            pool.tensor_scalar(dst[base:base + 2].rearrange("p g n -> p (g n)"), rows,
                                               mask_ab[base:base + 2, a:a + 1], mask_ab[base:base + 2, a + 1:a + 2],
                                               ALU.mult, ALU.add).then_inc(pool_mrow, 1)
                    pool.wait_ge(pool_mrow, i * 4 + 4)
                    settle(pool)
                    pool.tensor_copy(mbc[:], mask_bc8[:]).then_inc(pool_mbc, 1)

                def operator():
                    pool.wait_ge(dve_Be, i + 1)
                    settle(pool)
                    for g in range(G):
                        pool.tensor_scalar(BHT[:, g], HT[:, g], Be[:, g:g + 1], None, ALU.mult)\
                            .then_inc(pool_BHT, 1)

                def resid_():
                    pool.wait_ge(x_in, i * 16 + 16)
                    pool.tensor_tensor(ys0[:], xin[:], bout_bc[:].unsqueeze(1).to_broadcast([P, G, D]), ALU.add)\
                        .then_inc(pool_resid0, 1)

                def gate_():
                    pool.wait_ge(act_gate, i + 1)
                    pool.wait_ge(pool_mbc, i + 1)
                    flat = gate[:].rearrange("p g n -> p (g n)")
                    step.done(pool.tensor_tensor(gate[:], gate[:], adjT[:], ALU.add))
                    pool.tensor_tensor(flat, flat, mbc[:], ALU.mult).then_inc(pool_gate, 1)

                def gT_():
                    pool.wait_ge(act_gT, i + 1)
                    pool.tensor_tensor(gT[1][:], gate[:], gT[0][:].bitcast(F32), ALU.subtract).then_inc(pool_gT, 1)

                def rs0_(t):
                    scale(step, NORM0, t, dve_mv0, i * G + t + 1).then_inc(pool_rs0, 1)

                return step, mask_, operator, resid_, gate_, gT_, rs0_

            def back(j):
                step = Steps(pool, pool_bstep, j, POOL_BSTEPS)

                def resid_(g):
                    pool.wait_ge(act_u, j * G + g + 1)
                    step.done(pool.tensor_tensor(resid[:, g], resid[:, g], b2_bc[:], ALU.add))
                    pool.wait_ge(dve_x1, j * G + g + 1)
                    step.done(pool.tensor_tensor(resid[:, g], resid[:, g], x1[:, g], ALU.add))
                    pool.tensor_tensor(resid[:, g], resid[:, g], x1[:, g], ALU.add).then_inc(pool_resid1, 1)

                def rsh_(g):
                    scale(step, NORMH, g, dve_mvh, j * G + g + 1).then_inc(pool_rsh, 1)

                def rs1_(g):
                    scale(step, NORM1, g, dve_mv1, j * G + g + 1).then_inc(pool_rs1, 1)

                def rs2_(g):
                    scale(step, NORM2, g, dve_mv2, j * G + g + 1).then_inc(pool_rs2, 1)

                def out_(g):
                    step.done(scale(step, NORM3, g, dve_mv3, j * G + g + 1))
                    if g == 0:
                        pool.wait_ge(y_out, j * 16)
                    settle(pool)
                    pool.tensor_scalar(xout[:, g], ysb[:, g], mv[:, NORM3, g, 0:1], rs[:, NORM3, g, 1:2],
                                       ALU.subtract, ALU.mult).then_inc(pool_out, 1)

                def aT_():
                    pool.wait_ge(act_aT, j + 1)
                    pool.tensor_tensor(aT[1][:], adjTb[:], aT[0][:].bitcast(F32), ALU.subtract).then_inc(pool_aT, 1)

                return step, resid_, rsh_, rs1_, rs2_, out_, aT_

            def group(i, j):
                F, B = i is not None, j is not None
                if F:
                    fstep, mask_, operator, fresid_, gate_, gT_, rs0_ = front(i)
                if B:
                    bstep, resid_, rsh_, rs1_, rs2_, out_, aT_ = back(j)
                if F:
                    mask_(j)
                if B:
                    resid_(0)
                if F:
                    operator()
                if B:
                    rsh_(0)
                    rsh_(1)
                    resid_(1)
                if F:
                    fresid_()
                    gate_()
                    gT_()
                if B:
                    rs1_(0)
                    rs1_(1)
                    aT_()
                    rs2_(0)
                    rs2_(1)
                if F:
                    rs0_(0)
                    rs0_(1)
                if B:
                    out_(0)
                    out_(1)
                if F:
                    assert fstep.n == POOL_FSTEPS, fstep.n
                if B:
                    assert bstep.n == POOL_BSTEPS, bstep.n

            set_up()
            set_up_done(pool)
            group(0, None)
            group(1, 0)
            with pool.Fori(1, ITERS - 1) as j:
                group(j + 1, j)
            group(None, ITERS - 1)


_INS = ['x', 'adj', 'nodemask', 'L0_gnn_W_qkv', 'L0_gnn_W_out', 'L0_gnn_b_out', 'L1_gnn_W1', 'L1_gnn_b1',
        'L1_gnn_gamma', 'L1_gnn_beta', 'L1_gnn_W2', 'L1_gnn_b2', 'L2_gnn_Wv', 'L2_gnn_bv', 'L2_gnn_aw', 'L2_gnn_ab',
        'L2_gnn_Wk', 'L2_gnn_bk', 'L3_gnn_W']


def kernel(**inputs):
    import numpy as _np
    import concourse.bacc as _bacc
    from concourse import mybir as _mybir
    from concourse.bass_utils import run_bass_kernel_spmd as _run

    nc = _bacc.Bacc("TRN2", target_bir_lowering=False, num_devices=1)
    arrays, args = {}, []
    for name in _INS:
        a = _np.ascontiguousarray(inputs[name])
        if a.dtype == _np.bool_:
            a = a.view(_np.uint8)
        arrays[f"in_{name}_dram"] = a
        args.append(nc.dram_tensor(f"in_{name}_dram", a.shape, _mybir.dt.from_np(a.dtype), kind="ExternalInput").ap())
    shape = tuple(inputs["x"].shape)
    args.append(nc.dram_tensor("out_0_dram", shape, _mybir.dt.float32, kind="ExternalOutput").ap())
    gnn_stack_kernel(nc, *args)
    r = _run(nc, [arrays], core_ids=[0])
    return r.results[0]["out_0_dram"]
```

```python
from contextlib import ExitStack

import concourse.bass as bass
from concourse import mybir

F32 = mybir.dt.float32
F32R = mybir.dt.float32r
BF16 = mybir.dt.bfloat16
U8 = mybir.dt.uint8
ALU = mybir.AluOpType
ACT = mybir.ActivationFunctionType
AX_X = mybir.AxisListType.X
AX_XY = mybir.AxisListType.XY

P = 128
HEADS = 8
DH = 64
MIX = 0.33
LN_EPS = 1e-5
DEG_EPS = 1e-6
DEN_EPS = 1e-12
TINY = 1.2e-38
SLOPE = 0.2
BIG = float(2.0 ** 100)


def gnn_stack_kernel(nc, x, adj, nodemask, W_qkv, W_out, b_out, W1, b1, gamma, beta, W2, b2,
                     Wv, bv, aw, ab, Wk, bk, W3, out):
    NG, N, D = x.shape
    G = 2
    ITERS = NG // G
    DC = D // P
    INNER = HEADS * DH
    IC = INNER // P
    DHID = W1.shape[0]
    HC = DHID // P
    QKB = 2 * INNER // P
    SCALE = float(DH) ** -0.5
    VX = DH + 1
    assert N == P and D == 256 and DHID == 512 and INNER == 512 and QKB == 8

    ctx = ExitStack()
    with ctx:
        free = nc.sbuf_bytes_remaining - 64
        arena = ctx.enter_context(nc.sbuf_tensor("arena", [P, free // 4], F32))
        arena_base = (nc.sbuf_base - free + 31) // 32 * 32
        place = [arena_base]

        def at(name, shape, dt=F32, keep=True):
            size = 1
            for n in shape[1:]:
                size *= n
            size *= {F32: 4, F32R: 4, BF16: 2, U8: 1}[dt]
            t = nc.alloc_sbuf_tensor_at(name, shape, dt, offset=place[0])
            place[0] += (size + 31) // 32 * 32
            assert place[0] <= arena_base + free - 32, (name, place[0])
            return t

        def pair(name, shape):
            return at(name + "_hi", shape, F32R), at(name + "_lo", shape, F32R)

        ident = at("ident", [P, P])
        wqk = pair("wqk", [P, DC, 2, HEADS, DH])
        wvo = pair("wvo", [P, DC, INNER + D])
        wout = pair("wout", [P, IC, D])
        w1t = pair("w1t", [P, DC, DHID])
        w2t = pair("w2t", [P, HC, D])
        wk01 = pair("wk01", [P, DC, 2, D])
        wk2 = pair("wk2", [P, DC, D + 2])
        wi = pair("wi", [P, DC, P])
        w3t = pair("w3t", [P, DC, 2, D])
        bout_bc = at("bout_bc", [P, D])
        b1_bc = at("b1_bc", [P, DHID])
        b2_bc = at("b2_bc", [P, D])
        bk_bc = at("bk_bc", [P, D])
        bw_bc = at("bw_bc", [P, D])
        mask33 = at("mask33", [P, NG])
        gate_c = at("gate_c", [P, 1])
        mask_ab = at("mask_ab", [P, 4])
        mhalf = at("mhalf", [P, 1])
        eps_c = at("eps_c", [P, 1])

        vext = at("vext", [P, G, HEADS, VX])
        z2 = pair("z2", [P, G, D + 2])
        wone = at("wone", [P, G, 2])
        mrow_l = at("mrow_l", [P, G, P], BF16)
        mrow_r = at("mrow_r", [P, G, P], BF16)
        xin = at("xin", [P, G, D])
        adj_in = at("adj_in", [P, G, P])
        mask_bc8 = at("mask_bc8", [P, G * P], U8)
        work_base = place[0]

        adjT = at("adjT", [P, G, P])
        adjTb = at("adjTb", [P, G, P])
        gate = at("gate", [P, G, P])
        gT = pair("gT", [P, G, P])
        aT = pair("aT", [P, G, P])
        HT = at("HT", [P, G, P])
        BHT = at("BHT", [P, G, P])
        DHn = at("DHn", [P, G, P])
        DHT = at("DHT", [P, G, P])
        AT = at("AT", [P, G, P])
        mbc = at("mbc", [P, G * P])
        xT0 = pair("xT0", [P, DC, G, P])
        xT2 = pair("xT2", [P, DC, G, P])
        qk = at("qk", [P, QKB, G, P])
        vo = pair("vo", [P, G, D])
        prob = at("prob", [P, 2, HEADS, P])
        probT = at("probT", [P, HEADS, P])
        osb = at("osb", [P, HEADS, DH])
        oT = pair("oT", [P, G, IC, P])
        ys0 = at("ys0", [P, G, D])
        ysb = at("ysb", [P, G, D])
        x1 = at("x1", [P, G, D])
        x2 = at("x2", [P, G, D])
        x3 = at("x3", [P, G, D])
        xout = at("xout", [P, G, D])
        resid = at("resid", [P, G, D])
        x1_twice = at("x1_twice", [P, G, D])
        axT = pair("axT", [P, G, DC, P])
        hid = at("hid", [P, G, DHID])
        hT = pair("hT", [P, G, HC, P])
        z01 = at("z01", [P, G, 2, D])
        e1 = at("e1", [P, G, P])
        e2 = at("e2", [P, G, P])
        al = at("al", [P, G, P])
        alT = pair("alT", [P, G, P])
        yv = at("yv", [P, G, D])
        yT = pair("yT", [P, G, D])
        za = at("za", [P, G, D])
        zb = pair("zb", [P, G, D])
        m33 = at("m33", [P, G])
        cnt = at("cnt", [P, G])
        Be = at("Be", [P, G])
        degf = at("degf", [P, G])
        degb = at("degb", [P, G])
        dcol = at("dcol", [P, G, 2])
        dpos = at("dpos", [P, G])
        dsafe = at("dsafe", [P, G])
        drec = at("drec", [P, G])
        Dn = at("Dn", [P, G])
        rA = at("rA", [P, G])
        m8 = at("m8", [P, G, HEADS])
        rl = at("rl", [P, G, 2, HEADS // 2])
        sj = at("sj", [P, G, 2])
        den = at("den", [P, G])
        rden = at("rden", [P, G])
        NORM0, NORMH, NORM1, NORM2, NORM3 = range(5)
        st = at("st", [P, 5, G, 6])
        mv = at("mv", [P, 5, G, 2])
        rs = at("rs", [P, 5, G, 2])
        work_end = place[0]

        place[0] = work_base
        wqkv_raw = at("wqkv_raw", [P, DC, HEADS, 3, DH])
        wv_flat = at("wv_flat", [P, DC, INNER])
        wout_raw = at("wout_raw", [P, IC, D])
        w1_raw = at("w1_raw", [P, HC, D])
        w2_raw = at("w2_raw", [P, DC, DHID])
        w3_raw = at("w3_raw", [P, DC, 2 * D])
        wk_raw = at("wk_raw", [P, 3, DC, D])
        wv2_raw = at("wv2_raw", [P, DC, D])
        aw_bc = at("aw_bc", [P, 2, D])
        bv_bc = at("bv_bc", [P, D])
        ab_bc = at("ab_bc", [P, 1])
        bk_raw = at("bk_raw", [P, 3, D])
        gamma_c = at("gamma_c", [P, HC])
        beta_c = at("beta_c", [P, HC])
        beta_bc = at("beta_bc", [P, HC, P])
        wvT = at("wvT", [P, IC, D])
        w2T_raw = at("w2T_raw", [P, HC, D])
        prod = at("prod", [P, 2, DC, D])
        wji = at("wji", [P, 2, DC])
        bprod = at("bprod", [P, 2, D])
        bsum = at("bsum", [P, 1])
        mask8 = at("mask8", [NG, P], U8)
        maskf = at("maskf", [NG, P])
        assert place[0] <= work_end

        PS = ctx.enter_context(nc.psum_tensor("PS", [P, 8, 512], F32))
        bA, bB, bD, bC, bE, bP, bQ, bR = range(8)

        def sem(name):
            return ctx.enter_context(nc.semaphore(name))

        ld_wqkv, ld_wout, ld_w1, ld_w2, ld_w3, ld_wk, ld_vec, ld_mask, ld_gb = (
            sem(n) for n in ("ld_wqkv", "ld_wout", "ld_w1", "ld_w2", "ld_w3", "ld_wk", "ld_vec", "ld_mask", "ld_gb"))
        ident_ok = sem("ident_ok")
        pool_const = sem("pool_const")
        set_flat = sem("set_flat")
        set_maskf = sem("set_maskf")
        set_beta = sem("set_beta")
        set_prod = sem("set_prod")
        set_wji = sem("set_wji")
        set_pe = sem("set_pe")
        set_copy = sem("set_copy")
        set_hi = sem("set_hi")
        set_lo = sem("set_lo")
        set_small = sem("set_small")
        x_in, a_in, m_in, y_out = (sem(n) for n in ("x_in", "a_in", "m_in", "y_out"))
        (pe_adjT, pe_xT0, pe_qk, pe_D, pe_v, pe_vo, pe_DHT, pe_AT, pe_S, pe_PT, pe_PV, pe_OT, pe_y0) = (
            sem("pe_" + n) for n in ("adjT", "xT0", "qk", "D", "v", "vo", "DHT", "AT", "S", "PT", "PV", "OT", "y0"))
        (act_adjT, act_xT0, act_gate, act_qk, act_v, act_vo, act_DHT, act_AT, act_exp, act_PT, act_OT,
         act_gT, act_adjTb, act_mrow, act_mbc) = (
            sem("act_" + n) for n in ("adjT", "xT0", "gate", "qk", "v", "vo", "DHT", "AT", "exp", "PT", "OT",
                                        "gT", "adjTb", "mrow", "mbc"))
        (dve_xT0, dve_HT, dve_wone, dve_m33, dve_Be, dve_Dn, dve_DH, dve_vo, dve_sub, dve_O, dve_OT, dve_y0, dve_mv0,
         dve_deg, dve_x1) = (sem("dve_" + n) for n in ("xT0", "HT", "wone", "m33", "Be", "Dn", "DH", "vo", "sub", "O", "OT", "y0",
                                                "mv0", "deg", "x1"))
        (pool_resid0, pool_BHT, pool_gate, pool_gT, pool_rs0) = (
            sem("pool_" + n) for n in ("resid0", "BHT", "gate", "gT", "rs0"))
        (pe_ax, pe_h, pe_hT, pe_y1, pe_xT2, pe_Z01, pe_Z2, pe_si, pe_T1, pe_T2, pe_xT3, pe_Z3, pe_T3) = (
            sem("pe_" + n) for n in ("ax", "h", "hT", "y1", "xT2", "Z01", "Z2", "si", "T1", "T2", "xT3", "Z3", "T3"))
        (act_ax, act_relu, act_hT, act_xT2, act_Z01, act_Z2, act_E, act_Y, act_xT3, act_za, act_zb,
         act_u, act_aT, act_x1) = (
            sem("act_" + n) for n in ("ax", "relu", "hT", "xT2", "Z01", "Z2", "E", "Y", "xT3", "za", "zb", "u",
                                        "aT", "x1"))
        (dve_ax, dve_hb, dve_mvh, dve_hT, dve_mv1, dve_xT2, dve_Z2, dve_sj, dve_al, dve_Y, dve_Yl, dve_o2,
         dve_mv2, dve_xT3, dve_zb, dve_o3, dve_mv3, dve_hn, dve_x2, dve_x3) = (
            sem("dve_" + n) for n in ("ax", "hb", "mvh", "hT", "mv1", "xT2", "Z2", "sj", "al", "Y", "Yl", "o2",
                                      "mv2", "xT3", "zb", "o3", "mv3", "hn", "x2", "x3"))
        (pool_resid1, pool_rsh, pool_rs1, pool_rs2, pool_aT, pool_z0, pool_out) = (
            sem("pool_" + n) for n in ("resid1", "rsh", "rs1", "rs2", "aT", "z0", "out"))
        dve_fstep, dve_bstep, pool_fstep, pool_bstep = (
            sem(n) for n in ("dve_fstep", "dve_bstep", "pool_fstep", "pool_bstep"))

        DVE_FSTEPS, DVE_BSTEPS, POOL_FSTEPS, POOL_BSTEPS = 7 + 3 * G, 5 + 10 * G, 1 + G, 6 * G

        class Steps:

            def __init__(self, eng, counter, i, per_group):
                self.eng, self.counter, self.i, self.per_group, self.n = eng, counter, i, per_group, 0

            def done(self, ins):
                self.n += 1
                ins.then_inc(self.counter, 1)
                self.eng.wait_ge(self.counter, self.i * self.per_group + self.n)

        raw = wqkv_raw
        splits = []
        for c in range(DC):
            splits.append((raw[:, c, :, 0:2, :].rearrange("p h t d -> p t h d"), wqk[0][:, c], wqk[1][:, c], None,
                           (ld_wqkv, 16)))
        for c in range(DC):
            splits.append((raw[:, c, :, 2, :], wvo[0][:, c, 0:INNER].rearrange("p (h d) -> p h d", h=HEADS),
                           wvo[1][:, c, 0:INNER].rearrange("p (h d) -> p h d", h=HEADS), None, (ld_wqkv, 16)))
        splits.append((wout_raw[:], wout[0][:], wout[1][:], None, (ld_wout, 16)))
        for k in range(2):
            splits.append((wk_raw[:, k], wk01[0][:, :, k, :], wk01[1][:, :, k, :], None, (ld_wk, 48)))
        splits.append((wk_raw[:, 2], wk2[0][:, :, 0:D], wk2[1][:, :, 0:D], None, (ld_wk, 48)))
        splits.append((wji[:, 0, :], wk2[0][:, :, D], wk2[1][:, :, D], None, (set_wji, 1)))
        for c in range(DC):
            splits.append((wji[:, 1, c:c + 1].to_broadcast([P, P]), wi[0][:, c, :], wi[1][:, c, :], None,
                           (set_wji, 1)))
        SET_WVT, SET_W2T, SET_W1, SET_W3, SET_WVO, SET_BW, SET_MASK = 1, 2, 3, 4, 5, 6, 7
        for c in range(DC):
            splits.append((PS[:, 2 + c, :], w1t[0][:, c], w1t[1][:, c], None, (set_pe, SET_W1)))
        for c in range(DC):
            splits.append((PS[:, 4 + c, :].rearrange("p (t o) -> p t o", t=2), w3t[0][:, c], w3t[1][:, c], None,
                           (set_pe, SET_W3)))
        splits.append((PS[:, bQ, :].rearrange("p (c d) -> p c d", c=DC), wvo[0][:, :, INNER:], wvo[1][:, :, INNER:],
                       None, (set_pe, SET_WVO)))
        for k in range(HC):
            splits.append((w2T_raw[:, k], w2t[0][:, k], w2t[1][:, k], gamma_c[:, k:k + 1], (set_copy, 2)))
        N_SPLITS = len(splits)
        N_COPIES = 4
        N_SMALL = 3

        xg = x.rearrange("g n d -> n g d")
        ag = adj.rearrange("g n m -> n g m")
        og = out.rearrange("g n d -> n g d")
        mask_rows = nodemask.rearrange("(i g) n -> i (g n)", g=G)

        def set_up_done(eng):
            eng.wait_ge(set_hi, N_SPLITS)
            eng.wait_ge(set_lo, N_SPLITS)
            eng.wait_ge(set_copy, N_COPIES)
            eng.wait_ge(set_small, N_SMALL)
            eng.wait_ge(pool_const, 13)

        dve_past, pool_past = sem("dve_past"), sem("pool_past")

        def settle(eng):
            eng.sem_inc(dve_past if eng is nc.vector else pool_past, 1)

        block = ctx.enter_context(nc.Block())

        @block.sync
        def _(sp):
            sp.dma_start(wqkv_raw[:].rearrange("p c h t d -> p c (h t d)"),
                         W_qkv.rearrange("(c p) n -> p c n", p=P)).then_inc(ld_wqkv, 16)
            sp.dma_start(w2_raw[:], W2.rearrange("(c p) n -> p c n", p=P)).then_inc(ld_w2, 16)
            sp.dma_start(w1_raw[:], W1.rearrange("(c p) n -> p c n", p=P)).then_inc(ld_w1, 16)
            sp.dma_start(wout_raw[:], W_out.rearrange("(c p) n -> p c n", p=P)).then_inc(ld_wout, 16)
            sp.dma_start(w3_raw[:], W3.rearrange("(c p) n -> p c n", p=P)).then_inc(ld_w3, 16)
            for k in range(3):
                sp.dma_start(wk_raw[:, k], Wk[k].rearrange("(c p) n -> p c n", p=P)).then_inc(ld_wk, 16)

            def load_group(i):
                sp.dma_start(adj_in[:], ag[:, bass.ds(i * G, G), :]).then_inc(a_in, 16)
                sp.dma_start(xin[:], xg[:, bass.ds(i * G, G), :]).then_inc(x_in, 16)
                sp.dma_start(mask_bc8[:], mask_rows[bass.ds(i, 1), :].rearrange("a n -> (a n)").partition_broadcast(P))\
                    .then_inc(m_in, 16)

            def used(i):
                sp.wait_ge(pe_adjT, i + 1)
                sp.wait_ge(pe_xT0, i + 1)
                sp.wait_ge(dve_deg, i + 1)
                sp.wait_ge(dve_DH, i * G + G)
                sp.wait_ge(pool_resid0, i + 1)
                sp.wait_ge(act_mbc, i + 1)
                sp.wait_ge(act_mrow, i * 2 + 2)

            def store_group(j):
                sp.wait_ge(pool_out, j * G + G)
                sp.dma_start(og[:, bass.ds(j * G, G), :], xout[:]).then_inc(y_out, 16)

            load_group(0)
            used(0)
            load_group(1)
            with sp.Fori(0, ITERS - 2) as j:
                used(j + 1)
                load_group(j + 2)
                store_group(j)
            store_group(ITERS - 2)
            store_group(ITERS - 1)
            sp.wait_ge(y_out, 16 * ITERS)

        @block.tensor
        def _(pe):
            def mm3(dst, lhs, rhs, start=True, stop=True):
                pe.matmul(dst, lhs[0], rhs[0], start=start, stop=False)
                pe.matmul(dst, lhs[0], rhs[1], start=False, stop=False)
                return pe.matmul(dst, lhs[1], rhs[0], start=False, stop=stop)

            def both(t, *index):
                return t[0][index], t[1][index]

            A = slice(None)

            def set_up():
                pe.wait_ge(ident_ok, 2)
                pe.wait_ge(set_flat, 1)
                for k in range(IC):
                    for c in range(DC):
                        last = pe.transpose(PS[:, bA + k // 2, (k % 2) * D + c * P:(k % 2) * D + (c + 1) * P],
                                            wv_flat[:, c, k * P:(k + 1) * P], ident[:])
                last.then_inc(set_pe, 1)
                pe.wait_ge(ld_w2, 16)
                for k in range(HC):
                    for c in range(DC):
                        last = pe.transpose(PS[:, bQ + k // 2, (k % 2) * D + c * P:(k % 2) * D + (c + 1) * P],
                                            w2_raw[:, c, k * P:(k + 1) * P], ident[:])
                last.then_inc(set_pe, 1)
                pe.wait_ge(ld_w1, 16)
                for c in range(DC):
                    for k in range(HC):
                        last = pe.transpose(PS[:, 2 + c, k * P:(k + 1) * P], w1_raw[:, k, c * P:(c + 1) * P], ident[:])
                last.then_inc(set_pe, 1)
                pe.wait_ge(ld_w3, 16)
                for c in range(DC):
                    for t in range(2):
                        for o in range(DC):
                            last = pe.transpose(PS[:, 4 + c, t * D + o * P:t * D + (o + 1) * P],
                                                w3_raw[:, o, t * D + c * P:t * D + (c + 1) * P], ident[:])
                last.then_inc(set_pe, 1)
                pe.wait_ge(set_copy, 2)
                pe.wait_ge(ld_wout, 16)
                for c in range(DC):
                    for k in range(IC):
                        last = pe.matmul(PS[:, bQ, c * D:(c + 1) * D], wvT[:, k, c * P:(c + 1) * P], wout_raw[:, k, :],
                                         start=(k == 0), stop=(k == IC - 1))
                last.then_inc(set_pe, 1)
                pe.wait_ge(set_beta, 1)
                for k in range(HC):
                    last = pe.matmul(PS[:, bR, 0:D], beta_bc[:, k, :], w2T_raw[:, k, :],
                                     start=(k == 0), stop=(k == HC - 1))
                last.then_inc(set_pe, 1)
                pe.wait_ge(set_maskf, 1)
                pe.transpose(PS[:, bA, 0:NG], maskf[:], ident[0:NG, 0:NG]).then_inc(set_pe, 1)

            def adjT_(i, j):
                pe.wait_ge(a_in, i * 16 + 16)
                if j is not None:
                    pe.wait_ge(dve_o2, j * G + G)
                for g in range(G):
                    last = pe.transpose(PS[:, bA, g * P:(g + 1) * P], adj_in[:, g, :], ident[:])
                last.then_inc(pe_adjT, 1)

            def xT0_(i, first):
                pe.wait_ge(x_in, i * 16 + 16)
                if not first:
                    pe.wait_ge(dve_y0, (i - 1) * G + 1)
                for c in range(DC):
                    for g in range(G):
                        last = pe.transpose(PS[:, bB, (c * G + g) * P:(c * G + g + 1) * P],
                                            xin[:, g, c * P:(c + 1) * P], ident[:])
                last.then_inc(pe_xT0, 1)

            def qk_(i, k):
                bank = (bC, bD)[k % 2]
                if k == 0:
                    pe.wait_ge(act_xT0, i + 1)
                    pe.wait_ge(dve_xT0, i + 1)
                    pe.wait_ge(dve_O, i * G)
                if k == 1:
                    pe.wait_ge(dve_y0, i * G)
                if k >= 2:
                    pe.wait_ge(act_qk, i * 4 + k - 1)
                for m in range(2 * k, 2 * k + 2):
                    t, h = m // 4, 2 * (m % 4)
                    for c in range(DC):
                        last = mm3(PS[:, bank, (m % 2) * G * P:(m % 2 + 1) * G * P],
                                   both(wqk, A, c, t, slice(h, h + 2)), both(xT0, A, c),
                                   start=(c == 0), stop=(c == DC - 1))
                last.then_inc(pe_qk, 1)

            def D_(i):
                pe.wait_ge(act_adjT, i + 1)
                pe.wait_ge(dve_ax, i * G)
                pe.wait_ge(dve_HT, i + 1)
                pe.wait_ge(dve_wone, i + 1)
                for g in range(G):
                    last = pe.matmul(PS[:, bA, 2 * g:2 * g + 2], HT[:, g, :], wone[:, g, :], start=True, stop=True)
                last.then_inc(pe_D, 1)

            def v_(i, g):
                bv_, bo_ = ((bB, bD), (bE, bC))[g]
                for c in range(DC):
                    last = mm3(PS[:, bv_, :], both(xT0, A, c, g), both(wvo, A, c, slice(0, INNER)),
                               start=(c == 0), stop=(c == DC - 1))
                last.then_inc(pe_v, 1)
                pe.wait_ge(act_qk, i * 4 + 4)
                for c in range(DC):
                    last = mm3(PS[:, bo_, 0:D], both(xT0, A, c, g), both(wvo, A, c, slice(INNER, INNER + D)),
                               start=(c == 0), stop=(c == DC - 1))
                last.then_inc(pe_vo, 1)

            def DHT_(i):
                pe.wait_ge(dve_DH, i * G + G)
                for g in range(G):
                    last = pe.transpose(PS[:, bA, g * P:(g + 1) * P], DHn[:, g, :], ident[:])
                last.then_inc(pe_DHT, 1)

            def AT_(i):
                pe.wait_ge(act_DHT, i + 1)
                pe.wait_ge(pool_BHT, i * G + G)
                for g in range(G):
                    last = pe.matmul(PS[:, bA, g * P:(g + 1) * P], BHT[:, g, :], DHT[:, g, :], start=True, stop=True)
                last.then_inc(pe_AT, 1)

            def S_(i, t):
                if t == 0:
                    pe.wait_ge(act_mrow, i * 2 + 2)
                pe.wait_ge(act_v, i * G + t + 1)
                pe.wait_ge(act_vo, i * G + t + 1)
                pe.wait_ge(dve_vo, i * G + t + 1)
                banks = ((bB, bD), (bC, bE))[t]
                for par in range(2):
                    p = par * DH
                    pe.matmul(PS[:, banks[par], :], mrow_l[p:p + DH, t, :],
                              mrow_r[p:p + DH, t:t + 1, :].to_broadcast([DH, HEADS // 2, P]),
                              start=True, stop=False, skip_group_check=True)
                for k in range(HEADS // 2):
                    for par in range(2):
                        p = par * DH
                        last = pe.matmul(PS[:, banks[par], k * P:(k + 1) * P], qk[p:p + DH, k, t, :],
                                         qk[p:p + DH, QKB // 2 + k, t, :], start=False,
                                         stop=(k == HEADS // 2 - 1), skip_group_check=True)
                last.then_inc(pe_S, 1)

            def PT_(i, t):
                pe.wait_ge(act_exp, i * G + t + 1)
                for h in range(HEADS):
                    last = pe.transpose(PS[:, (bB, bD)[h // 4], (h % 4) * P:(h % 4 + 1) * P], prob[:, t, h, :],
                                        ident[:])
                last.then_inc(pe_PT, 1)

            def PV_(i, t):
                if t == 0:
                    pe.wait_ge(dve_sub, i * G + G)
                    pe.wait_ge(act_v, i * G + G)
                pe.wait_ge(act_PT, i * G + t + 1)
                for slot in range(HEADS):
                    h = 2 * (slot % 4) + slot // 4
                    last = pe.matmul(PS[:, (bC, bE)[h // 4], (h % 4) * VX:(h % 4 + 1) * VX], probT[:, slot, :],
                                     vext[:, t, h, :], start=True, stop=True)
                last.then_inc(pe_PV, 1)

            def OT_(i, t, j):
                pe.wait_ge(dve_O, i * G + t + 1)
                if t == 0 and j is not None:
                    pe.wait_ge(act_Z2, j * G + 1)
                    pe.wait_ge(dve_Z2, j * G + 1)
                    pe.wait_ge(dve_sj, j * G + 1)
                for k in range(IC):
                    last = pe.transpose(PS[:, bQ, k * P:(k + 1) * P], osb[:, 2 * k:2 * k + 2, :], ident[:])
                last.then_inc(pe_OT, 1)

            def W_(i, t):
                pe.wait_ge(act_OT, i * G + t + 1)
                pe.wait_ge(dve_OT, i * G + t + 1)
                if t == 0:
                    pe.wait_ge(pool_gT, i + 1)
                dst = PS[:, (bB, bD)[t], 0:D]
                for k in range(IC):
                    mm3(dst, both(oT, A, t, k), both(wout, A, k), start=(k == 0), stop=False)
                mm3(dst, both(gT, A, t), both(vo, A, t), start=False, stop=True).then_inc(pe_y0, 1)

            def ax_(j, g):
                pe.wait_ge(dve_x1, j * G + g + 1)
                pe.wait_ge(act_AT, j + 1)
                for c in range(DC):
                    last = pe.matmul(PS[:, (bP, bA)[g], c * P:(c + 1) * P], x1[:, g, c * P:(c + 1) * P], AT[:, g, :],
                                     start=True, stop=True)
                last.then_inc(pe_ax, 1)

            def h_(j, g):
                pe.wait_ge(act_ax, j * G + g + 1)
                pe.wait_ge(dve_ax, j * G + g + 1)
                for c in range(DC):
                    last = mm3(PS[:, (bR, bP)[g], :], both(axT, A, g, c), both(w1t, A, c),
                               start=(c == 0), stop=(c == DC - 1))
                last.then_inc(pe_h, 1)

            def hT_(j, g):
                pe.wait_ge(dve_hn, j * G + g + 1)
                if g == 0:
                    pe.wait_ge(dve_o3, j * G)
                for k in range(HC):
                    last = pe.matmul(PS[:, (bQ, bR)[g], k * P:(k + 1) * P], hid[:, g, k * P:(k + 1) * P], AT[:, g, :],
                                     start=True, stop=True)
                last.then_inc(pe_hT, 1)

            def y1_(j, g):
                pe.wait_ge(act_hT, j * G + g + 1)
                pe.wait_ge(dve_hT, j * G + g + 1)
                for k in range(HC):
                    last = mm3(PS[:, (bP, bQ)[g], 0:D], both(hT, A, g, k), both(w2t, A, k),
                               start=(k == 0), stop=(k == HC - 1))
                last.then_inc(pe_y1, 1)

            def xT_(j, src, ready, done):
                pe.wait_ge(ready, j * G + G)
                for c in range(DC):
                    for g in range(G):
                        last = pe.transpose(PS[:, bR, (c * G + g) * P:(c * G + g + 1) * P],
                                            src[:, g, c * P:(c + 1) * P], ident[:])
                last.then_inc(done, 1)

            def Z_(j, g, i):
                if g == 0:
                    pe.wait_ge(act_xT2, j + 1)
                    pe.wait_ge(dve_xT2, j + 1)
                elif i is not None:
                    pe.wait_ge(act_AT, i + 1)
                for c in range(DC):
                    last = mm3(PS[:, (bP, bR)[g], :], both(xT2, A, c, g), both(wk01, A, c),
                               start=(c == 0), stop=(c == DC - 1))
                last.then_inc(pe_Z01, 1)
                for c in range(DC):
                    last = mm3(PS[:, (bQ, bA)[g], 0:D + 2], both(xT2, A, c, g), both(wk2, A, c),
                               start=(c == 0), stop=(c == DC - 1))
                last.then_inc(pe_Z2, 1)

            def si_(j):
                pe.wait_ge(act_Z01, j * G + 1)
                for c in range(DC):
                    last = mm3(PS[:, bP, 0:G * P], both(wi, A, c), both(xT2, A, c), start=(c == 0), stop=(c == DC - 1))
                last.then_inc(pe_si, 1)

            def T1_(j, g):
                pe.wait_ge(dve_al, j + 1)
                pe.wait_ge(act_Z2, j * G + G)
                pe.wait_ge(dve_Z2, j * G + G)
                pe.wait_ge(dve_sj, j * G + G)
                pe.wait_ge(act_Z01, j * G + G)
                mm3(PS[:, (bA, bR)[g], 0:D + 2], both(alT, A, g), both(z2, A, g)).then_inc(pe_T1, 1)

            def T2_(j, g):
                pe.wait_ge(act_Y, j * G + g + 1)
                pe.wait_ge(dve_Yl, j * G + g + 1)
                mm3(PS[:, (bP, bA)[g], 0:D], both(alT, A, g), both(yT, A, g)).then_inc(pe_T2, 1)

            def Z3_(j, g):
                pe.wait_ge(act_xT3, j + 1)
                pe.wait_ge(dve_xT3, j + 1)
                for c in range(DC):
                    last = mm3(PS[:, (bP, bA)[g], :], both(xT2, A, c, g), both(w3t, A, c),
                               start=(c == 0), stop=(c == DC - 1))
                last.then_inc(pe_Z3, 1)

            def T3_(j, g):
                pe.wait_ge(pool_aT, j + 1)
                pe.wait_ge(act_za, j * G + g + 1)
                pe.wait_ge(act_zb, j * G + g + 1)
                pe.wait_ge(dve_zb, j * G + g + 1)
                mm3(PS[:, (bQ, bE)[g], 0:D], both(aT, A, g), both(zb, A, g)).then_inc(pe_T3, 1)

            def group(i, j, n):
                F, B, L = i is not None, j is not None, n is not None
                if F:
                    qk_(i, 2)
                if B:
                    h_(j, 0)
                    h_(j, 1)
                if F:
                    qk_(i, 3)
                    D_(i)
                    v_(i, 0)
                if B:
                    hT_(j, 0)
                    hT_(j, 1)
                if F:
                    DHT_(i)
                    v_(i, 1)
                if B:
                    y1_(j, 0)
                    y1_(j, 1)
                if F:
                    AT_(i)
                    S_(i, 0)
                if B:
                    xT_(j, x2, dve_x2, pe_xT2)
                if F:
                    S_(i, 1)
                if B:
                    Z_(j, 0, i)
                if F:
                    PT_(i, 0)
                if B:
                    Z_(j, 1, i)
                    si_(j)
                if F:
                    PV_(i, 0)
                    PT_(i, 1)
                if B:
                    T1_(j, 0)
                    T1_(j, 1)
                if F:
                    OT_(i, 0, j)
                    PV_(i, 1)
                if B:
                    T2_(j, 0)
                    T2_(j, 1)
                if F:
                    OT_(i, 1, j)
                    W_(i, 0)
                    W_(i, 1)
                if L:
                    adjT_(n, j)
                    xT0_(n, not F)
                if B:
                    xT_(j, x3, dve_x3, pe_xT3)
                if L:
                    qk_(n, 0)
                if B:
                    Z3_(j, 0)
                    Z3_(j, 1)
                    T3_(j, 0)
                if F:
                    ax_(i, 0)
                if L:
                    qk_(n, 1)
                if B:
                    T3_(j, 1)
                if F:
                    ax_(i, 1)

            set_up()
            set_up_done(pe)
            group(None, None, 0)
            group(0, None, 1)
            group(1, 0, 2)
            with pe.Fori(1, ITERS - 2) as j:
                group(j + 1, j, j + 2)
            group(ITERS - 1, ITERS - 2, None)
            group(None, ITERS - 1, None)

        @block.scalar
        def _(act):
            act.dma_start(wv2_raw[:], Wv.rearrange("(c p) n -> p c n", p=P)).then_inc(ld_vec, 16)
            act.dma_start(aw_bc[:], aw.rearrange("(t n) a -> t (n a)", t=2).partition_broadcast(P)).then_inc(ld_vec, 16)
            act.dma_start(bv_bc[:], bv.partition_broadcast(P)).then_inc(ld_vec, 16)
            act.dma_start(ab_bc[:], ab.partition_broadcast(P)).then_inc(ld_vec, 16)
            act.dma_start(bk_raw[:], bk.partition_broadcast(P)).then_inc(ld_vec, 16)
            act.dma_start(bout_bc[:], b_out.partition_broadcast(P)).then_inc(ld_vec, 16)
            act.dma_start(b1_bc[:], b1.partition_broadcast(P)).then_inc(ld_vec, 16)
            act.dma_start(b2_bc[:], b2.partition_broadcast(P)).then_inc(ld_vec, 16)
            act.dma_start(gamma_c[:], gamma.rearrange("(k p) -> p k", p=P), allow_slow_non_contiguous=True).then_inc(ld_gb, 16)
            act.dma_start(beta_c[:], beta.rearrange("(k p) -> p k", p=P), allow_slow_non_contiguous=True).then_inc(ld_gb, 16)
            act.dma_start(mask8[:], nodemask).then_inc(ld_mask, 16)

            copy = ACT.Copy

            def set_up():
                def move(dst, src, n):
                    act.wait_ge(set_pe, n)
                    act.activation(dst, src, copy).then_inc(set_copy, 1)

                act.wait_ge(ld_gb, 32)
                move(wvT[:].rearrange("p (b k) d -> p b (k d)", b=2), PS[:, bA:bA + 2, :], SET_WVT)
                move(w2T_raw[:].rearrange("p (b k) d -> p b (k d)", b=2), PS[:, bQ:bQ + 2, :], SET_W2T)
                for n, (src, hi, lo, factor, (ready, value)) in enumerate(splits):
                    act.wait_ge(ready, value)
                    if factor is None:
                        act.activation(hi, src, copy).then_inc(set_hi, 1)
                    else:
                        act.activation(hi, src, copy, scale=factor).then_inc(set_hi, 1)
                move(bw_bc[:], PS[:, bR, 0:D], SET_BW)
                move(mask33[:], PS[:, bA, 0:NG], SET_MASK)

            def adjT_(i):
                act.wait_ge(pe_adjT, i + 1)
                act.wait_ge(act_adjTb, i)
                act.activation(adjT[:].rearrange("p g n -> p (g n)"), PS[:, bA, 0:G * P], copy).then_inc(act_adjT, 1)

            def xT0_(i):
                act.wait_ge(pe_xT0, i + 1)
                act.activation(xT0[0][:].rearrange("p c g n -> p (c g n)"), PS[:, bB, :], copy).then_inc(act_xT0, 1)

            def gate_(i):
                act.wait_ge(act_adjT, i + 1)
                act.wait_ge(pool_gT, i)
                act.activation(gate[:], adjT[:], ACT.Exp, scale=-1.0).then_inc(act_gate, 1)

            def mask_(i):
                act.wait_ge(m_in, i * 16 + 16)
                act.wait_ge(pe_S, i * G)
                act.wait_ge(pool_gate, i)
                for dst, a in ((mrow_l, 0), (mrow_r, 2)):
                    act.activation(dst[:].rearrange("p g n -> p (g n)"), mask_bc8[:], ACT.Identity,
                                   bias=mask_ab[:, a + 1:a + 2], scale=mask_ab[:, a:a + 1]).then_inc(act_mrow, 1)
                act.activation(mbc[:], mask_bc8[:], copy).then_inc(act_mbc, 1)

            def gT_(i):
                act.wait_ge(pool_gate, i + 1)
                act.activation(gT[0][:], gate[:], copy).then_inc(act_gT, 1)

            def carry(i):
                act.wait_ge(dve_al, i)
                act.wait_ge(pool_aT, i)
                act.activation(adjTb[:], adjT[:], copy).then_inc(act_adjTb, 1)

            def qk_(i, k):
                act.wait_ge(pe_qk, i * 4 + k + 1)
                act.activation(qk[:, 2 * k:2 * k + 2].rearrange("p m g n -> p (m g n)"),
                               PS[:, (bC, bD)[k % 2], :], copy).then_inc(act_qk, 1)

            def v_(i, g):
                bv_, bo_ = ((bB, bD), (bE, bC))[g]
                act.wait_ge(pe_v, i * G + g + 1)
                act.activation(vext[:, g, :, 0:DH], PS[:, bv_, :].rearrange("p (h d) -> p h d", h=HEADS), copy)\
                    .then_inc(act_v, 1)
                act.wait_ge(pe_vo, i * G + g + 1)
                act.wait_ge(dve_m33, i + 1)
                act.activation(vo[0][:, g, :], PS[:, bo_, 0:D], copy, scale=m33[:, g:g + 1]).then_inc(act_vo, 1)

            def DHT_(i):
                act.wait_ge(pe_DHT, i + 1)
                act.activation(DHT[:].rearrange("p g n -> p (g n)"), PS[:, bA, 0:G * P], copy).then_inc(act_DHT, 1)

            def AT_(i):
                act.wait_ge(pe_AT, i + 1)
                act.activation(AT[:].rearrange("p g n -> p (g n)"), PS[:, bA, 0:G * P], copy).then_inc(act_AT, 1)

            def exp_(i, t):
                act.wait_ge(dve_sub, i * G + t + 1)
                act.activation(prob[:, t], prob[:, t], ACT.Exp, scale=SCALE).then_inc(act_exp, 1)

            def PT_(i, t):
                act.wait_ge(pe_PT, i * G + t + 1)
                act.activation(probT[:].rearrange("p (b k) n -> p b (k n)", b=2), PS[:, bB:bD + 1, :], copy)\
                    .then_inc(act_PT, 1)

            def OT_(i, t):
                act.wait_ge(pe_OT, i * G + t + 1)
                act.activation(oT[0][:, t].rearrange("p k n -> p (k n)"), PS[:, bQ, :], copy).then_inc(act_OT, 1)

            def u_(j, g):
                act.wait_ge(dve_Dn, j + 1)
                act.activation(resid[:, g], bw_bc[:], copy, scale=rA[:, g:g + 1]).then_inc(act_u, 1)

            def x1_(j, g):
                act.wait_ge(dve_x1, j * G + g + 1)
                act.activation(x1_twice[:, g], x1[:, g], copy, scale=2.0).then_inc(act_x1, 1)

            def aT_(j):
                act.wait_ge(pe_T3, j * G)
                act.wait_ge(act_adjTb, j + 1)
                act.activation(aT[0][:], adjTb[:], copy).then_inc(act_aT, 1)

            def ax_(j, g):
                act.wait_ge(pe_ax, j * G + g + 1)
                act.activation(axT[0][:, g].rearrange("p c n -> p (c n)"), PS[:, (bP, bA)[g], 0:D], copy)\
                    .then_inc(act_ax, 1)

            def relu_(j, g):
                act.wait_ge(dve_hb, j * G + g + 1)
                act.activation(hid[:, g], hid[:, g], ACT.Relu).then_inc(act_relu, 1)

            def hT_(j, g):
                act.wait_ge(pe_hT, j * G + g + 1)
                act.activation(hT[0][:, g].rearrange("p k n -> p (k n)"), PS[:, (bQ, bR)[g], :], copy)\
                    .then_inc(act_hT, 1)

            def xT_(j, pe_done, done):
                act.wait_ge(pe_done, j + 1)
                act.activation(xT2[0][:].rearrange("p c g n -> p (c g n)"), PS[:, bR, :], copy).then_inc(done, 1)

            def Z_(j, g):
                act.wait_ge(pe_Z01, j * G + g + 1)
                act.activation(z01[:, g].rearrange("p t d -> p (t d)"), PS[:, (bP, bR)[g], :], copy)\
                    .then_inc(act_Z01, 1)
                act.wait_ge(pe_Z2, j * G + g + 1)
                act.wait_ge(dve_sj, j * G + g + 1)
                act.activation(z2[0][:, g, 0:D], PS[:, (bQ, bA)[g], 0:D], copy).then_inc(act_Z2, 1)

            def E_(j, g):
                act.wait_ge(pe_si, j + 1)
                act.wait_ge(dve_sj, j * G + g + 1)
                src = PS[:, bP, g * P:(g + 1) * P]
                act.activation(e1[:, g], src, ACT.Exp, bias=sj[:, g, 0:1]).then_inc(act_E, 1)
                act.activation(e2[:, g], src, ACT.Exp, bias=sj[:, g, 1:2], scale=SLOPE).then_inc(act_E, 1)

            def Y_(j, g):
                act.wait_ge(dve_Y, j * G + g + 1)
                act.activation(yT[0][:, g], yv[:, g], copy).then_inc(act_Y, 1)

            def Z3_(j, g):
                act.wait_ge(pe_Z3, j * G + g + 1)
                act.activation(zb[0][:, g], PS[:, (bP, bA)[g], D:2 * D], copy).then_inc(act_zb, 1)
                act.activation(za[:, g], PS[:, (bP, bA)[g], 0:D], copy).then_inc(act_za, 1)

            def group(i, j, n):
                F, B, L = i is not None, j is not None, n is not None
                if F:
                    gate_(i)
                if B:
                    u_(j, 0)
                    u_(j, 1)
                if F:
                    qk_(i, 2)
                if B:
                    relu_(j, 0)
                    relu_(j, 1)
                if F:
                    qk_(i, 3)
                    mask_(i)
                if B:
                    aT_(j)
                if F:
                    v_(i, 0)
                if B:
                    hT_(j, 0)
                if F:
                    DHT_(i)
                if B:
                    hT_(j, 1)
                if F:
                    v_(i, 1)
                    AT_(i)
                    gT_(i)
                if B:
                    xT_(j, pe_xT2, act_xT2)
                if F:
                    exp_(i, 0)
                if B:
                    Z_(j, 0)
                if F:
                    PT_(i, 0)
                    exp_(i, 1)
                if B:
                    Z_(j, 1)
                    E_(j, 0)
                    E_(j, 1)
                if F:
                    PT_(i, 1)
                    OT_(i, 0)
                    carry(i)
                if B:
                    Y_(j, 0)
                    Y_(j, 1)
                if F:
                    OT_(i, 1)
                if L:
                    adjT_(n)
                    xT0_(n)
                if B:
                    xT_(j, pe_xT3, act_xT3)
                if L:
                    qk_(n, 0)
                if B:
                    Z3_(j, 0)
                    Z3_(j, 1)
                if F:
                    x1_(i, 0)
                    ax_(i, 0)
                if L:
                    qk_(n, 1)
                if F:
                    ax_(i, 1)
                    x1_(i, 1)

            set_up()
            set_up_done(act)
            group(None, None, 0)
            group(0, None, 1)
            group(1, 0, 2)
            with act.Fori(1, ITERS - 2) as j:
                group(j + 1, j, j + 2)
            group(ITERS - 1, ITERS - 2, None)
            group(None, ITERS - 1, None)

        @block.vector
        def _(dve):
            def f32(t):
                return t.bitcast(F32)

            def set_up():
                dve.wait_ge(ld_wqkv, 16)
                dve.tensor_copy(wv_flat[:].rearrange("p c (h d) -> p c h d", h=HEADS), wqkv_raw[:, :, :, 2, :])\
                    .then_inc(set_flat, 1)
                dve.wait_ge(ld_mask, 16)
                dve.tensor_scalar(maskf[:], mask8[:], MIX, None, ALU.mult).then_inc(set_maskf, 1)
                dve.wait_ge(ld_gb, 32)
                dve.tensor_copy(beta_bc[:], beta_c[:].unsqueeze(2).to_broadcast([P, HC, P])).then_inc(set_beta, 1)
                dve.wait_ge(ld_vec, 16 * 8)
                for t in range(2):
                    dve.tensor_tensor(prod[:, t], wv2_raw[:], aw_bc[:, t:t + 1, :].to_broadcast([P, DC, D]), ALU.mult)\
                        .then_inc(set_prod, 1)
                dve.wait_ge(set_prod, 2)
                dve.tensor_reduce(wji[:], prod[:], AX_X, ALU.add).then_inc(set_wji, 1)
                dve.tensor_tensor(bprod[:], aw_bc[:], bv_bc[:].unsqueeze(1).to_broadcast([P, 2, D]), ALU.mult)\
                    .then_inc(set_prod, 1)
                dve.wait_ge(set_prod, 3)
                dve.tensor_reduce(bsum[:], bprod[:], AX_XY, ALU.add).then_inc(set_small, 1)
                dve.wait_ge(set_small, 1)
                dve.tensor_tensor(gate_c[:], bsum[:], ab_bc[:], ALU.add).then_inc(set_small, 1)
                dve.tensor_reduce(bk_bc[:], bk_raw[:].rearrange("p k d -> p d k"), AX_X, ALU.add).then_inc(set_small, 1)
                for n, (src, hi, lo, factor, (ready, value)) in enumerate(splits):
                    dve.wait_ge(set_hi, n + 1)
                    dve.wait_ge(ready, value)
                    if factor is None:
                        dve.tensor_tensor(lo, src, f32(hi), ALU.subtract).then_inc(set_lo, 1)
                    else:
                        dve.scalar_tensor_tensor(lo, src, factor, f32(hi), ALU.mult, ALU.subtract).then_inc(set_lo, 1)

            def low_part(lo, src, hi, hi_ready, value, done):
                dve.wait_ge(hi_ready, value)
                dve.tensor_tensor(lo, src, f32(hi), ALU.subtract).then_inc(done, 1)

            def stats(step, src, n, g, done):
                step.done(dve.bn_stats(st[:, n, g], src))
                settle(dve)
                dve.bn_aggr(mv[:, n, g], st[:, n, g]).then_inc(done, 1)

            def normalise(dst, src, n, g, scale_ready, value, done):
                dve.wait_ge(scale_ready, value)
                dve.tensor_scalar(dst, src, mv[:, n, g, 0:1], rs[:, n, g, 1:2], ALU.subtract, ALU.mult)\
                    .then_inc(done, 1)

            def front(i):
                step = Steps(dve, dve_fstep, i, DVE_FSTEPS)

                def xT0_():
                    low_part(xT0[1][:].rearrange("p c g n -> p (c g n)"), PS[:, bB, :],
                             xT0[0][:].rearrange("p c g n -> p (c g n)"), act_xT0, i + 1, dve_xT0)

                def incidence():
                    dve.wait_ge(act_adjT, i + 1)
                    dve.tensor_scalar(HT[:], adjT[:], 0.0, None, ALU.not_equal).then_inc(dve_HT, 1)
                    dve.tensor_copy(wone[:, :, 0:1], adjT[:, :, 0:1]).then_inc(dve_wone, 1)
                    dve.wait_ge(dve_HT, i + 1)
                    step.done(dve.tensor_reduce(cnt[:], HT[:], AX_X, ALU.add))
                    step.done(dve.tensor_scalar(cnt[:], cnt[:], 1.0, None, ALU.max))
                    dve.reciprocal(Be[:], cnt[:]).then_inc(dve_Be, 1)
                    dve.wait_ge(a_in, i * 16 + 16)
                    dve.tensor_reduce(degf[:], adj_in[:], AX_X, ALU.add).then_inc(dve_deg, 1)
                    dve.tensor_copy(m33[:], mask33[:, bass.ds(i * G, G)]).then_inc(dve_m33, 1)

                def Dn_():
                    dve.wait_ge(pe_D, i + 1)
                    step.done(dve.tensor_copy(dcol[:].rearrange("p g t -> p (g t)"), PS[:, bA, 0:2 * G]))
                    dve.tensor_scalar(dpos[:], dcol[:, :, 0], 0.0, None, ALU.is_gt).then_inc(dve_fstep, 1)
                    step.n += 1
                    step.done(dve.tensor_scalar(dsafe[:], dcol[:, :, 0], TINY, None, ALU.max))
                    step.done(dve.reciprocal(drec[:], dsafe[:]))
                    step.done(dve.tensor_tensor(Dn[:], drec[:], dpos[:], ALU.mult))
                    dve.wait_ge(act_u, i * G)
                    dve.tensor_tensor(rA[:], Dn[:], dcol[:, :, 1], ALU.mult).then_inc(dve_Dn, 1)
                    for g in range(G):
                        dve.tensor_scalar(DHn[:, g], adj_in[:, g], 0.0, Dn[:, g:g + 1], ALU.not_equal, ALU.mult)\
                            .then_inc(dve_DH, 1)

                def vo_(g):
                    dve.wait_ge(act_vo, i * G + g + 1)
                    dve.scalar_tensor_tensor(vo[1][:, g], PS[:, (bD, bC)[g], 0:D], m33[:, g:g + 1], f32(vo[0][:, g]),
                                             ALU.mult, ALU.subtract).then_inc(dve_vo, 1)

                def scores(t):
                    dve.wait_ge(pe_S, i * G + t + 1)
                    return (PS[:, bB:bD + 1, :], PS[:, bC:bE + 1, :])[t].rearrange("p b (h n) -> p b h n", n=P)

                def max_(t):
                    s = scores(t)
                    step.done(dve.tensor_reduce(m8[:, t].rearrange("p (b h) -> p b h", b=2), s, AX_X, ALU.max))

                def sub_(t):
                    s = scores(t)
                    m = m8[:, t].rearrange("p (b h) -> p b h", b=2).unsqueeze(3).to_broadcast([P, 2, HEADS // 2, P])
                    dve.tensor_tensor(prob[:, t].rearrange("p (b h) n -> p b h n", b=2), s, m, ALU.subtract)\
                        .then_inc(dve_sub, 1)

                def O_(t):
                    dve.wait_ge(pe_PV, i * G + t + 1)
                    o = PS[:, bC:bE + 1, 0:HEADS // 2 * VX].rearrange("p b (h d) -> p b h d", d=VX)
                    step.done(dve.reciprocal(rl[:, t], o[:, :, :, DH]))
                    dve.tensor_tensor(osb[:].rearrange("p (b h) d -> p b h d", b=2), o[:, :, :, 0:DH],
                                      rl[:, t].unsqueeze(3).to_broadcast([P, 2, HEADS // 2, DH]), ALU.mult)\
                        .then_inc(dve_O, 1)

                def OT_(t):
                    low_part(oT[1][:, t].rearrange("p k n -> p (k n)"), PS[:, bQ, :],
                             oT[0][:, t].rearrange("p k n -> p (k n)"), act_OT, i * G + t + 1, dve_OT)

                def y0_(t):
                    dve.wait_ge(pe_y0, i * G + t + 1)
                    dve.wait_ge(pool_resid0, i + 1)
                    dve.tensor_tensor(ys0[:, t], PS[:, (bB, bD)[t], 0:D], ys0[:, t], ALU.add).then_inc(dve_y0, 1)
                    dve.wait_ge(dve_y0, i * G + t + 1)
                    stats(step, ys0[:, t], NORM0, t, dve_mv0)

                def x1_(t):
                    normalise(x1[:, t], ys0[:, t], NORM0, t, pool_rs0, i * G + t + 1, dve_x1)

                return step, xT0_, incidence, Dn_, vo_, max_, sub_, O_, OT_, y0_, x1_

            def back(j):
                step = Steps(dve, dve_bstep, j, DVE_BSTEPS)

                def ax_(g):
                    low_part(axT[1][:, g].rearrange("p c n -> p (c n)"), PS[:, (bP, bA)[g], 0:D],
                             axT[0][:, g].rearrange("p c n -> p (c n)"), act_ax, j * G + g + 1, dve_ax)

                def hb_(g):
                    dve.wait_ge(pe_h, j * G + g + 1)
                    dve.tensor_tensor(hid[:, g], PS[:, (bR, bP)[g], :], b1_bc[:], ALU.add).then_inc(dve_hb, 1)

                def hstats_(g):
                    dve.wait_ge(act_relu, j * G + g + 1)
                    stats(step, hid[:, g], NORMH, g, dve_mvh)

                def hn_(g):
                    normalise(hid[:, g], hid[:, g], NORMH, g, pool_rsh, j * G + g + 1, dve_hn)

                def hT_(g):
                    low_part(hT[1][:, g].rearrange("p k n -> p (k n)"), PS[:, (bQ, bR)[g], :],
                             hT[0][:, g].rearrange("p k n -> p (k n)"), act_hT, j * G + g + 1, dve_hT)

                def y1_(g):
                    dve.wait_ge(pe_y1, j * G + g + 1)
                    dve.wait_ge(pool_resid1, j * G + g + 1)
                    dve.wait_ge(pool_out, j * G)
                    step.done(dve.tensor_tensor(ysb[:, g], PS[:, (bP, bQ)[g], 0:D], resid[:, g], ALU.add))
                    stats(step, ysb[:, g], NORM1, g, dve_mv1)

                def x2_(g):
                    normalise(x2[:, g], ysb[:, g], NORM1, g, pool_rs1, j * G + g + 1, dve_x2)

                def xT_(hi_ready, done):
                    low_part(xT2[1][:].rearrange("p c g n -> p (c g n)"), PS[:, bR, :],
                             xT2[0][:].rearrange("p c g n -> p (c g n)"), hi_ready, j + 1, done)

                def Z_(g):
                    s = PS[:, (bQ, bA)[g], D:D + 1]
                    dve.wait_ge(pe_Z2, j * G + g + 1)
                    step.done(dve.tensor_tensor(sj[:, g, 0:1], s, gate_c[:], ALU.add))
                    dve.tensor_scalar(sj[:, g, 1:2], sj[:, g, 0:1], SLOPE, None, ALU.mult).then_inc(dve_sj, 1)
                    low_part(z2[1][:, g, 0:D], PS[:, (bQ, bA)[g], 0:D], z2[0][:, g, 0:D], act_Z2, j * G + g + 1,
                             dve_Z2)

                def al_():
                    dve.wait_ge(act_E, j * 2 * G + 2 * G)
                    step.done(dve.tensor_tensor(al[:], e1[:], e2[:], ALU.max))
                    dve.wait_ge(act_adjTb, j + 1)
                    step.done(dve.tensor_tensor(al[:], al[:], adjTb[:], ALU.mult))
                    step.done(dve.tensor_copy(alT[0][:], al[:]))
                    dve.tensor_tensor(alT[1][:], al[:], f32(alT[0][:]), ALU.subtract).then_inc(dve_al, 1)

                def Y_(g):
                    dve.wait_ge(pe_T1, j * G + g + 1)
                    dve.wait_ge(act_Z01, j * G + g + 1)
                    b = (bA, bR)[g]
                    step.done(dve.tensor_scalar(den[:, g:g + 1], PS[:, b, D:D + 1], DEN_EPS, None, ALU.add))
                    step.done(dve.reciprocal(rden[:, g:g + 1], den[:, g:g + 1]))
                    dve.scalar_tensor_tensor(yv[:, g], PS[:, b, 0:D], rden[:, g:g + 1], z01[:, g, 1], ALU.mult,
                                             ALU.add)\
                        .then_inc(dve_Y, 1)

                def Yl_(g):
                    low_part(yT[1][:, g], yv[:, g], yT[0][:, g], act_Y, j * G + g + 1, dve_Yl)

                def o2_(g):
                    dve.wait_ge(pe_T2, j * G + g + 1)
                    dve.wait_ge(pool_z0, j * G + g + 1)
                    dve.scalar_tensor_tensor(ysb[:, g], PS[:, (bP, bA)[g], 0:D], rden[:, g:g + 1], z01[:, g, 0],
                                             ALU.mult, ALU.add).then_inc(dve_o2, 1)
                    dve.wait_ge(dve_o2, j * G + g + 1)
                    step.done(dve.scalar_tensor_tensor(ysb[:, g], ysb[:, g], 0.0, x2[:, g], ALU.max, ALU.add))
                    stats(step, ysb[:, g], NORM2, g, dve_mv2)

                def x3_(g):
                    normalise(x3[:, g], ysb[:, g], NORM2, g, pool_rs2, j * G + g + 1, dve_x3)

                def deg_():
                    step.done(dve.tensor_scalar(degb[:], degf[:], DEG_EPS, None, ALU.max))
                    step.done(dve.reciprocal(degb[:], degb[:]))

                def zb_(g):
                    dve.wait_ge(act_za, j * G + g + 1)
                    low_part(zb[1][:, g], PS[:, (bP, bA)[g], D:2 * D], zb[0][:, g], act_zb, j * G + g + 1, dve_zb)

                def o3_(g):
                    dve.wait_ge(pe_T3, j * G + g + 1)
                    dve.scalar_tensor_tensor(ysb[:, g], PS[:, (bQ, bE)[g], 0:D], degb[:, g:g + 1], za[:, g],
                                             ALU.mult, ALU.add).then_inc(dve_o3, 1)
                    dve.wait_ge(dve_o3, j * G + g + 1)
                    step.done(dve.scalar_tensor_tensor(ysb[:, g], ysb[:, g], 0.0, x3[:, g], ALU.max, ALU.add))
                    stats(step, ysb[:, g], NORM3, g, dve_mv3)

                return (step, ax_, hb_, hstats_, hn_, hT_, y1_, x2_, xT_, Z_, al_, Y_, Yl_, o2_, x3_, deg_, zb_,
                        o3_)

            def group(i, j, n):
                F, B, L = i is not None, j is not None, n is not None
                if F:
                    fstep, _, incidence, Dn_, vo_, max_, sub_, O_, fOT_, y0_, x1_ = front(i)
                if B:
                    (bstep, ax_, hb_, hstats_, hn_, hT_, y1_, x2_, xT_, Z_, al_, Y_, Yl_, o2_, x3_, deg_, zb_,
                     o3_) = back(j)
                if B:
                    deg_()
                if F:
                    incidence()
                if B:
                    hb_(0)
                    hb_(1)
                    hstats_(0)
                    hstats_(1)
                    hn_(0)
                    hn_(1)
                if F:
                    Dn_()
                    vo_(0)
                if B:
                    hT_(0)
                    hT_(1)
                if F:
                    vo_(1)
                if B:
                    y1_(0)
                    y1_(1)
                    x2_(0)
                    x2_(1)
                if F:
                    max_(0)
                if B:
                    xT_(act_xT2, dve_xT2)
                if F:
                    sub_(0)
                    max_(1)
                    sub_(1)
                if B:
                    Z_(0)
                    Z_(1)
                if B:
                    al_()
                if F:
                    O_(0)
                if B:
                    Y_(0)
                    Y_(1)
                if F:
                    fOT_(0)
                if B:
                    Yl_(0)
                    Yl_(1)
                if F:
                    O_(1)
                if B:
                    o2_(0)
                if F:
                    fOT_(1)
                if B:
                    o2_(1)
                    x3_(0)
                if F:
                    y0_(0)
                if B:
                    x3_(1)
                if L:
                    front(n)[1]()
                if B:
                    xT_(act_xT3, dve_xT3)
                if F:
                    y0_(1)
                    x1_(0)
                    x1_(1)
                if B:
                    zb_(0)
                    zb_(1)
                    o3_(0)
                if F:
                    back(i)[1](0)
                    back(i)[1](1)
                if B:
                    o3_(1)
                if F:
                    assert fstep.n == DVE_FSTEPS, fstep.n
                if B:
                    assert bstep.n == DVE_BSTEPS, bstep.n

            set_up()
            set_up_done(dve)
            group(None, None, 0)
            group(0, None, 1)
            group(1, 0, 2)
            with dve.Fori(1, ITERS - 2) as j:
                group(j + 1, j, j + 2)
            group(ITERS - 1, ITERS - 2, None)
            group(None, ITERS - 1, None)

        @block.gpsimd
        def _(pool):
            def set_up():
                pool.memset(ident[:], 0.0).then_inc(ident_ok, 1)
                pool.wait_ge(ident_ok, 1)
                pool.affine_select(out=ident[:], in_=ident[:], compare_op=ALU.not_equal, fill=1.0, base=0,
                                   pattern=[[-1, P]], channel_multiplier=1).then_inc(ident_ok, 1)
                pool.memset(vext[:, :, :, DH:VX], 1.0 / MIX).then_inc(pool_const, 1)
                pool.memset(z2[0][:, :, D:D + 2].bitcast(F32), 1.0).then_inc(pool_const, 1)
                pool.memset(z2[1][:, :, D:D + 2].bitcast(F32), 0.0).then_inc(pool_const, 1)
                pool.memset(wone[:, :, 1:2], 1.0).then_inc(pool_const, 1)
                pool.memset(wk2[0][:, :, D + 1:D + 2].bitcast(F32), 0.0).then_inc(pool_const, 1)
                pool.memset(wk2[1][:, :, D + 1:D + 2].bitcast(F32), 0.0).then_inc(pool_const, 1)
                pool.memset(mhalf[:], -0.5).then_inc(pool_const, 1)
                pool.memset(eps_c[:], LN_EPS).then_inc(pool_const, 1)
                pool.memset(mask_ab[:], 0.0).then_inc(pool_const, 1)
                rows = 2
                for base in (0, DH):
                    for col, second in enumerate((1.0, 0.0, BIG, -BIG)):
                        pool.wait_ge(pool_const, 9)
                        last = pool.memset(mask_ab[base:base + rows, col:col + 1], second)
                    last.then_inc(pool_const, 1)
                pool.wait_ge(pool_const, 11)
                for base in (0, DH):
                    for col, first in enumerate((BIG, -BIG, 0.0, 1.0)):
                        last = pool.memset(mask_ab[base:base + 1, col:col + 1], first)
                    last.then_inc(pool_const, 1)

            def scale(step, n, g, ready, value):
                pool.wait_ge(ready, value)
                step.done(pool.tensor_tensor(rs[:, n, g, 0:1], mv[:, n, g, 1:2], eps_c[:], ALU.add))
                return pool.tensor_tensor(rs[:, n, g, 1:2], rs[:, n, g, 0:1], mhalf[:], ALU.pow)

            def front(i):
                step = Steps(pool, pool_fstep, i, POOL_FSTEPS)

                def operator():
                    pool.wait_ge(dve_Be, i + 1)
                    settle(pool)
                    for g in range(G):
                        pool.tensor_scalar(BHT[:, g], HT[:, g], Be[:, g:g + 1], None, ALU.mult)\
                            .then_inc(pool_BHT, 1)

                def resid_():
                    pool.wait_ge(x_in, i * 16 + 16)
                    pool.tensor_tensor(ys0[:], xin[:], bout_bc[:].unsqueeze(1).to_broadcast([P, G, D]), ALU.add)\
                        .then_inc(pool_resid0, 1)

                def gate_():
                    pool.wait_ge(act_gate, i + 1)
                    pool.wait_ge(act_mbc, i + 1)
                    flat = gate[:].rearrange("p g n -> p (g n)")
                    step.done(pool.tensor_tensor(gate[:], gate[:], adjT[:], ALU.add))
                    pool.tensor_tensor(flat, flat, mbc[:], ALU.mult).then_inc(pool_gate, 1)

                def gT_():
                    pool.wait_ge(act_gT, i + 1)
                    pool.tensor_tensor(gT[1][:], gate[:], gT[0][:].bitcast(F32), ALU.subtract).then_inc(pool_gT, 1)

                def rs0_(t):
                    scale(step, NORM0, t, dve_mv0, i * G + t + 1).then_inc(pool_rs0, 1)

                return step, operator, resid_, gate_, gT_, rs0_

            def back(j):
                step = Steps(pool, pool_bstep, j, POOL_BSTEPS)

                def resid_(g):
                    pool.wait_ge(act_u, j * G + g + 1)
                    step.done(pool.tensor_tensor(resid[:, g], resid[:, g], b2_bc[:], ALU.add))
                    pool.wait_ge(act_x1, j * G + g + 1)
                    pool.tensor_tensor(resid[:, g], resid[:, g], x1_twice[:, g], ALU.add).then_inc(pool_resid1, 1)

                def rsh_(g):
                    scale(step, NORMH, g, dve_mvh, j * G + g + 1).then_inc(pool_rsh, 1)

                def rs1_(g):
                    scale(step, NORM1, g, dve_mv1, j * G + g + 1).then_inc(pool_rs1, 1)

                def rs2_(g):
                    scale(step, NORM2, g, dve_mv2, j * G + g + 1).then_inc(pool_rs2, 1)

                def out_(g):
                    step.done(scale(step, NORM3, g, dve_mv3, j * G + g + 1))
                    if g == 0:
                        pool.wait_ge(y_out, j * 16)
                    settle(pool)
                    pool.tensor_scalar(xout[:, g], ysb[:, g], mv[:, NORM3, g, 0:1], rs[:, NORM3, g, 1:2],
                                       ALU.subtract, ALU.mult).then_inc(pool_out, 1)

                def aT_():
                    pool.wait_ge(act_aT, j + 1)
                    pool.tensor_tensor(aT[1][:], adjTb[:], aT[0][:].bitcast(F32), ALU.subtract).then_inc(pool_aT, 1)

                def z0_(g):
                    pool.wait_ge(act_Z01, j * G + g + 1)
                    pool.tensor_tensor(z01[:, g, 0], z01[:, g, 0], bk_bc[:], ALU.add).then_inc(pool_z0, 1)

                return step, resid_, rsh_, rs1_, rs2_, out_, aT_, z0_

            def group(i, j, n):
                F, B = i is not None, j is not None
                if F:
                    fstep, operator, fresid_, gate_, gT_, rs0_ = front(i)
                if B:
                    bstep, resid_, rsh_, rs1_, rs2_, out_, aT_, z0_ = back(j)
                if B:
                    rsh_(0)
                    rsh_(1)
                if F:
                    operator()
                if B:
                    resid_(0)
                    resid_(1)
                if F:
                    gate_()
                if B:
                    rs1_(0)
                    rs1_(1)
                if F:
                    gT_()
                    fresid_()
                if B:
                    aT_()
                    z0_(0)
                    z0_(1)
                    rs2_(0)
                    rs2_(1)
                if F:
                    rs0_(0)
                    rs0_(1)
                if B:
                    out_(0)
                    out_(1)
                if F:
                    assert fstep.n == POOL_FSTEPS, fstep.n
                if B:
                    assert bstep.n == POOL_BSTEPS, bstep.n

            set_up()
            set_up_done(pool)
            group(None, None, 0)
            group(0, None, 1)
            group(1, 0, 2)
            with pool.Fori(1, ITERS - 2) as j:
                group(j + 1, j, j + 2)
            group(ITERS - 1, ITERS - 2, None)
            group(None, ITERS - 1, None)


_INS = ['x', 'adj', 'nodemask', 'L0_gnn_W_qkv', 'L0_gnn_W_out', 'L0_gnn_b_out', 'L1_gnn_W1', 'L1_gnn_b1',
        'L1_gnn_gamma', 'L1_gnn_beta', 'L1_gnn_W2', 'L1_gnn_b2', 'L2_gnn_Wv', 'L2_gnn_bv', 'L2_gnn_aw', 'L2_gnn_ab',
        'L2_gnn_Wk', 'L2_gnn_bk', 'L3_gnn_W']


def kernel(**inputs):
    import numpy as _np
    import concourse.bacc as _bacc
    from concourse import mybir as _mybir
    from concourse.bass_utils import run_bass_kernel_spmd as _run

    nc = _bacc.Bacc("TRN2", target_bir_lowering=False, num_devices=1)
    arrays, args = {}, []
    for name in _INS:
        a = _np.ascontiguousarray(inputs[name])
        if a.dtype == _np.bool_:
            a = a.view(_np.uint8)
        arrays[f"in_{name}_dram"] = a
        args.append(nc.dram_tensor(f"in_{name}_dram", a.shape, _mybir.dt.from_np(a.dtype), kind="ExternalInput").ap())
    shape = tuple(inputs["x"].shape)
    args.append(nc.dram_tensor("out_0_dram", shape, _mybir.dt.float32, kind="ExternalOutput").ap())
    gnn_stack_kernel(nc, *args)
    r = _run(nc, [arrays], core_ids=[0])
    return r.results[0]["out_0_dram"]
```

```python
from contextlib import ExitStack

import concourse.bass as bass
from concourse import mybir

F32 = mybir.dt.float32
F32R = mybir.dt.float32r
BF16 = mybir.dt.bfloat16
U8 = mybir.dt.uint8
ALU = mybir.AluOpType
ACT = mybir.ActivationFunctionType
AX_X = mybir.AxisListType.X
AX_XY = mybir.AxisListType.XY

P = 128
HEADS = 8
DH = 64
MIX = 0.33
LN_EPS = 1e-5
DEG_EPS = 1e-6
DEN_EPS = 1e-12
TINY = 1.2e-38
SLOPE = 0.2
BIG = float(2.0 ** 100)


def gnn_stack_kernel(nc, x, adj, nodemask, W_qkv, W_out, b_out, W1, b1, gamma, beta, W2, b2,
                     Wv, bv, aw, ab, Wk, bk, W3, out):
    NG, N, D = x.shape
    G = 2
    ITERS = NG // G
    DC = D // P
    INNER = HEADS * DH
    IC = INNER // P
    DHID = W1.shape[0]
    HC = DHID // P
    QKB = 2 * INNER // P
    SCALE = float(DH) ** -0.5
    VX = DH + 1
    assert N == P and D == 256 and DHID == 512 and INNER == 512 and QKB == 8

    ctx = ExitStack()
    with ctx:
        free = nc.sbuf_bytes_remaining - 64
        arena = ctx.enter_context(nc.sbuf_tensor("arena", [P, free // 4], F32))
        arena_base = (nc.sbuf_base - free + 31) // 32 * 32
        place = [arena_base]

        def at(name, shape, dt=F32, keep=True):
            size = 1
            for n in shape[1:]:
                size *= n
            size *= {F32: 4, F32R: 4, BF16: 2, U8: 1}[dt]
            t = nc.alloc_sbuf_tensor_at(name, shape, dt, offset=place[0])
            place[0] += (size + 31) // 32 * 32
            assert place[0] <= arena_base + free - 32, (name, place[0])
            return t

        def pair(name, shape):
            return at(name + "_hi", shape, F32R), at(name + "_lo", shape, F32R)

        ident = at("ident", [P, P])
        wqk = pair("wqk", [P, DC, 2, HEADS, DH])
        wvo = pair("wvo", [P, DC, INNER + D])
        wout = pair("wout", [P, IC, D])
        w1t = pair("w1t", [P, DC, DHID])
        w2t = pair("w2t", [P, HC, D])
        wk01 = pair("wk01", [P, DC, 2, D])
        wk2 = pair("wk2", [P, DC, D + 2])
        w3t = pair("w3t", [P, DC, 2, D])
        bout_bc = at("bout_bc", [P, D])
        b1_bc = at("b1_bc", [P, DHID])
        b2_bc = at("b2_bc", [P, D])
        bk_bc = at("bk_bc", [P, D])
        bw_bc = at("bw_bc", [P, D])
        mask33 = at("mask33", [P, NG])
        gate_c = at("gate_c", [P, 2])
        mask_ab = at("mask_ab", [P, 4])
        mhalf = at("mhalf", [P, 1])
        eps_c = at("eps_c", [P, 1])

        vext = at("vext", [P, G, HEADS, VX])
        z2 = pair("z2", [P, G, D + 2])
        wone = at("wone", [P, G, 2])
        mrow_l = at("mrow_l", [P, G, P], BF16)
        mrow_r = at("mrow_r", [P, G, P], BF16)
        xin = at("xin", [P, G, D])
        adj_in = at("adj_in", [P, G, P])
        mask_bc8 = at("mask_bc8", [P, G * P], U8)
        work_base = place[0]

        adjTb = at("adjTb", [P, G, P])
        gate = at("gate", [P, G, P])
        gT = pair("gT", [P, G, P])
        aT = pair("aT", [P, G, P])
        HT = at("HT", [P, G, P])
        BHT = at("BHT", [P, G, P])
        DHn = at("DHn", [P, G, P])
        DHT = at("DHT", [P, G, P])
        AT = at("AT", [P, G, P])
        mbc = at("mbc", [P, G * P])
        xT2 = pair("xT2", [P, DC, G, P])
        vo = pair("vo", [P, G, D])
        prob = at("prob", [P, 2, HEADS, P])
        probT = at("probT", [P, HEADS, P])
        osb = at("osb", [P, HEADS, DH])
        oT = pair("oT", [P, G, IC, P])
        ys0 = at("ys0", [P, G, D])
        ysb = at("ysb", [P, G, D])
        x1 = at("x1", [P, G, D])
        x2 = at("x2", [P, G, D])
        x3 = at("x3", [P, G, D])
        xout = at("xout", [P, G, D])
        resid = at("resid", [P, G, D])
        x1_twice = at("x1_twice", [P, G, D])
        axT = pair("axT", [P, G, DC, P])
        hid = at("hid", [P, G, DHID])
        hT = pair("hT", [P, G, HC, P])
        z01 = at("z01", [P, G, 2, D])
        e1 = at("e1", [P, G, P])
        e2 = at("e2", [P, G, P])
        al = at("al", [P, G, P])
        alT = pair("alT", [P, G, P])
        yv = at("yv", [P, G, D])
        yT = pair("yT", [P, G, D])
        za = at("za", [P, G, D])
        zb = pair("zb", [P, G, D])
        m33 = at("m33", [P, G])
        cnt = at("cnt", [P, G])
        Be = at("Be", [P, G])
        degf = at("degf", [P, G])
        degb = at("degb", [P, G])
        dcol = at("dcol", [P, G, 2])
        dpos = at("dpos", [P, G])
        dsafe = at("dsafe", [P, G])
        drec = at("drec", [P, G])
        Dn = at("Dn", [P, G])
        rA = at("rA", [P, G])
        m8 = at("m8", [P, G, HEADS])
        rl = at("rl", [P, G, 2, HEADS // 2])
        sji = at("sji", [P, G, 3])
        den = at("den", [P, G])
        rden = at("rden", [P, G])
        NORM0, NORMH, NORM1, NORM2, NORM3 = range(5)
        st = at("st", [P, 5, G, 6])
        mv = at("mv", [P, 5, G, 2])
        rs = at("rs", [P, 5, G, 2])
        early_base = place[0]
        adjT = at("adjT", [P, G, P])
        xT0 = pair("xT0", [P, DC, G, P])
        qk = at("qk", [P, QKB, G, P])

        place[0] = work_base
        wqkv_raw = at("wqkv_raw", [P, DC, HEADS, 3, DH])
        wv_flat = at("wv_flat", [P, DC, INNER])
        wout_raw = at("wout_raw", [P, IC, D])
        w1_raw = at("w1_raw", [P, HC, D])
        w2_raw = at("w2_raw", [P, DC, DHID])
        w3_raw = at("w3_raw", [P, DC, 2 * D])
        wk_raw = at("wk_raw", [P, 3, DC, D])
        wv2_raw = at("wv2_raw", [P, DC, D])
        aw_bc = at("aw_bc", [P, 2, D])
        bv_bc = at("bv_bc", [P, D])
        ab_bc = at("ab_bc", [P, 1])
        bk_raw = at("bk_raw", [P, 3, D])
        gamma_c = at("gamma_c", [P, HC])
        beta_c = at("beta_c", [P, HC])
        beta_bc = at("beta_bc", [P, HC, P])
        wvT = at("wvT", [P, IC, D])
        w2T_raw = at("w2T_raw", [P, HC, D])
        prod = at("prod", [P, 2, DC, D])
        wji = at("wji", [P, 2, DC])
        bprod = at("bprod", [P, 2, D])
        bsum = at("bsum", [P, 1])
        mask8 = at("mask8", [NG, P], U8)
        maskf = at("maskf", [NG, P])
        assert place[0] <= early_base

        PS = ctx.enter_context(nc.psum_tensor("PS", [P, 8, 512], F32))
        bA, bB, bD, bC, bE, bP, bQ, bR = range(8)

        def sem(name):
            return ctx.enter_context(nc.semaphore(name))

        ld_wqkv, ld_wout, ld_w1, ld_w2, ld_w3, ld_wk, ld_wv, ld_gate, ld_vec, ld_mask, ld_gb = (
            sem(n) for n in ("ld_wqkv", "ld_wout", "ld_w1", "ld_w2", "ld_w3", "ld_wk", "ld_wv", "ld_gate",
                             "ld_vec", "ld_mask", "ld_gb"))
        ident_ok = sem("ident_ok")
        pool_const = sem("pool_const")
        set_flat = sem("set_flat")
        set_maskf = sem("set_maskf")
        set_beta = sem("set_beta")
        set_prod = sem("set_prod")
        set_wji = sem("set_wji")
        set_pe = sem("set_pe")
        set_copy = sem("set_copy")
        set_hi = sem("set_hi")
        set_lo = sem("set_lo")
        set_pool_lo = sem("set_pool_lo")
        set_small = sem("set_small")
        x_in, a_in, m_in, y_out = (sem(n) for n in ("x_in", "a_in", "m_in", "y_out"))
        (pe_adjT, pe_xT0, pe_qk, pe_D, pe_v, pe_vo, pe_DHT, pe_AT, pe_S, pe_PT, pe_PV, pe_OT, pe_y0) = (
            sem("pe_" + n) for n in ("adjT", "xT0", "qk", "D", "v", "vo", "DHT", "AT", "S", "PT", "PV", "OT", "y0"))
        (act_adjT, act_xT0, act_gate, act_qk, act_v, act_vo, act_DHT, act_AT, act_exp, act_PT, act_OT,
         act_gT, act_adjTb, act_mrow, act_mbc) = (
            sem("act_" + n) for n in ("adjT", "xT0", "gate", "qk", "v", "vo", "DHT", "AT", "exp", "PT", "OT",
                                        "gT", "adjTb", "mrow", "mbc"))
        (dve_xT0, dve_HT, dve_wone, dve_m33, dve_Be, dve_Dn, dve_DH, dve_vo, dve_sub, dve_O, dve_OT, dve_y0, dve_mv0,
         dve_deg, dve_x1) = (sem("dve_" + n) for n in ("xT0", "HT", "wone", "m33", "Be", "Dn", "DH", "vo", "sub", "O", "OT", "y0",
                                                "mv0", "deg", "x1"))
        (pool_resid0, pool_BHT, pool_gate, pool_gT, pool_rs0) = (
            sem("pool_" + n) for n in ("resid0", "BHT", "gate", "gT", "rs0"))
        (pe_ax, pe_h, pe_hT, pe_y1, pe_xT2, pe_Z01, pe_Z2, pe_si, pe_T1, pe_T2, pe_xT3, pe_Z3, pe_T3) = (
            sem("pe_" + n) for n in ("ax", "h", "hT", "y1", "xT2", "Z01", "Z2", "si", "T1", "T2", "xT3", "Z3", "T3"))
        (act_ax, act_relu, act_hT, act_xT2, act_Z01, act_Z2, act_E, act_Y, act_xT3, act_za, act_zb,
         act_u, act_aT, act_x1, act_al) = (
            sem("act_" + n) for n in ("ax", "relu", "hT", "xT2", "Z01", "Z2", "E", "Y", "xT3", "za", "zb", "u",
                                        "aT", "x1", "al"))
        (dve_ax, dve_hb, dve_mvh, dve_hT, dve_mv1, dve_xT2, dve_Z2, dve_sj, dve_al, dve_Y, dve_Yl, dve_o2,
         dve_mv2, dve_xT3, dve_zb, dve_o3, dve_mv3, dve_hn, dve_x2, dve_x3,
         dve_alw) = (
            sem("dve_" + n) for n in ("ax", "hb", "mvh", "hT", "mv1", "xT2", "Z2", "sj", "al", "Y", "Yl", "o2",
                                      "mv2", "xT3", "zb", "o3", "mv3", "hn", "x2", "x3",
                                      "alw"))
        (pool_resid1, pool_rsh, pool_rs1, pool_rs2, pool_aT, pool_z0, pool_Yl, pool_out) = (
            sem("pool_" + n) for n in ("resid1", "rsh", "rs1", "rs2", "aT", "z0", "Yl", "out"))
        dve_fstep, dve_bstep, pool_fstep, pool_bstep = (
            sem(n) for n in ("dve_fstep", "dve_bstep", "pool_fstep", "pool_bstep"))

        DVE_FSTEPS, DVE_BSTEPS, POOL_FSTEPS, POOL_BSTEPS = 7 + 3 * G, 4 + 9 * G, 1 + G, 1 + 5 * G

        class Steps:

            def __init__(self, eng, counter, i, per_group):
                self.eng, self.counter, self.i, self.per_group, self.n = eng, counter, i, per_group, 0

            def count(self, ins):
                self.n += 1
                ins.then_inc(self.counter, 1)
                return self.n

            def wait(self, n):
                self.eng.wait_ge(self.counter, self.i * self.per_group + n)

            def done(self, ins):
                self.wait(self.count(ins))

        raw = wqkv_raw
        splits = []
        for c in range(DC):
            splits.append((raw[:, c, :, 0:2, :].rearrange("p h t d -> p t h d"), wqk[0][:, c], wqk[1][:, c], None,
                           (ld_wqkv, 16)))
        for c in range(DC):
            splits.append((raw[:, c, :, 2, :], wvo[0][:, c, 0:INNER].rearrange("p (h d) -> p h d", h=HEADS),
                           wvo[1][:, c, 0:INNER].rearrange("p (h d) -> p h d", h=HEADS), None, (ld_wqkv, 16)))
        SET_WVT, SET_W2T, SET_W1, SET_W3, SET_WVO, SET_BW, SET_MASK = 1, 2, 3, 4, 5, 6, 7
        FIRST_FROM_PSUM = len(splits)
        for c in range(DC):
            splits.append((PS[:, 2 + c, :], w1t[0][:, c], w1t[1][:, c], None, (set_pe, SET_W1)))
        for c in range(DC):
            splits.append((PS[:, 4 + c, :].rearrange("p (t o) -> p t o", t=2), w3t[0][:, c], w3t[1][:, c], None,
                           (set_pe, SET_W3)))
        FIRST_FROM_SBUF = len(splits)
        splits.append((wout_raw[:], wout[0][:], wout[1][:], None, (ld_wout, 16)))
        for k in range(2):
            splits.append((wk_raw[:, k], wk01[0][:, :, k, :], wk01[1][:, :, k, :], None, (ld_wk, 48)))
        splits.append((wk_raw[:, 2], wk2[0][:, :, 0:D], wk2[1][:, :, 0:D], None, (ld_wk, 48)))
        FIRST_DERIVED = len(splits)
        splits.append((PS[:, bQ, :].rearrange("p (c d) -> p c d", c=DC), wvo[0][:, :, INNER:], wvo[1][:, :, INNER:],
                       None, (set_pe, SET_WVO)))
        for k in range(HC):
            splits.append((w2T_raw[:, k], w2t[0][:, k], w2t[1][:, k], gamma_c[:, k:k + 1], (set_copy, 2)))
        splits.append((wji[:].rearrange("p t c -> p c t"), wk2[0][:, :, D:], wk2[1][:, :, D:], None, (set_wji, 1)))
        N_SPLITS = len(splits)
        N_COPIES = 4
        N_SMALL = 3

        xg = x.rearrange("g n d -> n g d")
        ag = adj.rearrange("g n m -> n g m")
        og = out.rearrange("g n d -> n g d")
        mask_rows = nodemask.rearrange("(i g) n -> i (g n)", g=G)

        def set_up_done(eng):
            eng.wait_ge(set_hi, N_SPLITS)
            eng.wait_ge(set_lo, N_SPLITS - (FIRST_DERIVED - FIRST_FROM_SBUF))
            eng.wait_ge(set_pool_lo, FIRST_DERIVED - FIRST_FROM_SBUF)
            eng.wait_ge(set_copy, N_COPIES)
            eng.wait_ge(set_small, N_SMALL)
            eng.wait_ge(pool_const, 12)
            eng.wait_ge(ld_vec, 16 * 3)

        dve_past, pool_past = sem("dve_past"), sem("pool_past")

        def settle(eng):
            eng.sem_inc(dve_past if eng is nc.vector else pool_past, 1)

        block = ctx.enter_context(nc.Block())

        @block.sync
        def _(sp):
            sp.dma_start(wqkv_raw[:].rearrange("p c h t d -> p c (h t d)"),
                         W_qkv.rearrange("(c p) n -> p c n", p=P)).then_inc(ld_wqkv, 16)
            sp.dma_start(w2_raw[:], W2.rearrange("(c p) n -> p c n", p=P)).then_inc(ld_w2, 16)
            sp.dma_start(w1_raw[:], W1.rearrange("(c p) n -> p c n", p=P)).then_inc(ld_w1, 16)
            sp.dma_start(w3_raw[:], W3.rearrange("(c p) n -> p c n", p=P)).then_inc(ld_w3, 16)

            def load_group(i):
                sp.dma_start(adj_in[:], ag[:, bass.ds(i * G, G), :]).then_inc(a_in, 16)
                sp.dma_start(xin[:], xg[:, bass.ds(i * G, G), :]).then_inc(x_in, 16)
                sp.dma_start(mask_bc8[:], mask_rows[bass.ds(i, 1), :].rearrange("a n -> (a n)").partition_broadcast(P))\
                    .then_inc(m_in, 16)

            load_group(0)
            sp.dma_start(aw_bc[:], aw.rearrange("(t n) a -> t (n a)", t=2).partition_broadcast(P)).then_inc(ld_gate, 16)
            sp.dma_start(bv_bc[:], bv.partition_broadcast(P)).then_inc(ld_gate, 16)
            sp.dma_start(ab_bc[:], ab.partition_broadcast(P)).then_inc(ld_gate, 16)
            sp.dma_start(bk_raw[:], bk.partition_broadcast(P)).then_inc(ld_gate, 16)
            sp.dma_start(wout_raw[:], W_out.rearrange("(c p) n -> p c n", p=P)).then_inc(ld_wout, 16)
            for k in range(3):
                sp.dma_start(wk_raw[:, k], Wk[k].rearrange("(c p) n -> p c n", p=P)).then_inc(ld_wk, 16)

            def used(i):
                sp.wait_ge(pe_adjT, i + 1)
                sp.wait_ge(pe_xT0, i + 1)
                sp.wait_ge(dve_deg, i + 1)
                sp.wait_ge(dve_DH, i * G + G)
                sp.wait_ge(pool_resid0, i + 1)
                sp.wait_ge(act_mbc, i + 1)
                sp.wait_ge(act_mrow, i * 2 + 2)

            def store_group(j):
                sp.wait_ge(pool_out, j * G + G)
                sp.dma_start(og[:, bass.ds(j * G, G), :], xout[:]).then_inc(y_out, 16)

            used(0)
            load_group(1)
            with sp.Fori(0, ITERS - 2) as j:
                used(j + 1)
                load_group(j + 2)
                store_group(j)
            store_group(ITERS - 2)
            store_group(ITERS - 1)
            sp.wait_ge(y_out, 16 * ITERS)

        @block.tensor
        def _(pe):
            def mm3(dst, lhs, rhs, start=True, stop=True):
                pe.matmul(dst, lhs[0], rhs[0], start=start, stop=False)
                pe.matmul(dst, lhs[0], rhs[1], start=False, stop=False)
                return pe.matmul(dst, lhs[1], rhs[0], start=False, stop=stop)

            def both(t, *index):
                return t[0][index], t[1][index]

            A = slice(None)

            def set_up():
                pe.wait_ge(ident_ok, 2)
                pe.wait_ge(set_flat, 1)
                for k in range(IC):
                    for c in range(DC):
                        last = pe.transpose(PS[:, bA + k // 2, (k % 2) * D + c * P:(k % 2) * D + (c + 1) * P],
                                            wv_flat[:, c, k * P:(k + 1) * P], ident[:])
                last.then_inc(set_pe, 1)
                pe.wait_ge(ld_w2, 16)
                for k in range(HC):
                    for c in range(DC):
                        last = pe.transpose(PS[:, bQ + k // 2, (k % 2) * D + c * P:(k % 2) * D + (c + 1) * P],
                                            w2_raw[:, c, k * P:(k + 1) * P], ident[:])
                last.then_inc(set_pe, 1)
                pe.wait_ge(ld_w1, 16)
                for c in range(DC):
                    for k in range(HC):
                        last = pe.transpose(PS[:, 2 + c, k * P:(k + 1) * P], w1_raw[:, k, c * P:(c + 1) * P], ident[:])
                last.then_inc(set_pe, 1)
                pe.wait_ge(ld_w3, 16)
                for c in range(DC):
                    for t in range(2):
                        for o in range(DC):
                            last = pe.transpose(PS[:, 4 + c, t * D + o * P:t * D + (o + 1) * P],
                                                w3_raw[:, o, t * D + c * P:t * D + (c + 1) * P], ident[:])
                last.then_inc(set_pe, 1)

                pe.wait_ge(set_copy, 2)
                pe.wait_ge(set_hi, FIRST_FROM_SBUF)
                pe.wait_ge(set_lo, FIRST_FROM_SBUF)
                group(None, None, 0)

                pe.wait_ge(ld_wout, 16)
                for c in range(DC):
                    for k in range(IC):
                        last = pe.matmul(PS[:, bQ, c * D:(c + 1) * D], wvT[:, k, c * P:(c + 1) * P], wout_raw[:, k, :],
                                         start=(k == 0), stop=(k == IC - 1))
                last.then_inc(set_pe, 1)
                pe.wait_ge(set_beta, 1)
                for k in range(HC):
                    last = pe.matmul(PS[:, bR, 0:D], beta_bc[:, k, :], w2T_raw[:, k, :],
                                     start=(k == 0), stop=(k == HC - 1))
                last.then_inc(set_pe, 1)
                pe.wait_ge(set_maskf, 1)
                pe.transpose(PS[:, bB, 0:NG], maskf[:], ident[0:NG, 0:NG]).then_inc(set_pe, 1)

            def adjT_(i, j):
                pe.wait_ge(a_in, i * 16 + 16)
                if j is not None:
                    pe.wait_ge(dve_o2, j * G + 1)
                for g in range(G):
                    last = pe.transpose(PS[:, bA, g * P:(g + 1) * P], adj_in[:, g, :], ident[:])
                last.then_inc(pe_adjT, 1)

            def xT0_(i):
                pe.wait_ge(x_in, i * 16 + 16)
                pe.wait_ge(dve_O, i * G)
                for c in range(DC):
                    for g in range(G):
                        last = pe.transpose(PS[:, bE, (c * G + g) * P:(c * G + g + 1) * P],
                                            xin[:, g, c * P:(c + 1) * P], ident[:])
                last.then_inc(pe_xT0, 1)

            def qk_(i, k):
                bank = (bC, bD)[k % 2]
                if k == 0:
                    pe.wait_ge(act_xT0, i + 1)
                    pe.wait_ge(dve_xT0, i + 1)
                    pe.wait_ge(dve_O, i * G)
                if k == 1:
                    pe.wait_ge(dve_y0, i * G)
                if k >= 2:
                    pe.wait_ge(act_qk, i * 4 + k - 1)
                for m in range(2 * k, 2 * k + 2):
                    t, h = m // 4, 2 * (m % 4)
                    for c in range(DC):
                        last = mm3(PS[:, bank, (m % 2) * G * P:(m % 2 + 1) * G * P],
                                   both(wqk, A, c, t, slice(h, h + 2)), both(xT0, A, c),
                                   start=(c == 0), stop=(c == DC - 1))
                last.then_inc(pe_qk, 1)

            def D_(i):
                pe.wait_ge(act_adjT, i + 1)
                pe.wait_ge(dve_ax, i * G)
                pe.wait_ge(dve_HT, i + 1)
                pe.wait_ge(dve_wone, i + 1)
                for g in range(G):
                    last = pe.matmul(PS[:, bA, 2 * g:2 * g + 2], HT[:, g, :], wone[:, g, :], start=True, stop=True)
                last.then_inc(pe_D, 1)

            def v_(i, g):
                bv_, bo_ = ((bB, bD), (bE, bC))[g]
                for c in range(DC):
                    last = mm3(PS[:, bv_, :], both(xT0, A, c, g), both(wvo, A, c, slice(0, INNER)),
                               start=(c == 0), stop=(c == DC - 1))
                last.then_inc(pe_v, 1)
                pe.wait_ge(act_qk, i * 4 + 4)
                for c in range(DC):
                    last = mm3(PS[:, bo_, 0:D], both(xT0, A, c, g), both(wvo, A, c, slice(INNER, INNER + D)),
                               start=(c == 0), stop=(c == DC - 1))
                last.then_inc(pe_vo, 1)

            def DHT_(i):
                pe.wait_ge(dve_DH, i * G + G)
                for g in range(G):
                    last = pe.transpose(PS[:, bA, g * P:(g + 1) * P], DHn[:, g, :], ident[:])
                last.then_inc(pe_DHT, 1)

            def AT_(i):
                pe.wait_ge(act_DHT, i + 1)
                pe.wait_ge(pool_BHT, i * G + G)
                for g in range(G):
                    last = pe.matmul(PS[:, bA, g * P:(g + 1) * P], BHT[:, g, :], DHT[:, g, :], start=True, stop=True)
                last.then_inc(pe_AT, 1)

            def S_(i, t):
                if t == 0:
                    pe.wait_ge(act_mrow, i * 2 + 2)
                pe.wait_ge(act_v, i * G + t + 1)
                pe.wait_ge(act_vo, i * G + t + 1)
                pe.wait_ge(dve_vo, i * G + t + 1)
                banks = ((bB, bD), (bC, bE))[t]
                for par in range(2):
                    p = par * DH
                    pe.matmul(PS[:, banks[par], :], mrow_l[p:p + DH, t, :],
                              mrow_r[p:p + DH, t:t + 1, :].to_broadcast([DH, HEADS // 2, P]),
                              start=True, stop=False, skip_group_check=True)
                for k in range(HEADS // 2):
                    for par in range(2):
                        p = par * DH
                        last = pe.matmul(PS[:, banks[par], k * P:(k + 1) * P], qk[p:p + DH, k, t, :],
                                         qk[p:p + DH, QKB // 2 + k, t, :], start=False,
                                         stop=(k == HEADS // 2 - 1), skip_group_check=True)
                last.then_inc(pe_S, 1)

            def PT_(i, t):
                pe.wait_ge(act_exp, i * G + t + 1)
                for h in range(HEADS):
                    last = pe.transpose(PS[:, (bB, bD)[h // 4], (h % 4) * P:(h % 4 + 1) * P], prob[:, t, h, :],
                                        ident[:])
                last.then_inc(pe_PT, 1)

            def PV_(i, t, half):
                if t == 0:
                    pe.wait_ge(dve_sub, i * G + G)
                    pe.wait_ge(act_v, i * G + G)
                pe.wait_ge(act_PT, i * G + t + 1)
                for slot in range(half * HEADS // 2, (half + 1) * HEADS // 2):
                    h = 2 * (slot % 4) + slot // 4
                    last = pe.matmul(PS[:, (bC, bE)[h // 4], (h % 4) * VX:(h % 4 + 1) * VX], probT[:, slot, :],
                                     vext[:, t, h, :], start=True, stop=True)
                if half == 1:
                    last.then_inc(pe_PV, 1)

            def OT_(i, t, j):
                pe.wait_ge(dve_O, i * G + t + 1)
                if t == 0 and j is not None:
                    pe.wait_ge(act_E, j * 2 * G + 2 * G)
                for k in range(IC):
                    last = pe.transpose(PS[:, bP, k * P:(k + 1) * P], osb[:, 2 * k:2 * k + 2, :], ident[:])
                last.then_inc(pe_OT, 1)

            def W_(i, t):
                pe.wait_ge(act_OT, i * G + t + 1)
                pe.wait_ge(dve_OT, i * G + t + 1)
                if t == 0:
                    pe.wait_ge(pool_gT, i + 1)
                dst = PS[:, (bB, bD)[t], 0:D]
                for k in range(IC):
                    mm3(dst, both(oT, A, t, k), both(wout, A, k), start=(k == 0), stop=False)
                mm3(dst, both(gT, A, t), both(vo, A, t), start=False, stop=True).then_inc(pe_y0, 1)

            def ax_(j, g, n):
                if g == 1 and n is not None:
                    pe.wait_ge(act_adjT, n + 1)
                pe.wait_ge(dve_x1, j * G + g + 1)
                pe.wait_ge(act_AT, j + 1)
                for c in range(DC):
                    last = pe.matmul(PS[:, (bP, bA)[g], c * P:(c + 1) * P], x1[:, g, c * P:(c + 1) * P], AT[:, g, :],
                                     start=True, stop=True)
                last.then_inc(pe_ax, 1)

            def h_(j, g):
                pe.wait_ge(act_ax, j * G + g + 1)
                pe.wait_ge(dve_ax, j * G + g + 1)
                for c in range(DC):
                    last = mm3(PS[:, (bR, bP)[g], :], both(axT, A, g, c), both(w1t, A, c),
                               start=(c == 0), stop=(c == DC - 1))
                last.then_inc(pe_h, 1)

            def hT_(j, g):
                pe.wait_ge(dve_hn, j * G + g + 1)
                if g == 0:
                    pe.wait_ge(dve_o3, j * G)
                for k in range(HC):
                    last = pe.matmul(PS[:, (bQ, bR)[g], k * P:(k + 1) * P], hid[:, g, k * P:(k + 1) * P], AT[:, g, :],
                                     start=True, stop=True)
                last.then_inc(pe_hT, 1)

            def y1_(j, g):
                pe.wait_ge(act_hT, j * G + g + 1)
                pe.wait_ge(dve_hT, j * G + g + 1)
                for k in range(HC):
                    last = mm3(PS[:, (bP, bQ)[g], 0:D], both(hT, A, g, k), both(w2t, A, k),
                               start=(k == 0), stop=(k == HC - 1))
                last.then_inc(pe_y1, 1)

            def xT2_(j):
                pe.wait_ge(dve_x2, j * G + G)
                for c in range(DC):
                    for g in range(G):
                        last = pe.transpose(PS[:, bR, (c * G + g) * P:(c * G + g + 1) * P],
                                            x2[:, g, c * P:(c + 1) * P], ident[:])
                last.then_inc(pe_xT2, 1)

            def xT3_(j, g):
                pe.wait_ge(dve_x3, j * G + g + 1)
                for c in range(DC):
                    last = pe.transpose(PS[:, (bQ, bR)[g], c * P:(c + 1) * P], x3[:, g, c * P:(c + 1) * P], ident[:])
                last.then_inc(pe_xT3, 1)

            def Z_(j, g, i):
                if g == 0:
                    pe.wait_ge(act_xT2, j + 1)
                    pe.wait_ge(dve_xT2, j + 1)
                elif i is not None:
                    pe.wait_ge(act_AT, i + 1)
                for c in range(DC):
                    last = mm3(PS[:, (bP, bR)[g], :], both(xT2, A, c, g), both(wk01, A, c),
                               start=(c == 0), stop=(c == DC - 1))
                last.then_inc(pe_Z01, 1)
                for c in range(DC):
                    last = mm3(PS[:, (bQ, bA)[g], 0:D + 2], both(xT2, A, c, g), both(wk2, A, c),
                               start=(c == 0), stop=(c == DC - 1))
                last.then_inc(pe_Z2, 1)

            def si_(j, g):
                pe.wait_ge(dve_sj, j * G + g + 1)
                pe.wait_ge(act_Z01, j * G + 1)
                if g == 1:
                    pe.wait_ge(act_Z2, j * G + 1)
                    pe.wait_ge(dve_Z2, j * G + 1)
                pe.transpose(PS[:, (bP, bQ)[g], 0:P], sji[:, g, 1:2].to_broadcast([P, P]), ident[:]).then_inc(pe_si, 1)

            def T1_(j, g):
                pe.wait_ge(dve_al, j * G + g + 1)
                pe.wait_ge(act_E, j * 2 * G + 2 * G)
                pe.wait_ge(act_Z2, j * G + g + 1)
                pe.wait_ge(dve_Z2, j * G + g + 1)
                pe.wait_ge(act_Z01, j * G + g + 1)
                mm3(PS[:, (bQ, bR)[g], 0:D + 2], both(alT, A, g), both(z2, A, g)).then_inc(pe_T1, 1)

            def T2_(j, g):
                pe.wait_ge(act_Y, j * G + g + 1)
                pe.wait_ge((dve_Yl, pool_Yl)[g], j + 1)
                mm3(PS[:, (bA, bQ)[g], 0:D], both(alT, A, g), both(yT, A, g)).then_inc(pe_T2, 1)

            def Z3_(j, g):
                pe.wait_ge(act_xT3, j * G + g + 1)
                pe.wait_ge(dve_xT3, j * G + g + 1)
                for c in range(DC):
                    last = mm3(PS[:, (bP, bA)[g], :], both(xT2, A, c, g), both(w3t, A, c),
                               start=(c == 0), stop=(c == DC - 1))
                last.then_inc(pe_Z3, 1)

            def T3_(j, g):
                pe.wait_ge(pool_aT, j + 1)
                pe.wait_ge(act_za, j * G + g + 1)
                pe.wait_ge(act_zb, j * G + g + 1)
                pe.wait_ge(dve_zb, j * G + g + 1)
                mm3(PS[:, (bQ, bE)[g], 0:D], both(aT, A, g), both(zb, A, g)).then_inc(pe_T3, 1)

            def group(i, j, n):
                F, B, L = i is not None, j is not None, n is not None
                if F:
                    qk_(i, 2)
                if B:
                    h_(j, 0)
                    h_(j, 1)
                if F:
                    qk_(i, 3)
                    D_(i)
                    v_(i, 0)
                if B:
                    hT_(j, 0)
                    hT_(j, 1)
                if F:
                    DHT_(i)
                    v_(i, 1)
                if B:
                    y1_(j, 0)
                    y1_(j, 1)
                if F:
                    AT_(i)
                    S_(i, 0)
                if B:
                    xT2_(j)
                if F:
                    S_(i, 1)
                if B:
                    Z_(j, 0, i)
                if F:
                    PT_(i, 0)
                if B:
                    Z_(j, 1, i)
                    si_(j, 0)
                if F:
                    PV_(i, 0, 0)
                if B:
                    si_(j, 1)
                if F:
                    PV_(i, 0, 1)
                    PT_(i, 1)
                if B:
                    T1_(j, 0)
                    T1_(j, 1)
                if F:
                    OT_(i, 0, j)
                    PV_(i, 1, 0)
                    PV_(i, 1, 1)
                if B:
                    T2_(j, 0)
                    T2_(j, 1)
                if F:
                    OT_(i, 1, j)
                    W_(i, 0)
                if L:
                    xT0_(n)
                if F:
                    W_(i, 1)
                if L:
                    adjT_(n, j)
                if B:
                    xT3_(j, 0)
                    xT3_(j, 1)
                if L:
                    qk_(n, 0)
                if B:
                    Z3_(j, 0)
                    Z3_(j, 1)
                    T3_(j, 0)
                if F:
                    ax_(i, 0, n)
                if L:
                    qk_(n, 1)
                if B:
                    T3_(j, 1)
                if F:
                    ax_(i, 1, n)

            set_up()
            set_up_done(pe)
            group(0, None, 1)
            group(1, 0, 2)
            with pe.Fori(1, ITERS - 2) as j:
                group(j + 1, j, j + 2)
            group(ITERS - 1, ITERS - 2, None)
            group(None, ITERS - 1, None)

        @block.scalar
        def _(act):
            act.dma_start(mask8[:], nodemask).then_inc(ld_mask, 16)
            act.dma_start(beta_c[:], beta.rearrange("(k p) -> p k", p=P), allow_slow_non_contiguous=True).then_inc(ld_gb, 16)
            act.dma_start(gamma_c[:], gamma.rearrange("(k p) -> p k", p=P), allow_slow_non_contiguous=True).then_inc(ld_gb, 16)
            act.dma_start(wv2_raw[:], Wv.rearrange("(c p) n -> p c n", p=P)).then_inc(ld_wv, 16)

            copy = ACT.Copy

            def set_up():
                def move(dst, src, n):
                    act.wait_ge(set_pe, n)
                    act.activation(dst, src, copy).then_inc(set_copy, 1)

                for n, (src, hi, lo, factor, (ready, value)) in enumerate(splits):
                    if n == FIRST_FROM_PSUM:
                        move(wvT[:].rearrange("p (b k) d -> p b (k d)", b=2), PS[:, bA:bA + 2, :], SET_WVT)
                        move(w2T_raw[:].rearrange("p (b k) d -> p b (k d)", b=2), PS[:, bQ:bQ + 2, :], SET_W2T)
                    if n == FIRST_FROM_SBUF:
                        xT0_(0)
                        adjT_(0)
                    if n == FIRST_DERIVED:
                        qk_(0, 0)
                        qk_(0, 1)
                    act.wait_ge(ready, value)
                    if factor is None:
                        act.activation(hi, src, copy).then_inc(set_hi, 1)
                    else:
                        act.wait_ge(ld_gb, 32)
                        act.activation(hi, src, copy, scale=factor).then_inc(set_hi, 1)
                move(bw_bc[:], PS[:, bR, 0:D], SET_BW)
                move(mask33[:], PS[:, bB, 0:NG], SET_MASK)

            def adjT_(i):
                act.wait_ge(pe_adjT, i + 1)
                act.wait_ge(act_adjTb, i)
                act.activation(adjT[:].rearrange("p g n -> p (g n)"), PS[:, bA, 0:G * P], copy).then_inc(act_adjT, 1)

            def xT0_(i):
                act.wait_ge(pe_xT0, i + 1)
                act.activation(xT0[0][:].rearrange("p c g n -> p (c g n)"), PS[:, bE, :], copy).then_inc(act_xT0, 1)

            def gate_(i):
                act.wait_ge(act_adjT, i + 1)
                act.wait_ge(pool_gT, i)
                act.activation(gate[:], adjT[:], ACT.Exp, scale=-1.0).then_inc(act_gate, 1)

            def mask_(i):
                act.wait_ge(m_in, i * 16 + 16)
                act.wait_ge(pe_S, i * G)
                act.wait_ge(pool_gate, i)
                for dst, a in ((mrow_l, 0), (mrow_r, 2)):
                    act.activation(dst[:].rearrange("p g n -> p (g n)"), mask_bc8[:], ACT.Identity,
                                   bias=mask_ab[:, a + 1:a + 2], scale=mask_ab[:, a:a + 1]).then_inc(act_mrow, 1)
                act.activation(mbc[:], mask_bc8[:], copy).then_inc(act_mbc, 1)

            def gT_(i):
                act.wait_ge(pool_gate, i + 1)
                act.activation(gT[0][:], gate[:], copy).then_inc(act_gT, 1)

            def carry(i):
                act.wait_ge(dve_al, i * G)
                act.wait_ge(pool_aT, i)
                act.activation(adjTb[:], adjT[:], copy).then_inc(act_adjTb, 1)

            def qk_(i, k):
                act.wait_ge(pe_qk, i * 4 + k + 1)
                act.activation(qk[:, 2 * k:2 * k + 2].rearrange("p m g n -> p (m g n)"),
                               PS[:, (bC, bD)[k % 2], :], copy).then_inc(act_qk, 1)

            def v_(i, g):
                bv_, bo_ = ((bB, bD), (bE, bC))[g]
                act.wait_ge(pe_v, i * G + g + 1)
                act.activation(vext[:, g, :, 0:DH], PS[:, bv_, :].rearrange("p (h d) -> p h d", h=HEADS), copy)\
                    .then_inc(act_v, 1)
                act.wait_ge(pe_vo, i * G + g + 1)
                act.wait_ge(dve_m33, i + 1)
                act.activation(vo[0][:, g, :], PS[:, bo_, 0:D], copy, scale=m33[:, g:g + 1]).then_inc(act_vo, 1)

            def DHT_(i):
                act.wait_ge(pe_DHT, i + 1)
                act.activation(DHT[:].rearrange("p g n -> p (g n)"), PS[:, bA, 0:G * P], copy).then_inc(act_DHT, 1)

            def AT_(i):
                act.wait_ge(pe_AT, i + 1)
                act.activation(AT[:].rearrange("p g n -> p (g n)"), PS[:, bA, 0:G * P], copy).then_inc(act_AT, 1)

            def exp_(i, t):
                act.wait_ge(dve_sub, i * G + t + 1)
                act.activation(prob[:, t], prob[:, t], ACT.Exp, scale=SCALE).then_inc(act_exp, 1)

            def PT_(i, t):
                act.wait_ge(pe_PT, i * G + t + 1)
                act.activation(probT[:].rearrange("p (b k) n -> p b (k n)", b=2), PS[:, bB:bD + 1, :], copy)\
                    .then_inc(act_PT, 1)

            def OT_(i, t):
                act.wait_ge(pe_OT, i * G + t + 1)
                act.activation(oT[0][:, t].rearrange("p k n -> p (k n)"), PS[:, bP, :], copy).then_inc(act_OT, 1)

            def u_(j, g):
                act.wait_ge(dve_Dn, j + 1)
                act.activation(resid[:, g], bw_bc[:], copy, scale=rA[:, g:g + 1]).then_inc(act_u, 1)

            def x1_(j, g):
                act.wait_ge(dve_x1, j * G + g + 1)
                act.activation(x1_twice[:, g], x1[:, g], copy, scale=2.0).then_inc(act_x1, 1)

            def aT_(j):
                act.wait_ge(pe_T3, j * G)
                act.wait_ge(act_adjTb, j + 1)
                act.activation(aT[0][:], adjTb[:], copy).then_inc(act_aT, 1)

            def ax_(j, g):
                act.wait_ge(pe_ax, j * G + g + 1)
                act.activation(axT[0][:, g].rearrange("p c n -> p (c n)"), PS[:, (bP, bA)[g], 0:D], copy)\
                    .then_inc(act_ax, 1)

            def relu_(j, g):
                act.wait_ge(dve_hb, j * G + g + 1)
                act.activation(hid[:, g], hid[:, g], ACT.Relu).then_inc(act_relu, 1)

            def hT_(j, g):
                act.wait_ge(pe_hT, j * G + g + 1)
                act.activation(hT[0][:, g].rearrange("p k n -> p (k n)"), PS[:, (bQ, bR)[g], :], copy)\
                    .then_inc(act_hT, 1)

            def xT2_(j):
                act.wait_ge(pe_xT2, j + 1)
                act.activation(xT2[0][:].rearrange("p c g n -> p (c g n)"), PS[:, bR, :], copy).then_inc(act_xT2, 1)

            def xT3_(j, g):
                act.wait_ge(pe_xT3, j * G + g + 1)
                act.activation(xT2[0][:, :, g, :], PS[:, (bQ, bR)[g], 0:D].rearrange("p (c n) -> p c n", c=DC), copy)\
                    .then_inc(act_xT3, 1)

            def Z01_(j, g):
                act.wait_ge(pe_Z01, j * G + g + 1)
                act.activation(z01[:, g].rearrange("p t d -> p (t d)"), PS[:, (bP, bR)[g], :], copy)\
                    .then_inc(act_Z01, 1)

            def Z2_(j, g):
                act.wait_ge(pe_Z2, j * G + g + 1)
                act.wait_ge(dve_sj, j * G + g + 1)
                act.activation(z2[0][:, g, 0:D], PS[:, (bQ, bA)[g], 0:D], copy).then_inc(act_Z2, 1)

            def E_(j, g):
                act.wait_ge(pe_si, j * G + g + 1)
                act.wait_ge(dve_sj, j * G + g + 1)
                src = PS[:, (bP, bQ)[g], 0:P]
                act.activation(e1[:, g], src, ACT.Exp, bias=sji[:, g, 0:1]).then_inc(act_E, 1)
                act.activation(e2[:, g], src, ACT.Exp, bias=sji[:, g, 2:3], scale=SLOPE).then_inc(act_E, 1)

            def al_(j, g):
                act.wait_ge(dve_alw, j * G + g + 1)
                act.activation(alT[0][:, g], al[:, g], copy).then_inc(act_al, 1)

            def Y_(j, g):
                act.wait_ge(dve_Y, j * G + g + 1)
                act.activation(yT[0][:, g], yv[:, g], copy).then_inc(act_Y, 1)

            def Z3_(j, g):
                act.wait_ge(pe_Z3, j * G + g + 1)
                act.activation(zb[0][:, g], PS[:, (bP, bA)[g], D:2 * D], copy).then_inc(act_zb, 1)
                act.activation(za[:, g], PS[:, (bP, bA)[g], 0:D], copy).then_inc(act_za, 1)

            def group(i, j, n):
                F, B, L = i is not None, j is not None, n is not None
                if F:
                    gate_(i)
                if B:
                    u_(j, 0)
                    u_(j, 1)
                if F:
                    qk_(i, 2)
                    mask_(i)
                if B:
                    relu_(j, 0)
                    relu_(j, 1)
                if F:
                    qk_(i, 3)
                    v_(i, 0)
                if B:
                    aT_(j)
                    hT_(j, 0)
                if F:
                    DHT_(i)
                if B:
                    hT_(j, 1)
                if F:
                    v_(i, 1)
                    AT_(i)
                    gT_(i)
                if B:
                    xT2_(j)
                if F:
                    exp_(i, 0)
                if B:
                    Z01_(j, 0)
                    Z2_(j, 0)
                if F:
                    PT_(i, 0)
                    exp_(i, 1)
                if B:
                    E_(j, 0)
                    E_(j, 1)
                    al_(j, 0)
                    Z2_(j, 1)
                    al_(j, 1)
                    Z01_(j, 1)
                if F:
                    PT_(i, 1)
                    OT_(i, 0)
                if B:
                    Y_(j, 0)
                    Y_(j, 1)
                if F:
                    carry(i)
                    OT_(i, 1)
                if L:
                    xT0_(n)
                    adjT_(n)
                if B:
                    xT3_(j, 0)
                    xT3_(j, 1)
                if L:
                    qk_(n, 0)
                if B:
                    Z3_(j, 0)
                    Z3_(j, 1)
                if F:
                    x1_(i, 0)
                    ax_(i, 0)
                if L:
                    qk_(n, 1)
                if F:
                    ax_(i, 1)
                    x1_(i, 1)

            set_up()
            set_up_done(act)
            group(0, None, 1)
            group(1, 0, 2)
            with act.Fori(1, ITERS - 2) as j:
                group(j + 1, j, j + 2)
            group(ITERS - 1, ITERS - 2, None)
            group(None, ITERS - 1, None)

        @block.vector
        def _(dve):
            def f32(t):
                return t.bitcast(F32)

            def set_up():
                dve.wait_ge(ld_wqkv, 16)
                dve.tensor_copy(wv_flat[:].rearrange("p c (h d) -> p c h d", h=HEADS), wqkv_raw[:, :, :, 2, :])\
                    .then_inc(set_flat, 1)

                def rows():
                    dve.wait_ge(ld_mask, 16)
                    dve.tensor_scalar(maskf[:], mask8[:], MIX, None, ALU.mult).then_inc(set_maskf, 1)
                    dve.wait_ge(ld_gb, 32)
                    dve.tensor_copy(beta_bc[:], beta_c[:].unsqueeze(2).to_broadcast([P, HC, P])).then_inc(set_beta, 1)

                def gate_vectors():
                    dve.wait_ge(set_prod, 2)
                    dve.tensor_reduce(wji[:], prod[:], AX_X, ALU.add).then_inc(set_wji, 1)
                    dve.wait_ge(set_prod, 3)
                    dve.tensor_reduce(bsum[:], bprod[:], AX_XY, ALU.add).then_inc(set_small, 1)
                    dve.wait_ge(set_small, 1)
                    dve.tensor_tensor(gate_c[:, 0:1], bsum[:], ab_bc[:], ALU.add).then_inc(set_small, 1)
                    dve.tensor_reduce(bk_bc[:], bk_raw[:].rearrange("p k d -> p d k"), AX_X, ALU.add).then_inc(set_small, 1)

                for n, (src, hi, lo, factor, (ready, value)) in enumerate(splits):
                    if n == FIRST_FROM_PSUM:
                        rows()
                    if n == FIRST_DERIVED:
                        group(None, None, 0)
                        gate_vectors()
                    if FIRST_FROM_SBUF <= n < FIRST_DERIVED:
                        continue
                    dve.wait_ge(set_hi, n + 1)
                    dve.wait_ge(ready, value)
                    if factor is None:
                        dve.tensor_tensor(lo, src, f32(hi), ALU.subtract).then_inc(set_lo, 1)
                    else:
                        dve.scalar_tensor_tensor(lo, src, factor, f32(hi), ALU.mult, ALU.subtract).then_inc(set_lo, 1)

            def low_part(lo, src, hi, hi_ready, value, done):
                dve.wait_ge(hi_ready, value)
                dve.tensor_tensor(lo, src, f32(hi), ALU.subtract).then_inc(done, 1)

            def stats(step, src, n, g, done):
                aggregate(step, step.count(dve.bn_stats(st[:, n, g], src)), n, g, done)

            def aggregate(step, counted, n, g, done):
                step.wait(counted)
                settle(dve)
                dve.bn_aggr(mv[:, n, g], st[:, n, g]).then_inc(done, 1)

            def normalise(dst, src, n, g, scale_ready, value, done):
                dve.wait_ge(scale_ready, value)
                dve.tensor_scalar(dst, src, mv[:, n, g, 0:1], rs[:, n, g, 1:2], ALU.subtract, ALU.mult)\
                    .then_inc(done, 1)

            def front(i):
                step = Steps(dve, dve_fstep, i, DVE_FSTEPS)
                counted = {}

                def xT0_():
                    low_part(xT0[1][:].rearrange("p c g n -> p (c g n)"), PS[:, bE, :],
                             xT0[0][:].rearrange("p c g n -> p (c g n)"), act_xT0, i + 1, dve_xT0)

                def incidence():
                    dve.wait_ge(act_adjT, i + 1)
                    dve.tensor_scalar(HT[:], adjT[:], 0.0, None, ALU.not_equal).then_inc(dve_HT, 1)
                    dve.tensor_copy(wone[:, :, 0:1], adjT[:, :, 0:1]).then_inc(dve_wone, 1)
                    dve.tensor_copy(m33[:], mask33[:, bass.ds(i * G, G)]).then_inc(dve_m33, 1)

                def counts():
                    dve.wait_ge(dve_HT, i + 1)
                    step.done(dve.tensor_reduce(cnt[:], HT[:], AX_X, ALU.add))
                    step.done(dve.tensor_scalar(cnt[:], cnt[:], 1.0, None, ALU.max))
                    dve.reciprocal(Be[:], cnt[:]).then_inc(dve_Be, 1)
                    dve.wait_ge(a_in, i * 16 + 16)
                    dve.tensor_reduce(degf[:], adj_in[:], AX_X, ALU.add).then_inc(dve_deg, 1)

                def Dn_():
                    dve.wait_ge(pe_D, i + 1)
                    step.done(dve.tensor_copy(dcol[:].rearrange("p g t -> p (g t)"), PS[:, bA, 0:2 * G]))
                    dve.tensor_scalar(dpos[:], dcol[:, :, 0], 0.0, None, ALU.is_gt).then_inc(dve_fstep, 1)
                    step.n += 1
                    step.done(dve.tensor_scalar(dsafe[:], dcol[:, :, 0], TINY, None, ALU.max))
                    step.done(dve.reciprocal(drec[:], dsafe[:]))
                    step.done(dve.tensor_tensor(Dn[:], drec[:], dpos[:], ALU.mult))
                    dve.wait_ge(act_u, i * G)
                    dve.tensor_tensor(rA[:], Dn[:], dcol[:, :, 1], ALU.mult).then_inc(dve_Dn, 1)
                    for g in range(G):
                        dve.tensor_scalar(DHn[:, g], adj_in[:, g], 0.0, Dn[:, g:g + 1], ALU.not_equal, ALU.mult)\
                            .then_inc(dve_DH, 1)

                def vo_(g):
                    dve.wait_ge(act_vo, i * G + g + 1)
                    dve.scalar_tensor_tensor(vo[1][:, g], PS[:, (bD, bC)[g], 0:D], m33[:, g:g + 1], f32(vo[0][:, g]),
                                             ALU.mult, ALU.subtract).then_inc(dve_vo, 1)

                def scores(t):
                    dve.wait_ge(pe_S, i * G + t + 1)
                    return (PS[:, bB:bD + 1, :], PS[:, bC:bE + 1, :])[t].rearrange("p b (h n) -> p b h n", n=P)

                def max_(t):
                    s = scores(t)
                    step.done(dve.tensor_reduce(m8[:, t].rearrange("p (b h) -> p b h", b=2), s, AX_X, ALU.max))

                def sub_(t):
                    s = scores(t)
                    m = m8[:, t].rearrange("p (b h) -> p b h", b=2).unsqueeze(3).to_broadcast([P, 2, HEADS // 2, P])
                    dve.tensor_tensor(prob[:, t].rearrange("p (b h) n -> p b h n", b=2), s, m, ALU.subtract)\
                        .then_inc(dve_sub, 1)

                def heads(t):
                    dve.wait_ge(pe_PV, i * G + t + 1)
                    return PS[:, bC:bE + 1, 0:HEADS // 2 * VX].rearrange("p b (h d) -> p b h d", d=VX)

                def rl_(t):
                    counted[t] = step.count(dve.reciprocal(rl[:, t], heads(t)[:, :, :, DH]))

                def O_(t):
                    o = heads(t)
                    step.wait(counted[t])
                    dve.tensor_tensor(osb[:].rearrange("p (b h) d -> p b h d", b=2), o[:, :, :, 0:DH],
                                      rl[:, t].unsqueeze(3).to_broadcast([P, 2, HEADS // 2, DH]), ALU.mult)\
                        .then_inc(dve_O, 1)

                def OT_(t):
                    low_part(oT[1][:, t].rearrange("p k n -> p (k n)"), PS[:, bP, :],
                             oT[0][:, t].rearrange("p k n -> p (k n)"), act_OT, i * G + t + 1, dve_OT)

                def y0_(t):
                    dve.wait_ge(pe_y0, i * G + t + 1)
                    dve.wait_ge(pool_resid0, i + 1)
                    dve.tensor_tensor(ys0[:, t], PS[:, (bB, bD)[t], 0:D], ys0[:, t], ALU.add).then_inc(dve_y0, 1)

                def bn0_(t):
                    dve.wait_ge(dve_y0, i * G + t + 1)
                    counted[t] = step.count(dve.bn_stats(st[:, NORM0, t], ys0[:, t]))

                def mv0_(t):
                    aggregate(step, counted[t], NORM0, t, dve_mv0)

                def x1_(t):
                    normalise(x1[:, t], ys0[:, t], NORM0, t, pool_rs0, i * G + t + 1, dve_x1)

                return step, xT0_, incidence, counts, Dn_, vo_, max_, sub_, rl_, O_, OT_, y0_, bn0_, mv0_, x1_

            def back(j):
                step = Steps(dve, dve_bstep, j, DVE_BSTEPS)
                counted = {}

                def ax_(g):
                    low_part(axT[1][:, g].rearrange("p c n -> p (c n)"), PS[:, (bP, bA)[g], 0:D],
                             axT[0][:, g].rearrange("p c n -> p (c n)"), act_ax, j * G + g + 1, dve_ax)

                def hb_(g):
                    dve.wait_ge(pe_h, j * G + g + 1)
                    dve.tensor_tensor(hid[:, g], PS[:, (bR, bP)[g], :], b1_bc[:], ALU.add).then_inc(dve_hb, 1)

                def hstats_(g):
                    dve.wait_ge(act_relu, j * G + g + 1)
                    stats(step, hid[:, g], NORMH, g, dve_mvh)

                def hn_(g):
                    normalise(hid[:, g], hid[:, g], NORMH, g, pool_rsh, j * G + g + 1, dve_hn)

                def hT_(g):
                    low_part(hT[1][:, g].rearrange("p k n -> p (k n)"), PS[:, (bQ, bR)[g], :],
                             hT[0][:, g].rearrange("p k n -> p (k n)"), act_hT, j * G + g + 1, dve_hT)

                def y1_(g):
                    dve.wait_ge(pe_y1, j * G + g + 1)
                    dve.wait_ge(pool_resid1, j * G + g + 1)
                    dve.wait_ge(pool_out, j * G)
                    step.done(dve.tensor_tensor(ysb[:, g], PS[:, (bP, bQ)[g], 0:D], resid[:, g], ALU.add))
                    stats(step, ysb[:, g], NORM1, g, dve_mv1)

                def x2_(g):
                    normalise(x2[:, g], ysb[:, g], NORM1, g, pool_rs1, j * G + g + 1, dve_x2)

                def xT2_():
                    low_part(xT2[1][:].rearrange("p c g n -> p (c g n)"), PS[:, bR, :],
                             xT2[0][:].rearrange("p c g n -> p (c g n)"), act_xT2, j + 1, dve_xT2)

                def xT3_(g):
                    low_part(xT2[1][:, :, g, :], PS[:, (bQ, bR)[g], 0:D].rearrange("p (c n) -> p c n", c=DC),
                             xT2[0][:, :, g, :], act_xT3, j * G + g + 1, dve_xT3)

                def Z_(g):
                    dve.wait_ge(pe_Z2, j * G + g + 1)
                    step.done(dve.tensor_tensor(sji[:, g, 0:2], PS[:, (bQ, bA)[g], D:D + 2], gate_c[:], ALU.add))
                    dve.tensor_scalar(sji[:, g, 2:3], sji[:, g, 0:1], SLOPE, None, ALU.mult).then_inc(dve_sj, 1)

                def z2_(g):
                    low_part(z2[1][:, g, 0:D], PS[:, (bQ, bA)[g], 0:D], z2[0][:, g, 0:D], act_Z2, j * G + g + 1,
                             dve_Z2)

                def gmax_(g):
                    dve.wait_ge(act_E, j * 2 * G + 2 * g + 2)
                    counted[g] = step.count(dve.tensor_tensor(al[:, g], e1[:, g], e2[:, g], ALU.max))

                def al_(g):
                    step.wait(counted[g])
                    dve.wait_ge(act_adjTb, j + 1)
                    dve.tensor_tensor(al[:, g], al[:, g], adjTb[:, g], ALU.mult).then_inc(dve_alw, 1)

                def all_(g):
                    dve.wait_ge(act_al, j * G + g + 1)
                    dve.wait_ge(dve_alw, j * G + g + 1)
                    dve.tensor_tensor(alT[1][:, g], al[:, g], f32(alT[0][:, g]), ALU.subtract).then_inc(dve_al, 1)

                def den_():
                    dve.wait_ge(pe_T1, j * G + G)
                    step.done(dve.tensor_scalar(den[:], PS[:, bQ:bR + 1, D], DEN_EPS, None, ALU.add))
                    step.done(dve.reciprocal(rden[:], den[:]))

                def Y_(g):
                    dve.wait_ge(act_Z01, j * G + g + 1)
                    b = (bQ, bR)[g]
                    dve.scalar_tensor_tensor(yv[:, g], PS[:, b, 0:D], rden[:, g:g + 1], z01[:, g, 1], ALU.mult,
                                             ALU.add)\
                        .then_inc(dve_Y, 1)

                def Yl_():
                    low_part(yT[1][:, 0], yv[:, 0], yT[0][:, 0], act_Y, j * G + 1, dve_Yl)

                def o2_(g):
                    dve.wait_ge(pe_T2, j * G + g + 1)
                    dve.wait_ge(pool_z0, j * G + g + 1)
                    dve.scalar_tensor_tensor(ysb[:, g], PS[:, (bA, bQ)[g], 0:D], rden[:, g:g + 1], z01[:, g, 0],
                                             ALU.mult, ALU.add).then_inc(dve_o2, 1)

                def y2_(g):
                    dve.wait_ge(dve_o2, j * G + g + 1)
                    counted[g] = step.count(
                        dve.scalar_tensor_tensor(ysb[:, g], ysb[:, g], 0.0, x2[:, g], ALU.max, ALU.add))

                def bn2_(g):
                    step.wait(counted[g])
                    counted[g] = step.count(dve.bn_stats(st[:, NORM2, g], ysb[:, g]))

                def mv2_(g):
                    aggregate(step, counted[g], NORM2, g, dve_mv2)

                def x3_(g):
                    normalise(x3[:, g], ysb[:, g], NORM2, g, pool_rs2, j + 1, dve_x3)

                def deg_():
                    step.done(dve.tensor_scalar(degb[:], degf[:], DEG_EPS, None, ALU.max))
                    step.done(dve.reciprocal(degb[:], degb[:]))

                def zb_(g):
                    dve.wait_ge(act_za, j * G + g + 1)
                    low_part(zb[1][:, g], PS[:, (bP, bA)[g], D:2 * D], zb[0][:, g], act_zb, j * G + g + 1, dve_zb)

                def o3_(g):
                    dve.wait_ge(pe_T3, j * G + g + 1)
                    dve.scalar_tensor_tensor(ysb[:, g], PS[:, (bQ, bE)[g], 0:D], degb[:, g:g + 1], za[:, g],
                                             ALU.mult, ALU.add).then_inc(dve_o3, 1)
                    dve.wait_ge(dve_o3, j * G + g + 1)
                    step.done(dve.scalar_tensor_tensor(ysb[:, g], ysb[:, g], 0.0, x3[:, g], ALU.max, ALU.add))
                    stats(step, ysb[:, g], NORM3, g, dve_mv3)

                return (step, ax_, hb_, hstats_, hn_, hT_, y1_, x2_, xT2_, xT3_, Z_, z2_, gmax_, al_, all_, den_, Y_, Yl_, o2_, y2_, bn2_, mv2_, x3_, deg_, zb_,
                        o3_)

            def group(i, j, n):
                F, B, L = i is not None, j is not None, n is not None
                if F:
                    fstep, _, incidence, counts, Dn_, vo_, max_, sub_, rl_, O_, fOT_, y0_, bn0_, mv0_, x1_ = front(i)
                if B:
                    (bstep, ax_, hb_, hstats_, hn_, hT_, y1_, x2_, xT2_, xT3_, Z_, z2_, gmax_, al_, all_, den_, Y_, Yl_, o2_, y2_, bn2_, mv2_, x3_, deg_, zb_,
                     o3_) = back(j)
                if B:
                    hb_(0)
                if F:
                    incidence()
                if B:
                    hb_(1)
                    hstats_(0)
                    hstats_(1)
                    hn_(0)
                    hn_(1)
                if F:
                    Dn_()
                    vo_(0)
                if B:
                    hT_(0)
                    deg_()
                if F:
                    counts()
                if B:
                    hT_(1)
                if F:
                    vo_(1)
                if B:
                    y1_(0)
                    y1_(1)
                    x2_(0)
                    x2_(1)
                if F:
                    max_(0)
                if B:
                    xT2_()
                if F:
                    sub_(0)
                    max_(1)
                    sub_(1)
                if B:
                    Z_(0)
                    z2_(0)
                    Z_(1)
                    gmax_(0)
                    al_(0)
                    gmax_(1)
                    al_(1)
                if F:
                    rl_(0)
                if B:
                    all_(0)
                    z2_(1)
                    all_(1)
                if F:
                    O_(0)
                if B:
                    den_()
                    Y_(0)
                    Y_(1)
                if F:
                    fOT_(0)
                if B:
                    Yl_()
                if F:
                    rl_(1)
                    O_(1)
                if B:
                    o2_(0)
                    o2_(1)
                    y2_(0)
                    y2_(1)
                if F:
                    fOT_(1)
                if B:
                    bn2_(0)
                    bn2_(1)
                    mv2_(0)
                    mv2_(1)
                if F:
                    y0_(0)
                if L:
                    front(n)[1]()
                if B:
                    x3_(0)
                    x3_(1)
                if F:
                    bn0_(0)
                    mv0_(0)
                if B:
                    xT3_(0)
                    xT3_(1)
                if F:
                    y0_(1)
                    x1_(0)
                    bn0_(1)
                    mv0_(1)
                if B:
                    zb_(0)
                if F:
                    x1_(1)
                if B:
                    zb_(1)
                    o3_(0)
                if F:
                    back(i)[1](0)
                    back(i)[1](1)
                if B:
                    o3_(1)
                if F:
                    assert fstep.n == DVE_FSTEPS, fstep.n
                if B:
                    assert bstep.n == DVE_BSTEPS, bstep.n

            set_up()
            set_up_done(dve)
            group(0, None, 1)
            group(1, 0, 2)
            with dve.Fori(1, ITERS - 2) as j:
                group(j + 1, j, j + 2)
            group(ITERS - 1, ITERS - 2, None)
            group(None, ITERS - 1, None)

        @block.gpsimd
        def _(pool):
            def set_up():
                pool.memset(ident[:], 0.0).then_inc(ident_ok, 1)
                pool.wait_ge(ident_ok, 1)
                pool.affine_select(out=ident[:], in_=ident[:], compare_op=ALU.not_equal, fill=1.0, base=0,
                                   pattern=[[-1, P]], channel_multiplier=1).then_inc(ident_ok, 1)
                pool.dma_start(bout_bc[:], b_out.partition_broadcast(P)).then_inc(ld_vec, 16)
                pool.dma_start(b1_bc[:], b1.partition_broadcast(P)).then_inc(ld_vec, 16)
                pool.dma_start(b2_bc[:], b2.partition_broadcast(P)).then_inc(ld_vec, 16)
                pool.memset(vext[:, :, :, DH:VX], 1.0 / MIX).then_inc(pool_const, 1)
                pool.memset(z2[0][:, :, D:D + 2].bitcast(F32), 1.0).then_inc(pool_const, 1)
                pool.memset(z2[1][:, :, D:D + 2].bitcast(F32), 0.0).then_inc(pool_const, 1)
                pool.memset(wone[:, :, 1:2], 1.0).then_inc(pool_const, 1)
                pool.memset(gate_c[:, 1:2], 0.0).then_inc(pool_const, 1)
                pool.memset(mhalf[:], -0.5).then_inc(pool_const, 1)
                pool.memset(eps_c[:], LN_EPS).then_inc(pool_const, 1)
                pool.memset(mask_ab[:], 0.0).then_inc(pool_const, 1)
                rows = 2
                for base in (0, DH):
                    for col, second in enumerate((1.0, 0.0, BIG, -BIG)):
                        pool.wait_ge(pool_const, 8)
                        last = pool.memset(mask_ab[base:base + rows, col:col + 1], second)
                    last.then_inc(pool_const, 1)
                pool.wait_ge(pool_const, 10)
                for base in (0, DH):
                    for col, first in enumerate((BIG, -BIG, 0.0, 1.0)):
                        last = pool.memset(mask_ab[base:base + 1, col:col + 1], first)
                    last.then_inc(pool_const, 1)
                pool.wait_ge(pool_const, 12)
                pool.wait_ge(ld_wv, 16)
                pool.wait_ge(ld_gate, 16 * 4)
                for t in range(2):
                    pool.tensor_tensor(prod[:, t], wv2_raw[:], aw_bc[:, t:t + 1, :].to_broadcast([P, DC, D]), ALU.mult)\
                        .then_inc(set_prod, 1)
                pool.tensor_tensor(bprod[:], aw_bc[:], bv_bc[:].unsqueeze(1).to_broadcast([P, 2, D]), ALU.mult)\
                    .then_inc(set_prod, 1)
                for n, (src, hi, lo, factor, (ready, value)) in enumerate(splits):
                    if FIRST_FROM_SBUF <= n < FIRST_DERIVED:
                        pool.wait_ge(set_hi, n + 1)
                        pool.wait_ge(ready, value)
                        pool.tensor_tensor(lo, src, hi.bitcast(F32), ALU.subtract).then_inc(set_pool_lo, 1)

            def scale(step, n, g, ready, value, graphs=1):
                pool.wait_ge(ready, value)
                gs = slice(g, g + graphs)
                step.done(pool.tensor_tensor(rs[:, n, gs, 0], mv[:, n, gs, 1], eps_c[:].to_broadcast([P, graphs]),
                                             ALU.add))
                return pool.tensor_tensor(rs[:, n, gs, 1], rs[:, n, gs, 0], mhalf[:].to_broadcast([P, graphs]),
                                          ALU.pow)

            def front(i):
                step = Steps(pool, pool_fstep, i, POOL_FSTEPS)

                def operator():
                    pool.wait_ge(dve_Be, i + 1)
                    settle(pool)
                    for g in range(G):
                        pool.tensor_scalar(BHT[:, g], HT[:, g], Be[:, g:g + 1], None, ALU.mult)\
                            .then_inc(pool_BHT, 1)

                def resid_():
                    pool.wait_ge(x_in, i * 16 + 16)
                    pool.tensor_tensor(ys0[:], xin[:], bout_bc[:].unsqueeze(1).to_broadcast([P, G, D]), ALU.add)\
                        .then_inc(pool_resid0, 1)

                def gate_():
                    pool.wait_ge(act_gate, i + 1)
                    pool.wait_ge(act_mbc, i + 1)
                    flat = gate[:].rearrange("p g n -> p (g n)")
                    step.done(pool.tensor_tensor(gate[:], gate[:], adjT[:], ALU.add))
                    pool.tensor_tensor(flat, flat, mbc[:], ALU.mult).then_inc(pool_gate, 1)

                def gT_():
                    pool.wait_ge(act_gT, i + 1)
                    pool.tensor_tensor(gT[1][:], gate[:], gT[0][:].bitcast(F32), ALU.subtract).then_inc(pool_gT, 1)

                def rs0_(t):
                    scale(step, NORM0, t, dve_mv0, i * G + t + 1).then_inc(pool_rs0, 1)

                return step, operator, resid_, gate_, gT_, rs0_

            def back(j):
                step = Steps(pool, pool_bstep, j, POOL_BSTEPS)

                def resid_(g):
                    pool.wait_ge(act_u, j * G + g + 1)
                    step.done(pool.tensor_tensor(resid[:, g], resid[:, g], b2_bc[:], ALU.add))
                    pool.wait_ge(act_x1, j * G + g + 1)
                    pool.tensor_tensor(resid[:, g], resid[:, g], x1_twice[:, g], ALU.add).then_inc(pool_resid1, 1)

                def rsh_(g):
                    scale(step, NORMH, g, dve_mvh, j * G + g + 1).then_inc(pool_rsh, 1)

                def rs1_(g):
                    scale(step, NORM1, g, dve_mv1, j * G + g + 1).then_inc(pool_rs1, 1)

                def rs2_():
                    scale(step, NORM2, 0, dve_mv2, j * G + G, G).then_inc(pool_rs2, 1)

                def out_(g):
                    step.done(scale(step, NORM3, g, dve_mv3, j * G + g + 1))
                    if g == 0:
                        pool.wait_ge(y_out, j * 16)
                    settle(pool)
                    pool.tensor_scalar(xout[:, g], ysb[:, g], mv[:, NORM3, g, 0:1], rs[:, NORM3, g, 1:2],
                                       ALU.subtract, ALU.mult).then_inc(pool_out, 1)

                def aT_():
                    pool.wait_ge(act_aT, j + 1)
                    pool.tensor_tensor(aT[1][:], adjTb[:], aT[0][:].bitcast(F32), ALU.subtract).then_inc(pool_aT, 1)

                def z0_(g):
                    pool.wait_ge(act_Z01, j * G + g + 1)
                    pool.tensor_tensor(z01[:, g, 0], z01[:, g, 0], bk_bc[:], ALU.add).then_inc(pool_z0, 1)

                def Yl_():
                    pool.wait_ge(act_Y, j * G + 2)
                    pool.tensor_tensor(yT[1][:, 1], yv[:, 1], yT[0][:, 1].bitcast(F32), ALU.subtract)\
                        .then_inc(pool_Yl, 1)

                return step, resid_, rsh_, rs1_, rs2_, out_, aT_, z0_, Yl_

            def group(i, j, n):
                F, B = i is not None, j is not None
                if F:
                    fstep, operator, fresid_, gate_, gT_, rs0_ = front(i)
                if B:
                    bstep, resid_, rsh_, rs1_, rs2_, out_, aT_, z0_, Yl_ = back(j)
                if B:
                    rsh_(0)
                    rsh_(1)
                    resid_(0)
                    resid_(1)
                if F:
                    operator()
                    gate_()
                if B:
                    rs1_(0)
                    rs1_(1)
                if F:
                    gT_()
                    fresid_()
                if B:
                    aT_()
                    z0_(0)
                    z0_(1)
                    Yl_()
                    rs2_()
                if F:
                    rs0_(0)
                    rs0_(1)
                if B:
                    out_(0)
                    out_(1)
                if F:
                    assert fstep.n == POOL_FSTEPS, fstep.n
                if B:
                    assert bstep.n == POOL_BSTEPS, bstep.n

            set_up()
            set_up_done(pool)
            group(0, None, 1)
            group(1, 0, 2)
            with pool.Fori(1, ITERS - 2) as j:
                group(j + 1, j, j + 2)
            group(ITERS - 1, ITERS - 2, None)
            group(None, ITERS - 1, None)


_INS = ['x', 'adj', 'nodemask', 'L0_gnn_W_qkv', 'L0_gnn_W_out', 'L0_gnn_b_out', 'L1_gnn_W1', 'L1_gnn_b1',
        'L1_gnn_gamma', 'L1_gnn_beta', 'L1_gnn_W2', 'L1_gnn_b2', 'L2_gnn_Wv', 'L2_gnn_bv', 'L2_gnn_aw', 'L2_gnn_ab',
        'L2_gnn_Wk', 'L2_gnn_bk', 'L3_gnn_W']


def kernel(**inputs):
    import numpy as _np
    import concourse.bacc as _bacc
    from concourse import mybir as _mybir
    from concourse.bass_utils import run_bass_kernel_spmd as _run

    nc = _bacc.Bacc("TRN2", target_bir_lowering=False, num_devices=1)
    arrays, args = {}, []
    for name in _INS:
        a = _np.ascontiguousarray(inputs[name])
        if a.dtype == _np.bool_:
            a = a.view(_np.uint8)
        arrays[f"in_{name}_dram"] = a
        args.append(nc.dram_tensor(f"in_{name}_dram", a.shape, _mybir.dt.from_np(a.dtype), kind="ExternalInput").ap())
    shape = tuple(inputs["x"].shape)
    args.append(nc.dram_tensor("out_0_dram", shape, _mybir.dt.float32, kind="ExternalOutput").ap())
    gnn_stack_kernel(nc, *args)
    r = _run(nc, [arrays], core_ids=[0])
    return r.results[0]["out_0_dram"]
```
